# Optimizing a Trainium2 kernel written in Bass

```python
import numpy as np
import jax
import jax.numpy as jnp

def _softmax(x, axis=-1):
    return jax.nn.softmax(x, axis=axis)

def _gelu(x):
    return jax.nn.gelu(x, approximate=True)

def _silu(x):
    return jax.nn.silu(x)

def _sigmoid(x):
    return jax.nn.sigmoid(x)

def _layernorm(x, axis=-1, eps=1e-05):
    m = jnp.mean(x, axis=axis, keepdims=True)
    v = jnp.var(x, axis=axis, keepdims=True)
    return (x - m) / jnp.sqrt(v + eps)

def _scatter_add(tgt, idx, src, axis=0):
    return tgt.at[idx].add(src)

def _segment_sum(src, seg, n):
    return jax.ops.segment_sum(src, seg, n)
kernel_name = 'mk_recurrent_d4_jaxref_r8_274595'

def setup_inputs(seed: int=0):
    np.random.seed(seed)
    _w = jnp.asarray

    def _L0_attn_setup():
        import jax, jax.numpy as jnp
        import numpy as np
        D_MODEL = 128
        EXPAND = 2
        HEADDIM = 64
        D_STATE = 128
        NGROUPS = 1
        D_CONV = 4
        CHUNK = 32
        D_INNER = EXPAND * D_MODEL
        NHEADS = D_INNER // HEADDIM
        CONV_DIM = D_INNER + 2 * NGROUPS * D_STATE
        D_IN_PROJ = 2 * D_INNER + 2 * NGROUPS * D_STATE + NHEADS
        BATCH, SEQLEN = (2, 512)
        EPS = 1e-05

        def _mamba2(u, W_in, conv_w, conv_b, dt_bias, A_log, D, norm_weight, W_out):
            b, l, _ = u.shape
            H, P, N, Lc = (NHEADS, HEADDIM, D_STATE, CHUNK)
            nc = l // Lc
            zxbcdt = u @ W_in.T
            z = zxbcdt[..., :D_INNER]
            xBC = zxbcdt[..., D_INNER:D_INNER + CONV_DIM]
            dt = zxbcdt[..., D_INNER + CONV_DIM:]
            xp = jnp.pad(xBC, ((0, 0), (D_CONV - 1, 0), (0, 0)))
            xc = conv_b + sum((xp[:, w:w + l, :] * conv_w[:, w] for w in range(D_CONV)))
            xBC = jax.nn.silu(xc)
            x = xBC[..., :D_INNER]
            Bm = xBC[..., D_INNER:D_INNER + N]
            Cm = xBC[..., D_INNER + N:]
            X = x.reshape(b, l, H, P)
            dt = jax.nn.softplus(dt + dt_bias)
            A = -jnp.exp(A_log)
            dA = (dt * A).reshape(b, nc, Lc, H)
            dtc = dt.reshape(b, nc, Lc, H)
            Xc = X.reshape(b, nc, Lc, H, P)
            Bc = Bm.reshape(b, nc, Lc, N)
            Cc = Cm.reshape(b, nc, Lc, N)
            cA = jnp.cumsum(dA, axis=2)
            mask = jnp.tril(jnp.ones((Lc, Lc), bool))
            diff = cA[:, :, :, None, :] - cA[:, :, None, :, :]
            decay = jnp.exp(jnp.where(mask[None, None, :, :, None], diff, -1000000000.0))
            CB = jnp.einsum('bcln,bcsn->bcls', Cc, Bc)
            M = CB[..., None] * decay * dtc[:, :, None, :, :]
            Y_intra = jnp.einsum('bclsh,bcshp->bclhp', M, Xc)
            dstate = jnp.exp(cA[:, :, -1:, :] - cA) * dtc
            states = jnp.einsum('bclh,bcln,bclhp->bchpn', dstate, Bc, Xc)
            cdecay = jnp.exp(cA[:, :, -1, :])

            def step(carry, inp):
                s, d = inp
                new = carry * d[:, :, None, None] + s
                return (new, carry)
            init = jnp.zeros((b, H, P, N), u.dtype)
            _, prev = jax.lax.scan(step, init, (jnp.moveaxis(states, 1, 0), jnp.moveaxis(cdecay, 1, 0)))
            prev = jnp.moveaxis(prev, 0, 1)
            Y_inter = jnp.einsum('bclh,bcln,bchpn->bclhp', jnp.exp(cA), Cc, prev)
            Y = (Y_intra + Y_inter).reshape(b, l, H, P) + D[None, None, :, None] * X
            y = Y.reshape(b, l, H * P)
            y = y * jax.nn.silu(z)
            y = y * jax.lax.rsqrt(jnp.mean(y * y, axis=-1, keepdims=True) + EPS) * norm_weight
            return y @ W_out.T
        key = jax.random.key(seed)
        ks = jax.random.split(key, 8)
        u = jax.random.normal(ks[0], (BATCH, SEQLEN, D_MODEL), jnp.float32)
        W_in = jax.random.normal(ks[1], (D_IN_PROJ, D_MODEL), jnp.float32) * 0.02
        conv_w = jax.random.normal(ks[2], (CONV_DIM, D_CONV), jnp.float32) * 0.2
        conv_b = jnp.zeros((CONV_DIM,), jnp.float32)
        dt = jnp.exp(jax.random.uniform(ks[3], (NHEADS,)) * (np.log(0.1) - np.log(0.001)) + np.log(0.001))
        dt = jnp.clip(dt, 0.0001, None)
        dt_bias = dt + jnp.log(-jnp.expm1(-dt))
        A_log = jnp.log(jax.random.uniform(ks[4], (NHEADS,), minval=1.0, maxval=16.0))
        D = jnp.ones((NHEADS,), jnp.float32)
        norm_weight = jnp.ones((D_INNER,), jnp.float32)
        W_out = jax.random.normal(ks[5], (D_MODEL, D_INNER), jnp.float32) * 0.02
        return {'u': u, 'W_in': W_in, 'conv_w': conv_w, 'conv_b': conv_b, 'dt_bias': dt_bias, 'A_log': A_log, 'D': D, 'norm_weight': norm_weight, 'W_out': W_out}
    _L0_attn_in = _L0_attn_setup()

    def _L0_ffn_setup():
        import jax, jax.numpy as jnp
        import numpy as np
        D_MODEL = 128
        D_FF = 512
        N_EXPERTS = 8
        D_EXPERT = D_FF // N_EXPERTS
        TOP_K = 2
        LB_WEIGHT = 0.01
        B, S = (4, 256)

        def _top_k_softmax(logits, k):
            vals, _ = jax.lax.top_k(logits, k)
            thresh = vals[..., -1:]
            masked = jnp.where(logits >= thresh, logits, -jnp.inf)
            return jax.nn.softmax(masked, axis=-1)
        key = jax.random.key(seed)
        ks = jax.random.split(key, 8)
        x = jax.random.normal(ks[0], (B, S, D_MODEL), dtype=jnp.float32)
        w1 = jax.random.normal(ks[1], (N_EXPERTS, D_MODEL, D_EXPERT), dtype=jnp.float32) * (1.0 / np.sqrt(D_MODEL))
        b1 = jnp.zeros((N_EXPERTS, D_EXPERT), dtype=jnp.float32)
        w2 = jax.random.normal(ks[2], (N_EXPERTS, D_EXPERT, D_MODEL), dtype=jnp.float32) * (1.0 / np.sqrt(D_EXPERT))
        b2 = jnp.zeros((N_EXPERTS, D_MODEL), dtype=jnp.float32)
        centroids = jax.random.normal(ks[3], (N_EXPERTS, D_MODEL), dtype=jnp.float32) * 0.02
        w_route = jax.random.normal(ks[4], (N_EXPERTS, D_MODEL), dtype=jnp.float32) * (1.0 / np.sqrt(D_MODEL))
        return {'x': x, 'w1': w1, 'b1': b1, 'w2': w2, 'b2': b2, 'centroids': centroids, 'w_route': w_route}
    _L0_ffn_in = _L0_ffn_setup()

    def _L1_attn_setup():
        import jax, jax.numpy as jnp
        import numpy as np
        B, L, D = (8, 256, 128)
        LN_EPS = 1e-05
        L2_EPS = 1e-12

        def _delta_scan(q, k, v, beta):

            def step(S, inp):
                qt, kt, vt, bt = inp
                v_adj = bt * (vt - kt @ S)
                S = S + kt[:, None] * v_adj[None, :]
                return (S, qt @ S)
            S0 = jnp.zeros((D, D), dtype=q.dtype)
            _, o = jax.lax.scan(step, S0, (q, k, v, beta))
            return o
        key = jax.random.key(seed)
        ks = jax.random.split(key, 5)
        s = 1.0 / np.sqrt(D)
        x = jax.random.normal(ks[0], (B, L, D), dtype=jnp.float32)
        Wq = jax.random.normal(ks[1], (D, D), dtype=jnp.float32) * s
        Wk = jax.random.normal(ks[2], (D, D), dtype=jnp.float32) * s
        Wv = jax.random.normal(ks[3], (D, D), dtype=jnp.float32) * s
        Wb = jax.random.normal(ks[4], (D,), dtype=jnp.float32) * s
        ln_g = jnp.ones((D,), dtype=jnp.float32)
        ln_b = jnp.zeros((D,), dtype=jnp.float32)
        return {'x': x, 'Wq': Wq, 'Wk': Wk, 'Wv': Wv, 'Wb': Wb, 'ln_g': ln_g, 'ln_b': ln_b}
    _L1_attn_in = _L1_attn_setup()

    def _L1_ffn_setup():
        import jax, jax.numpy as jnp
        import numpy as np
        D, H, E, K, S = (128, 256, 8, 2, 1)
        B, L = (4, 256)
        key = jax.random.key(seed)
        ks = jax.random.split(key, 9)
        std = 0.02
        return {'x': jax.random.normal(ks[0], (B, L, D), dtype=jnp.float32), 'router_w': jax.random.normal(ks[1], (E, D), dtype=jnp.float32) * std, 'experts_bias': jnp.zeros((E,), dtype=jnp.float32), 'w1': jax.random.normal(ks[2], (E, D, H), dtype=jnp.float32) * std, 'w3': jax.random.normal(ks[3], (E, D, H), dtype=jnp.float32) * std, 'w2': jax.random.normal(ks[4], (E, H, D), dtype=jnp.float32) * std, 'sw1': jax.random.normal(ks[5], (S, D, H), dtype=jnp.float32) * std, 'sw3': jax.random.normal(ks[6], (S, D, H), dtype=jnp.float32) * std, 'sw2': jax.random.normal(ks[7], (S, H, D), dtype=jnp.float32) * std}
    _L1_ffn_in = _L1_ffn_setup()

    def _L2_attn_setup():
        import jax, jax.numpy as jnp
        import numpy as np
        D_MODEL = 128
        N_HEADS = 16
        D_HEAD = D_MODEL // N_HEADS
        B, T = (2, 256)
        key = jax.random.key(seed)
        ks = jax.random.split(key, 8)
        s = 1.0 / np.sqrt(D_MODEL)
        return {'x': jax.random.normal(ks[0], (B, T, D_MODEL), dtype=jnp.float32), 'ln_g': jnp.ones((D_MODEL,), jnp.float32), 'ln_b': jnp.zeros((D_MODEL,), jnp.float32), 'w_qkv': jax.random.normal(ks[1], (D_MODEL, 3 * D_MODEL), jnp.float32) * s, 'b_qkv': jnp.zeros((3 * D_MODEL,), jnp.float32), 'w_gate': jax.random.normal(ks[2], (D_MODEL, D_MODEL), jnp.float32) * s, 'b_gate': jnp.zeros((D_MODEL,), jnp.float32), 'w_proj': jax.random.normal(ks[3], (D_MODEL, D_MODEL), jnp.float32) * s, 'b_proj': jnp.zeros((D_MODEL,), jnp.float32)}
    _L2_attn_in = _L2_attn_setup()

    def _L2_ffn_setup():
        import jax, jax.numpy as jnp
        import numpy as np
        D_MODEL = 128
        N_HEADS = 16
        N_GROUPS = 4
        D_FF = 512
        N_EXPERTS = 8
        TOP_K = 2
        BATCH = 2
        SEQ = 128
        D_K = D_MODEL // N_HEADS
        HPG = N_HEADS // N_GROUPS
        EPS = 1e-06

        def rms_norm(x, w):
            rms = jnp.sqrt(jnp.mean(x * x, axis=-1, keepdims=True) + EPS)
            return x / rms * w

        def rope(x):
            d = x.shape[-1]
            half = d // 2
            theta = 1.0 / 10000.0 ** (jnp.arange(half, dtype=jnp.float32) / half)
            pos = jnp.arange(x.shape[1], dtype=jnp.float32)[:, None]
            ang = pos * theta[None, :]
            cos, sin = (jnp.cos(ang), jnp.sin(ang))
            xe, xo = (x[..., 0::2], x[..., 1::2])
            return jnp.concatenate([xe * cos - xo * sin, xe * sin + xo * cos], axis=-1)

        def attention(x, Wq, Wk, Wv, Wo):
            B, S, _ = x.shape
            xr = rope(x)
            Q = (xr @ Wq).reshape(B, S, N_HEADS, D_K).transpose(0, 2, 1, 3)
            Q = Q.reshape(B, N_GROUPS, HPG, S, D_K)
            K = (xr @ Wk).reshape(B, S, N_GROUPS, D_K).transpose(0, 2, 1, 3)
            V = (xr @ Wv).reshape(B, S, N_GROUPS, D_K).transpose(0, 2, 1, 3)
            scores = jnp.einsum('bghsd,bgtd->bghst', Q, K) / jnp.sqrt(jnp.float32(D_K))
            mask = jnp.triu(jnp.full((S, S), -1000000000.0, dtype=scores.dtype), k=1)
            attn = jax.nn.softmax(scores + mask, axis=-1)
            out = jnp.einsum('bghst,bgtd->bghsd', attn, V)
            out = out.reshape(B, N_HEADS, S, D_K).transpose(0, 2, 1, 3).reshape(B, S, D_MODEL)
            return out @ Wo

        def moe(x, router_w, router_b, W1, b1, W2, b2, W3, b3):
            B, S, _ = x.shape
            logits = x @ router_w + router_b
            topv, topi = jax.lax.top_k(logits, TOP_K)
            topw = jax.nn.softmax(topv, axis=-1)
            onehot = jax.nn.one_hot(topi, N_EXPERTS, dtype=x.dtype)
            comb = jnp.einsum('bsk,bske->bse', topw, onehot)
            h1 = jnp.einsum('bsd,edf->ebsf', x, W1) + b1[:, None, None, :]
            h2 = jnp.einsum('bsd,edf->ebsf', x, W2) + b2[:, None, None, :]
            h = h2 * jax.nn.silu(h1)
            eo = jnp.einsum('ebsf,efd->ebsd', h, W3) + b3[:, None, None, :]
            return jnp.einsum('bse,ebsd->bsd', comb, eo)
        key = jax.random.key(seed)
        ks = jax.random.split(key, 16)
        s = 0.02
        return {'x': jax.random.normal(ks[0], (BATCH, SEQ, D_MODEL), dtype=jnp.float32), 'norm1_w': jnp.ones((D_MODEL,), jnp.float32), 'Wq': jax.random.normal(ks[1], (D_MODEL, D_MODEL), jnp.float32) * s, 'Wk': jax.random.normal(ks[2], (D_MODEL, N_GROUPS * D_K), jnp.float32) * s, 'Wv': jax.random.normal(ks[3], (D_MODEL, N_GROUPS * D_K), jnp.float32) * s, 'Wo': jax.random.normal(ks[4], (D_MODEL, D_MODEL), jnp.float32) * s, 'norm2_w': jnp.ones((D_MODEL,), jnp.float32), 'router_w': jax.random.normal(ks[5], (D_MODEL, N_EXPERTS), jnp.float32) * s, 'router_b': jnp.zeros((N_EXPERTS,), jnp.float32), 'W1': jax.random.normal(ks[6], (N_EXPERTS, D_MODEL, D_FF), jnp.float32) * s, 'b1': jnp.zeros((N_EXPERTS, D_FF), jnp.float32), 'W2': jax.random.normal(ks[7], (N_EXPERTS, D_MODEL, D_FF), jnp.float32) * s, 'b2': jnp.zeros((N_EXPERTS, D_FF), jnp.float32), 'W3': jax.random.normal(ks[8], (N_EXPERTS, D_FF, D_MODEL), jnp.float32) * s, 'b3': jnp.zeros((N_EXPERTS, D_MODEL), jnp.float32)}
    _L2_ffn_in = _L2_ffn_setup()

    def _L3_attn_setup():
        import jax, jax.numpy as jnp
        import numpy as np
        B, L = (2, 256)
        D_MODEL = 128
        D_STATE = 128
        D_CONV = 4
        EXPAND = 2
        HEADDIM = 64
        D_HALF = D_MODEL // 2
        D_INNER = EXPAND * D_HALF
        NHEADS = D_INNER // HEADDIM
        CONV_DIM = D_INNER + 2 * D_STATE
        D_IN_PROJ = 2 * D_INNER + 2 * D_STATE + NHEADS
        EPS = 1e-05

        def _rmsnorm(x, w):
            return x * jax.lax.rsqrt(jnp.mean(x * x, axis=-1, keepdims=True) + EPS) * w

        def _mamba2(u, in_w, conv_w, conv_b, dt_bias, A_log, D, gnorm_w, outp_w):
            b, l, _ = u.shape
            zxbcdt = u @ in_w.T
            z = zxbcdt[..., :D_INNER]
            xBC = zxbcdt[..., D_INNER:D_INNER + CONV_DIM]
            dt = zxbcdt[..., D_INNER + CONV_DIM:]
            xp = jnp.pad(xBC, ((0, 0), (D_CONV - 1, 0), (0, 0)))
            conv = conv_b + sum((xp[:, k:k + l, :] * conv_w[:, k] for k in range(D_CONV)))
            xBC = jax.nn.silu(conv)
            x = xBC[..., :D_INNER]
            Bm = xBC[..., D_INNER:D_INNER + D_STATE]
            Cm = xBC[..., D_INNER + D_STATE:]
            dt = jax.nn.softplus(dt + dt_bias)
            A = -jnp.exp(A_log)
            xh = x.reshape(b, l, NHEADS, HEADDIM)
            dA = jnp.exp(dt * A)
            dtx = dt[..., None] * xh

            def step(h, inp):
                dA_t, dtx_t, B_t, C_t = inp
                h = dA_t[:, :, None, None] * h + jnp.einsum('bhp,bn->bhpn', dtx_t, B_t)
                return (h, jnp.einsum('bhpn,bn->bhp', h, C_t))
            h0 = jnp.zeros((b, NHEADS, HEADDIM, D_STATE), u.dtype)
            xs = (jnp.moveaxis(dA, 1, 0), jnp.moveaxis(dtx, 1, 0), jnp.moveaxis(Bm, 1, 0), jnp.moveaxis(Cm, 1, 0))
            _, ys = jax.lax.scan(step, h0, xs)
            y = jnp.moveaxis(ys, 0, 1) + xh * D[None, None, :, None]
            y = y.reshape(b, l, D_INNER) * jax.nn.silu(z)
            y = _rmsnorm(y, gnorm_w)
            return y @ outp_w.T

        def _forward(x, norm_w, op_w, op_b, f_in_w, f_conv_w, f_conv_b, f_dt_bias, f_A_log, f_D, f_gnorm_w, f_outp_w, b_in_w, b_conv_w, b_conv_b, b_dt_bias, b_A_log, b_D, b_gnorm_w, b_outp_w):
            xn = _rmsnorm(x, norm_w)
            x_f, x_b = (xn[..., :D_HALF], xn[..., D_HALF:])
            out_f = _mamba2(x_f, f_in_w, f_conv_w, f_conv_b, f_dt_bias, f_A_log, f_D, f_gnorm_w, f_outp_w)
            out_b = jnp.flip(_mamba2(jnp.flip(x_b, 1), b_in_w, b_conv_w, b_conv_b, b_dt_bias, b_A_log, b_D, b_gnorm_w, b_outp_w), 1)
            out = jnp.concatenate([out_f, out_b], axis=-1) @ op_w.T + op_b
            return x + out

        def _mamba_params(key, prefix):
            k = jax.random.split(key, 5)
            return {prefix + 'in_w': jax.random.normal(k[0], (D_IN_PROJ, D_HALF), jnp.float32) * 0.02, prefix + 'conv_w': jax.random.normal(k[1], (CONV_DIM, D_CONV), jnp.float32) * 0.2, prefix + 'conv_b': jnp.zeros((CONV_DIM,), jnp.float32), prefix + 'dt_bias': jax.random.normal(k[2], (NHEADS,), jnp.float32) * 0.1, prefix + 'A_log': jnp.log(jax.random.uniform(k[3], (NHEADS,), jnp.float32, 1.0, 16.0)), prefix + 'D': jnp.ones((NHEADS,), jnp.float32), prefix + 'gnorm_w': jnp.ones((D_INNER,), jnp.float32), prefix + 'outp_w': jax.random.normal(k[4], (D_HALF, D_INNER), jnp.float32) * 0.02}
        key = jax.random.key(seed)
        k = jax.random.split(key, 4)
        inp = {'x': jax.random.normal(k[0], (B, L, D_MODEL), jnp.float32), 'norm_w': jnp.ones((D_MODEL,), jnp.float32), 'op_w': jax.random.normal(k[1], (D_MODEL, D_MODEL), jnp.float32) * 0.02, 'op_b': jnp.zeros((D_MODEL,), jnp.float32)}
        inp.update(_mamba_params(k[2], 'f_'))
        inp.update(_mamba_params(k[3], 'b_'))
        return inp
    _L3_attn_in = _L3_attn_setup()

    def _L3_ffn_setup():
        import jax, jax.numpy as jnp
        import numpy as np
        DIM = 128
        EXPERT_DIM = 64
        N_EXPERTS = 16
        TOPK = 2
        SHARED_HIDDEN = EXPERT_DIM * TOPK
        B, T = (4, 128)

        def _moe_forward(x, router_w, router_bias, up_proj, gate_proj, down_proj, sh_gate, sh_up, sh_down):
            Bb, Tt, D = x.shape
            flat = x.reshape(Bb * Tt, D)
            N = flat.shape[0]
            logits = flat @ router_w.T
            topk_scores, topk_idx = jax.lax.top_k(logits + router_bias, TOPK)
            topk_scores = jax.nn.softmax(topk_scores, axis=-1)
            combine = jnp.zeros((N, N_EXPERTS), flat.dtype)
            combine = combine.at[jnp.arange(N)[:, None], topk_idx].add(topk_scores)
            up_all = jnp.einsum('nd,kde->nke', flat, up_proj)
            gate_all = jnp.einsum('nd,kde->nke', flat, gate_proj)
            hidden = jax.nn.silu(gate_all) * up_all
            down_all = jnp.einsum('nke,ked->nkd', hidden, down_proj)
            out = jnp.einsum('nk,nkd->nd', combine, down_all)
            sh_hidden = jax.nn.silu(flat @ sh_gate.T) * (flat @ sh_up.T)
            out = out + sh_hidden @ sh_down.T
            return out.reshape(Bb, Tt, D)
        key = jax.random.key(seed)
        ks = jax.random.split(key, 9)
        std = 0.02
        return {'x': jax.random.normal(ks[0], (B, T, DIM), jnp.float32), 'router_w': jax.random.normal(ks[1], (N_EXPERTS, DIM), jnp.float32) * std, 'router_bias': jnp.zeros((N_EXPERTS,), jnp.float32), 'up_proj': jax.random.normal(ks[2], (N_EXPERTS, DIM, EXPERT_DIM), jnp.float32) * std, 'gate_proj': jax.random.normal(ks[3], (N_EXPERTS, DIM, EXPERT_DIM), jnp.float32) * std, 'down_proj': jax.random.normal(ks[4], (N_EXPERTS, EXPERT_DIM, DIM), jnp.float32) * std, 'sh_gate': jax.random.normal(ks[5], (SHARED_HIDDEN, DIM), jnp.float32) * std, 'sh_up': jax.random.normal(ks[6], (SHARED_HIDDEN, DIM), jnp.float32) * std, 'sh_down': jax.random.normal(ks[7], (DIM, SHARED_HIDDEN), jnp.float32) * std}
    _L3_ffn_in = _L3_ffn_setup()
    _d = {'L0_attn_u': _L0_attn_in['u'], 'L0_attn_W_in': _L0_attn_in['W_in'], 'L0_attn_conv_w': _L0_attn_in['conv_w'], 'L0_attn_conv_b': _L0_attn_in['conv_b'], 'L0_attn_dt_bias': _L0_attn_in['dt_bias'], 'L0_attn_A_log': _L0_attn_in['A_log'], 'L0_attn_D': _L0_attn_in['D'], 'L0_attn_norm_weight': _L0_attn_in['norm_weight'], 'L0_attn_W_out': _L0_attn_in['W_out'], 'L0_ffn_w1': _L0_ffn_in['w1'], 'L0_ffn_b1': _L0_ffn_in['b1'], 'L0_ffn_w2': _L0_ffn_in['w2'], 'L0_ffn_b2': _L0_ffn_in['b2'], 'L0_ffn_centroids': _L0_ffn_in['centroids'], 'L0_ffn_w_route': _L0_ffn_in['w_route'], 'L1_attn_Wq': _L1_attn_in['Wq'], 'L1_attn_Wk': _L1_attn_in['Wk'], 'L1_attn_Wv': _L1_attn_in['Wv'], 'L1_attn_Wb': _L1_attn_in['Wb'], 'L1_attn_ln_g': _L1_attn_in['ln_g'], 'L1_attn_ln_b': _L1_attn_in['ln_b'], 'L1_ffn_router_w': _L1_ffn_in['router_w'], 'L1_ffn_experts_bias': _L1_ffn_in['experts_bias'], 'L1_ffn_w1': _L1_ffn_in['w1'], 'L1_ffn_w3': _L1_ffn_in['w3'], 'L1_ffn_w2': _L1_ffn_in['w2'], 'L1_ffn_sw1': _L1_ffn_in['sw1'], 'L1_ffn_sw3': _L1_ffn_in['sw3'], 'L1_ffn_sw2': _L1_ffn_in['sw2'], 'L2_attn_ln_g': _L2_attn_in['ln_g'], 'L2_attn_ln_b': _L2_attn_in['ln_b'], 'L2_attn_w_qkv': _L2_attn_in['w_qkv'], 'L2_attn_b_qkv': _L2_attn_in['b_qkv'], 'L2_attn_w_gate': _L2_attn_in['w_gate'], 'L2_attn_b_gate': _L2_attn_in['b_gate'], 'L2_attn_w_proj': _L2_attn_in['w_proj'], 'L2_attn_b_proj': _L2_attn_in['b_proj'], 'L2_ffn_norm1_w': _L2_ffn_in['norm1_w'], 'L2_ffn_Wq': _L2_ffn_in['Wq'], 'L2_ffn_Wk': _L2_ffn_in['Wk'], 'L2_ffn_Wv': _L2_ffn_in['Wv'], 'L2_ffn_Wo': _L2_ffn_in['Wo'], 'L2_ffn_norm2_w': _L2_ffn_in['norm2_w'], 'L2_ffn_router_w': _L2_ffn_in['router_w'], 'L2_ffn_router_b': _L2_ffn_in['router_b'], 'L2_ffn_W1': _L2_ffn_in['W1'], 'L2_ffn_b1': _L2_ffn_in['b1'], 'L2_ffn_W2': _L2_ffn_in['W2'], 'L2_ffn_b2': _L2_ffn_in['b2'], 'L2_ffn_W3': _L2_ffn_in['W3'], 'L2_ffn_b3': _L2_ffn_in['b3'], 'L3_attn_norm_w': _L3_attn_in['norm_w'], 'L3_attn_op_w': _L3_attn_in['op_w'], 'L3_attn_op_b': _L3_attn_in['op_b'], 'L3_attn_f_in_w': _L3_attn_in['f_in_w'], 'L3_attn_f_conv_w': _L3_attn_in['f_conv_w'], 'L3_attn_f_conv_b': _L3_attn_in['f_conv_b'], 'L3_attn_f_dt_bias': _L3_attn_in['f_dt_bias'], 'L3_attn_f_A_log': _L3_attn_in['f_A_log'], 'L3_attn_f_D': _L3_attn_in['f_D'], 'L3_attn_f_gnorm_w': _L3_attn_in['f_gnorm_w'], 'L3_attn_f_outp_w': _L3_attn_in['f_outp_w'], 'L3_attn_b_in_w': _L3_attn_in['b_in_w'], 'L3_attn_b_conv_w': _L3_attn_in['b_conv_w'], 'L3_attn_b_conv_b': _L3_attn_in['b_conv_b'], 'L3_attn_b_dt_bias': _L3_attn_in['b_dt_bias'], 'L3_attn_b_A_log': _L3_attn_in['b_A_log'], 'L3_attn_b_D': _L3_attn_in['b_D'], 'L3_attn_b_gnorm_w': _L3_attn_in['b_gnorm_w'], 'L3_attn_b_outp_w': _L3_attn_in['b_outp_w'], 'L3_ffn_router_w': _L3_ffn_in['router_w'], 'L3_ffn_router_bias': _L3_ffn_in['router_bias'], 'L3_ffn_up_proj': _L3_ffn_in['up_proj'], 'L3_ffn_gate_proj': _L3_ffn_in['gate_proj'], 'L3_ffn_down_proj': _L3_ffn_in['down_proj'], 'L3_ffn_sh_gate': _L3_ffn_in['sh_gate'], 'L3_ffn_sh_up': _L3_ffn_in['sh_up'], 'L3_ffn_sh_down': _L3_ffn_in['sh_down']}
    _x0 = _d['L0_attn_u']
    _d['L0_attn_u'] = jax.random.normal(jax.random.fold_in(jax.random.key(seed), 1), (2, 1024, 128), dtype=_x0.dtype)
    del _x0
    return _d

def reference(L0_attn_u, L0_attn_W_in, L0_attn_conv_w, L0_attn_conv_b, L0_attn_dt_bias, L0_attn_A_log, L0_attn_D, L0_attn_norm_weight, L0_attn_W_out, L0_ffn_w1, L0_ffn_b1, L0_ffn_w2, L0_ffn_b2, L0_ffn_centroids, L0_ffn_w_route, L1_attn_Wq, L1_attn_Wk, L1_attn_Wv, L1_attn_Wb, L1_attn_ln_g, L1_attn_ln_b, L1_ffn_router_w, L1_ffn_experts_bias, L1_ffn_w1, L1_ffn_w3, L1_ffn_w2, L1_ffn_sw1, L1_ffn_sw3, L1_ffn_sw2, L2_attn_ln_g, L2_attn_ln_b, L2_attn_w_qkv, L2_attn_b_qkv, L2_attn_w_gate, L2_attn_b_gate, L2_attn_w_proj, L2_attn_b_proj, L2_ffn_norm1_w, L2_ffn_Wq, L2_ffn_Wk, L2_ffn_Wv, L2_ffn_Wo, L2_ffn_norm2_w, L2_ffn_router_w, L2_ffn_router_b, L2_ffn_W1, L2_ffn_b1, L2_ffn_W2, L2_ffn_b2, L2_ffn_W3, L2_ffn_b3, L3_attn_norm_w, L3_attn_op_w, L3_attn_op_b, L3_attn_f_in_w, L3_attn_f_conv_w, L3_attn_f_conv_b, L3_attn_f_dt_bias, L3_attn_f_A_log, L3_attn_f_D, L3_attn_f_gnorm_w, L3_attn_f_outp_w, L3_attn_b_in_w, L3_attn_b_conv_w, L3_attn_b_conv_b, L3_attn_b_dt_bias, L3_attn_b_A_log, L3_attn_b_D, L3_attn_b_gnorm_w, L3_attn_b_outp_w, L3_ffn_router_w, L3_ffn_router_bias, L3_ffn_up_proj, L3_ffn_gate_proj, L3_ffn_down_proj, L3_ffn_sh_gate, L3_ffn_sh_up, L3_ffn_sh_down):

    def _L0_attn_ref(u, W_in, conv_w, conv_b, dt_bias, A_log, D, norm_weight, W_out):
        import jax, jax.numpy as jnp
        import numpy as np
        D_MODEL = 128
        EXPAND = 2
        HEADDIM = 64
        D_STATE = 128
        NGROUPS = 1
        D_CONV = 4
        CHUNK = 32
        D_INNER = EXPAND * D_MODEL
        NHEADS = D_INNER // HEADDIM
        CONV_DIM = D_INNER + 2 * NGROUPS * D_STATE
        D_IN_PROJ = 2 * D_INNER + 2 * NGROUPS * D_STATE + NHEADS
        BATCH, SEQLEN = (2, 512)
        EPS = 1e-05

        def _mamba2(u, W_in, conv_w, conv_b, dt_bias, A_log, D, norm_weight, W_out):
            b, l, _ = u.shape
            H, P, N, Lc = (NHEADS, HEADDIM, D_STATE, CHUNK)
            nc = l // Lc
            zxbcdt = u @ W_in.T
            z = zxbcdt[..., :D_INNER]
            xBC = zxbcdt[..., D_INNER:D_INNER + CONV_DIM]
            dt = zxbcdt[..., D_INNER + CONV_DIM:]
            xp = jnp.pad(xBC, ((0, 0), (D_CONV - 1, 0), (0, 0)))
            xc = conv_b + sum((xp[:, w:w + l, :] * conv_w[:, w] for w in range(D_CONV)))
            xBC = jax.nn.silu(xc)
            x = xBC[..., :D_INNER]
            Bm = xBC[..., D_INNER:D_INNER + N]
            Cm = xBC[..., D_INNER + N:]
            X = x.reshape(b, l, H, P)
            dt = jax.nn.softplus(dt + dt_bias)
            A = -jnp.exp(A_log)
            dA = (dt * A).reshape(b, nc, Lc, H)
            dtc = dt.reshape(b, nc, Lc, H)
            Xc = X.reshape(b, nc, Lc, H, P)
            Bc = Bm.reshape(b, nc, Lc, N)
            Cc = Cm.reshape(b, nc, Lc, N)
            cA = jnp.cumsum(dA, axis=2)
            mask = jnp.tril(jnp.ones((Lc, Lc), bool))
            diff = cA[:, :, :, None, :] - cA[:, :, None, :, :]
            decay = jnp.exp(jnp.where(mask[None, None, :, :, None], diff, -1000000000.0))
            CB = jnp.einsum('bcln,bcsn->bcls', Cc, Bc)
            M = CB[..., None] * decay * dtc[:, :, None, :, :]
            Y_intra = jnp.einsum('bclsh,bcshp->bclhp', M, Xc)
            dstate = jnp.exp(cA[:, :, -1:, :] - cA) * dtc
            states = jnp.einsum('bclh,bcln,bclhp->bchpn', dstate, Bc, Xc)
            cdecay = jnp.exp(cA[:, :, -1, :])

            def step(carry, inp):
                s, d = inp
                new = carry * d[:, :, None, None] + s
                return (new, carry)
            init = jnp.zeros((b, H, P, N), u.dtype)
            _, prev = jax.lax.scan(step, init, (jnp.moveaxis(states, 1, 0), jnp.moveaxis(cdecay, 1, 0)))
            prev = jnp.moveaxis(prev, 0, 1)
            Y_inter = jnp.einsum('bclh,bcln,bchpn->bclhp', jnp.exp(cA), Cc, prev)
            Y = (Y_intra + Y_inter).reshape(b, l, H, P) + D[None, None, :, None] * X
            y = Y.reshape(b, l, H * P)
            y = y * jax.nn.silu(z)
            y = y * jax.lax.rsqrt(jnp.mean(y * y, axis=-1, keepdims=True) + EPS) * norm_weight
            return y @ W_out.T
        return _mamba2(u, W_in, conv_w, conv_b, dt_bias, A_log, D, norm_weight, W_out)

    def _L0_ffn_ref(x, w1, b1, w2, b2, centroids, w_route):
        import jax, jax.numpy as jnp
        import numpy as np
        D_MODEL = 128
        D_FF = 512
        N_EXPERTS = 8
        D_EXPERT = D_FF // N_EXPERTS
        TOP_K = 2
        LB_WEIGHT = 0.01
        B, S = (4, 256)

        def _top_k_softmax(logits, k):
            vals, _ = jax.lax.top_k(logits, k)
            thresh = vals[..., -1:]
            masked = jnp.where(logits >= thresh, logits, -jnp.inf)
            return jax.nn.softmax(masked, axis=-1)
        eps = 1e-12
        x_norm = x / jnp.maximum(jnp.linalg.norm(x, axis=-1, keepdims=True), eps)
        c_norm = centroids / jnp.maximum(jnp.linalg.norm(centroids, axis=-1, keepdims=True), eps)
        cos_scores = jnp.einsum('bsd,ed->bse', x_norm, c_norm)
        route_scores = jnp.einsum('bsd,ed->bse', x, w_route)
        logits = cos_scores + route_scores
        gates = _top_k_softmax(logits, TOP_K)
        h = jax.nn.gelu(jnp.einsum('bsd,edh->bseh', x, w1) + b1, approximate=False)
        expert_out = jnp.einsum('bseh,ehd->bsed', h, w2) + b2
        out = jnp.einsum('bse,bsed->bsd', gates, expert_out)
        return out

    def _L1_attn_ref(x, Wq, Wk, Wv, Wb, ln_g, ln_b):
        import jax, jax.numpy as jnp
        import numpy as np
        B, L, D = (8, 256, 128)
        LN_EPS = 1e-05
        L2_EPS = 1e-12

        def _delta_scan(q, k, v, beta):

            def step(S, inp):
                qt, kt, vt, bt = inp
                v_adj = bt * (vt - kt @ S)
                S = S + kt[:, None] * v_adj[None, :]
                return (S, qt @ S)
            S0 = jnp.zeros((D, D), dtype=q.dtype)
            _, o = jax.lax.scan(step, S0, (q, k, v, beta))
            return o
        scale = D ** (-0.5)
        q = x @ Wq * scale
        k = x @ Wk
        k = k / jnp.maximum(jnp.linalg.norm(k, axis=-1, keepdims=True), L2_EPS)
        v = jax.nn.silu(x @ Wv)
        beta = jax.nn.sigmoid(x @ Wb)
        o = jax.vmap(_delta_scan)(q, k, v, beta)
        mu = jnp.mean(o, axis=-1, keepdims=True)
        var = jnp.mean(jnp.square(o - mu), axis=-1, keepdims=True)
        return (o - mu) * jax.lax.rsqrt(var + LN_EPS) * ln_g + ln_b

    def _L1_ffn_ref(x, router_w, experts_bias, w1, w3, w2, sw1, sw3, sw2):
        import jax, jax.numpy as jnp
        import numpy as np
        D, H, E, K, S = (128, 256, 8, 2, 1)
        B, L = (4, 256)
        b, l, d = x.shape
        xf = x.reshape(-1, d)
        sg = jnp.einsum('td,sdh->tsh', xf, sw1)
        su = jnp.einsum('td,sdh->tsh', xf, sw3)
        shared_out = jnp.einsum('tsh,shd->td', jax.nn.silu(sg) * su, sw2)
        logits = xf @ router_w.T + experts_bias
        rw, sel = jax.lax.top_k(logits, K)
        rw = jax.nn.softmax(rw.astype(jnp.float32), axis=-1).astype(x.dtype)
        cw = (jax.nn.one_hot(sel, E, dtype=x.dtype) * rw[..., None]).sum(axis=1)
        g = jnp.einsum('td,edh->teh', xf, w1)
        u = jnp.einsum('td,edh->teh', xf, w3)
        eo = jax.nn.silu(g) * u
        moe_out = jnp.einsum('te,teh,ehd->td', cw, eo, w2)
        return (moe_out + shared_out).reshape(b, l, d)

    def _L2_attn_ref(x, ln_g, ln_b, w_qkv, b_qkv, w_gate, b_gate, w_proj, b_proj):
        import jax, jax.numpy as jnp
        import numpy as np
        D_MODEL = 128
        N_HEADS = 16
        D_HEAD = D_MODEL // N_HEADS
        B, T = (2, 256)
        Bb, Tt, Dd = x.shape
        H, dh = (N_HEADS, D_HEAD)
        mu = jnp.mean(x, axis=-1, keepdims=True)
        var = jnp.mean((x - mu) ** 2, axis=-1, keepdims=True)
        x_norm = (x - mu) / jnp.sqrt(var + 1e-05) * ln_g + ln_b
        qkv = x_norm @ w_qkv + b_qkv
        q, k, v = jnp.split(qkv, 3, axis=-1)
        gate_sig = jax.nn.sigmoid(x @ w_gate + b_gate)
        gate_norm = gate_sig / (jnp.mean(gate_sig, axis=-1, keepdims=True) + 1e-05)
        q = q * gate_norm
        k = k * gate_norm

        def to_heads(t):
            return t.reshape(Bb, Tt, H, dh).transpose(0, 2, 1, 3)
        q, k, v = (to_heads(q), to_heads(k), to_heads(v))
        q = jax.nn.elu(q) + 1.0
        k = jax.nn.elu(k) + 1.0
        kv = jnp.einsum('bhtd,bhtm->bhtdm', k, v)
        kv_cumsum = jnp.cumsum(kv, axis=2)
        out_num = jnp.einsum('bhtd,bhtdm->bhtm', q, kv_cumsum)
        k_cumsum = jnp.cumsum(k, axis=2)
        out_den = jnp.einsum('bhtd,bhtd->bht', q, k_cumsum)[..., None] + 1e-05
        out = out_num / out_den
        out = out.transpose(0, 2, 1, 3).reshape(Bb, Tt, Dd)
        return out @ w_proj + b_proj

    def _L2_ffn_ref(x, norm1_w, Wq, Wk, Wv, Wo, norm2_w, router_w, router_b, W1, b1, W2, b2, W3, b3):
        import jax, jax.numpy as jnp
        import numpy as np
        D_MODEL = 128
        N_HEADS = 16
        N_GROUPS = 4
        D_FF = 512
        N_EXPERTS = 8
        TOP_K = 2
        BATCH = 2
        SEQ = 128
        D_K = D_MODEL // N_HEADS
        HPG = N_HEADS // N_GROUPS
        EPS = 1e-06

        def rms_norm(x, w):
            rms = jnp.sqrt(jnp.mean(x * x, axis=-1, keepdims=True) + EPS)
            return x / rms * w

        def rope(x):
            d = x.shape[-1]
            half = d // 2
            theta = 1.0 / 10000.0 ** (jnp.arange(half, dtype=jnp.float32) / half)
            pos = jnp.arange(x.shape[1], dtype=jnp.float32)[:, None]
            ang = pos * theta[None, :]
            cos, sin = (jnp.cos(ang), jnp.sin(ang))
            xe, xo = (x[..., 0::2], x[..., 1::2])
            return jnp.concatenate([xe * cos - xo * sin, xe * sin + xo * cos], axis=-1)

        def attention(x, Wq, Wk, Wv, Wo):
            B, S, _ = x.shape
            xr = rope(x)
            Q = (xr @ Wq).reshape(B, S, N_HEADS, D_K).transpose(0, 2, 1, 3)
            Q = Q.reshape(B, N_GROUPS, HPG, S, D_K)
            K = (xr @ Wk).reshape(B, S, N_GROUPS, D_K).transpose(0, 2, 1, 3)
            V = (xr @ Wv).reshape(B, S, N_GROUPS, D_K).transpose(0, 2, 1, 3)
            scores = jnp.einsum('bghsd,bgtd->bghst', Q, K) / jnp.sqrt(jnp.float32(D_K))
            mask = jnp.triu(jnp.full((S, S), -1000000000.0, dtype=scores.dtype), k=1)
            attn = jax.nn.softmax(scores + mask, axis=-1)
            out = jnp.einsum('bghst,bgtd->bghsd', attn, V)
            out = out.reshape(B, N_HEADS, S, D_K).transpose(0, 2, 1, 3).reshape(B, S, D_MODEL)
            return out @ Wo

        def moe(x, router_w, router_b, W1, b1, W2, b2, W3, b3):
            B, S, _ = x.shape
            logits = x @ router_w + router_b
            topv, topi = jax.lax.top_k(logits, TOP_K)
            topw = jax.nn.softmax(topv, axis=-1)
            onehot = jax.nn.one_hot(topi, N_EXPERTS, dtype=x.dtype)
            comb = jnp.einsum('bsk,bske->bse', topw, onehot)
            h1 = jnp.einsum('bsd,edf->ebsf', x, W1) + b1[:, None, None, :]
            h2 = jnp.einsum('bsd,edf->ebsf', x, W2) + b2[:, None, None, :]
            h = h2 * jax.nn.silu(h1)
            eo = jnp.einsum('ebsf,efd->ebsd', h, W3) + b3[:, None, None, :]
            return jnp.einsum('bse,ebsd->bsd', comb, eo)
        h = x + attention(rms_norm(x, norm1_w), Wq, Wk, Wv, Wo)
        h = h + moe(rms_norm(h, norm2_w), router_w, router_b, W1, b1, W2, b2, W3, b3)
        return h

    def _L3_attn_ref(x, norm_w, op_w, op_b, f_in_w, f_conv_w, f_conv_b, f_dt_bias, f_A_log, f_D, f_gnorm_w, f_outp_w, b_in_w, b_conv_w, b_conv_b, b_dt_bias, b_A_log, b_D, b_gnorm_w, b_outp_w):
        import jax, jax.numpy as jnp
        import numpy as np
        B, L = (2, 256)
        D_MODEL = 128
        D_STATE = 128
        D_CONV = 4
        EXPAND = 2
        HEADDIM = 64
        D_HALF = D_MODEL // 2
        D_INNER = EXPAND * D_HALF
        NHEADS = D_INNER // HEADDIM
        CONV_DIM = D_INNER + 2 * D_STATE
        D_IN_PROJ = 2 * D_INNER + 2 * D_STATE + NHEADS
        EPS = 1e-05

        def _rmsnorm(x, w):
            return x * jax.lax.rsqrt(jnp.mean(x * x, axis=-1, keepdims=True) + EPS) * w

        def _mamba2(u, in_w, conv_w, conv_b, dt_bias, A_log, D, gnorm_w, outp_w):
            b, l, _ = u.shape
            zxbcdt = u @ in_w.T
            z = zxbcdt[..., :D_INNER]
            xBC = zxbcdt[..., D_INNER:D_INNER + CONV_DIM]
            dt = zxbcdt[..., D_INNER + CONV_DIM:]
            xp = jnp.pad(xBC, ((0, 0), (D_CONV - 1, 0), (0, 0)))
            conv = conv_b + sum((xp[:, k:k + l, :] * conv_w[:, k] for k in range(D_CONV)))
            xBC = jax.nn.silu(conv)
            x = xBC[..., :D_INNER]
            Bm = xBC[..., D_INNER:D_INNER + D_STATE]
            Cm = xBC[..., D_INNER + D_STATE:]
            dt = jax.nn.softplus(dt + dt_bias)
            A = -jnp.exp(A_log)
            xh = x.reshape(b, l, NHEADS, HEADDIM)
            dA = jnp.exp(dt * A)
            dtx = dt[..., None] * xh

            def step(h, inp):
                dA_t, dtx_t, B_t, C_t = inp
                h = dA_t[:, :, None, None] * h + jnp.einsum('bhp,bn->bhpn', dtx_t, B_t)
                return (h, jnp.einsum('bhpn,bn->bhp', h, C_t))
            h0 = jnp.zeros((b, NHEADS, HEADDIM, D_STATE), u.dtype)
            xs = (jnp.moveaxis(dA, 1, 0), jnp.moveaxis(dtx, 1, 0), jnp.moveaxis(Bm, 1, 0), jnp.moveaxis(Cm, 1, 0))
            _, ys = jax.lax.scan(step, h0, xs)
            y = jnp.moveaxis(ys, 0, 1) + xh * D[None, None, :, None]
            y = y.reshape(b, l, D_INNER) * jax.nn.silu(z)
            y = _rmsnorm(y, gnorm_w)
            return y @ outp_w.T

        def _forward(x, norm_w, op_w, op_b, f_in_w, f_conv_w, f_conv_b, f_dt_bias, f_A_log, f_D, f_gnorm_w, f_outp_w, b_in_w, b_conv_w, b_conv_b, b_dt_bias, b_A_log, b_D, b_gnorm_w, b_outp_w):
            xn = _rmsnorm(x, norm_w)
            x_f, x_b = (xn[..., :D_HALF], xn[..., D_HALF:])
            out_f = _mamba2(x_f, f_in_w, f_conv_w, f_conv_b, f_dt_bias, f_A_log, f_D, f_gnorm_w, f_outp_w)
            out_b = jnp.flip(_mamba2(jnp.flip(x_b, 1), b_in_w, b_conv_w, b_conv_b, b_dt_bias, b_A_log, b_D, b_gnorm_w, b_outp_w), 1)
            out = jnp.concatenate([out_f, out_b], axis=-1) @ op_w.T + op_b
            return x + out

        def _mamba_params(key, prefix):
            k = jax.random.split(key, 5)
            return {prefix + 'in_w': jax.random.normal(k[0], (D_IN_PROJ, D_HALF), jnp.float32) * 0.02, prefix + 'conv_w': jax.random.normal(k[1], (CONV_DIM, D_CONV), jnp.float32) * 0.2, prefix + 'conv_b': jnp.zeros((CONV_DIM,), jnp.float32), prefix + 'dt_bias': jax.random.normal(k[2], (NHEADS,), jnp.float32) * 0.1, prefix + 'A_log': jnp.log(jax.random.uniform(k[3], (NHEADS,), jnp.float32, 1.0, 16.0)), prefix + 'D': jnp.ones((NHEADS,), jnp.float32), prefix + 'gnorm_w': jnp.ones((D_INNER,), jnp.float32), prefix + 'outp_w': jax.random.normal(k[4], (D_HALF, D_INNER), jnp.float32) * 0.02}
        return _forward(x, norm_w, op_w, op_b, f_in_w, f_conv_w, f_conv_b, f_dt_bias, f_A_log, f_D, f_gnorm_w, f_outp_w, b_in_w, b_conv_w, b_conv_b, b_dt_bias, b_A_log, b_D, b_gnorm_w, b_outp_w)

    def _L3_ffn_ref(x, router_w, router_bias, up_proj, gate_proj, down_proj, sh_gate, sh_up, sh_down):
        import jax, jax.numpy as jnp
        import numpy as np
        DIM = 128
        EXPERT_DIM = 64
        N_EXPERTS = 16
        TOPK = 2
        SHARED_HIDDEN = EXPERT_DIM * TOPK
        B, T = (4, 128)

        def _moe_forward(x, router_w, router_bias, up_proj, gate_proj, down_proj, sh_gate, sh_up, sh_down):
            Bb, Tt, D = x.shape
            flat = x.reshape(Bb * Tt, D)
            N = flat.shape[0]
            logits = flat @ router_w.T
            topk_scores, topk_idx = jax.lax.top_k(logits + router_bias, TOPK)
            topk_scores = jax.nn.softmax(topk_scores, axis=-1)
            combine = jnp.zeros((N, N_EXPERTS), flat.dtype)
            combine = combine.at[jnp.arange(N)[:, None], topk_idx].add(topk_scores)
            up_all = jnp.einsum('nd,kde->nke', flat, up_proj)
            gate_all = jnp.einsum('nd,kde->nke', flat, gate_proj)
            hidden = jax.nn.silu(gate_all) * up_all
            down_all = jnp.einsum('nke,ked->nkd', hidden, down_proj)
            out = jnp.einsum('nk,nkd->nd', combine, down_all)
            sh_hidden = jax.nn.silu(flat @ sh_gate.T) * (flat @ sh_up.T)
            out = out + sh_hidden @ sh_down.T
            return out.reshape(Bb, Tt, D)
        return _moe_forward(x, router_w, router_bias, up_proj, gate_proj, down_proj, sh_gate, sh_up, sh_down)
    x = L0_attn_u
    xn = _layernorm(x, axis=-1)
    s = _L0_attn_ref(xn, L0_attn_W_in, L0_attn_conv_w, L0_attn_conv_b, L0_attn_dt_bias, L0_attn_A_log, L0_attn_D, L0_attn_norm_weight, L0_attn_W_out)
    g = _silu(_L0_ffn_ref(xn, L0_ffn_w1, L0_ffn_b1, L0_ffn_w2, L0_ffn_b2, L0_ffn_centroids, L0_ffn_w_route))
    x = x + s * g
    xn = _layernorm(x, axis=-1)
    s = _L1_attn_ref(xn, L1_attn_Wq, L1_attn_Wk, L1_attn_Wv, L1_attn_Wb, L1_attn_ln_g, L1_attn_ln_b)
    g = _silu(_L1_ffn_ref(xn, L1_ffn_router_w, L1_ffn_experts_bias, L1_ffn_w1, L1_ffn_w3, L1_ffn_w2, L1_ffn_sw1, L1_ffn_sw3, L1_ffn_sw2))
    x = x + s * g
    xn = _layernorm(x, axis=-1)
    s = _L2_attn_ref(xn, L2_attn_ln_g, L2_attn_ln_b, L2_attn_w_qkv, L2_attn_b_qkv, L2_attn_w_gate, L2_attn_b_gate, L2_attn_w_proj, L2_attn_b_proj)
    g = _silu(_L2_ffn_ref(xn, L2_ffn_norm1_w, L2_ffn_Wq, L2_ffn_Wk, L2_ffn_Wv, L2_ffn_Wo, L2_ffn_norm2_w, L2_ffn_router_w, L2_ffn_router_b, L2_ffn_W1, L2_ffn_b1, L2_ffn_W2, L2_ffn_b2, L2_ffn_W3, L2_ffn_b3))
    x = x + s * g
    xn = _layernorm(x, axis=-1)
    s = _L3_attn_ref(xn, L3_attn_norm_w, L3_attn_op_w, L3_attn_op_b, L3_attn_f_in_w, L3_attn_f_conv_w, L3_attn_f_conv_b, L3_attn_f_dt_bias, L3_attn_f_A_log, L3_attn_f_D, L3_attn_f_gnorm_w, L3_attn_f_outp_w, L3_attn_b_in_w, L3_attn_b_conv_w, L3_attn_b_conv_b, L3_attn_b_dt_bias, L3_attn_b_A_log, L3_attn_b_D, L3_attn_b_gnorm_w, L3_attn_b_outp_w)
    g = _silu(_L3_ffn_ref(xn, L3_ffn_router_w, L3_ffn_router_bias, L3_ffn_up_proj, L3_ffn_gate_proj, L3_ffn_down_proj, L3_ffn_sh_gate, L3_ffn_sh_up, L3_ffn_sh_down))
    x = x + s * g
    return x

_drawn_inputs = setup_inputs


def setup_inputs(seed=0):
    import zlib

    import numpy as np

    out = dict(_drawn_inputs(seed))
    spreads = {'L0_attn_conv_b': (0.0, 0.1),
     'L0_attn_D': (1.0, 0.6),
     'L0_attn_norm_weight': (1.0, 0.6),
     'L0_ffn_b1': (0.0, 0.8),
     'L0_ffn_b2': (0.0, 0.66),
     'L1_attn_ln_g': (1.0, 0.6),
     'L1_attn_ln_b': (0.0, 0.8),
     'L1_ffn_experts_bias': (0.0, 0.8),
     'L2_attn_ln_g': (1.0, 0.6),
     'L2_attn_ln_b': (0.0, 0.1),
     'L2_attn_b_qkv': (0.0, 0.1),
     'L2_attn_b_gate': (0.0, 0.8),
     'L2_attn_b_proj': (0.0, 0.1),
     'L2_ffn_norm1_w': (1.0, 0.6),
     'L2_ffn_norm2_w': (1.0, 0.6),
     'L2_ffn_router_b': (0.0, 0.8),
     'L2_ffn_b1': (0.0, 0.8),
     'L2_ffn_b2': (0.0, 0.8),
     'L2_ffn_b3': (0.0, 0.8),
     'L3_attn_norm_w': (1.0, 0.6),
     'L3_attn_op_b': (0.0, 0.8),
     'L3_attn_f_conv_b': (0.0, 0.8),
     'L3_attn_f_D': (1.0, 0.6),
     'L3_attn_f_gnorm_w': (1.0, 0.6),
     'L3_attn_b_conv_b': (0.0, 0.8),
     'L3_attn_b_D': (1.0, 0.6),
     'L3_attn_b_gnorm_w': (1.0, 0.6),
     'L3_ffn_router_bias': (0.0, 0.8)}
    factors = {'L0_attn_dt_bias': 8.0,
     'L0_attn_A_log': 8.0,
     'L0_ffn_centroids': 3.26,
     'L1_attn_Wq': 8.0,
     'L1_attn_Wk': 8.0,
     'L1_attn_Wv': 8.0,
     'L1_attn_Wb': 8.0,
     'L1_ffn_router_w': 8.0,
     'L1_ffn_w1': 8.0,
     'L1_ffn_w3': 8.0,
     'L1_ffn_w2': 8.0,
     'L1_ffn_sw1': 8.0,
     'L1_ffn_sw3': 8.0,
     'L1_ffn_sw2': 8.0,
     'L2_attn_w_gate': 8.0,
     'L2_ffn_Wq': 8.0,
     'L2_ffn_Wk': 8.0,
     'L2_ffn_Wv': 8.0,
     'L2_ffn_Wo': 8.0,
     'L2_ffn_router_w': 6.781,
     'L2_ffn_W1': 8.0,
     'L2_ffn_W2': 8.0,
     'L2_ffn_W3': 8.0,
     'L3_attn_op_w': 8.0,
     'L3_attn_f_in_w': 8.0,
     'L3_attn_f_conv_w': 8.0,
     'L3_attn_f_dt_bias': 8.0,
     'L3_attn_f_A_log': 8.0,
     'L3_attn_f_outp_w': 8.0,
     'L3_attn_b_in_w': 8.0,
     'L3_attn_b_conv_w': 8.0,
     'L3_attn_b_dt_bias': 8.0,
     'L3_attn_b_A_log': 8.0,
     'L3_attn_b_outp_w': 8.0,
     'L3_ffn_router_w': 8.0,
     'L3_ffn_up_proj': 8.0,
     'L3_ffn_gate_proj': 8.0,
     'L3_ffn_down_proj': 8.0,
     'L3_ffn_sh_gate': 8.0,
     'L3_ffn_sh_up': 8.0,
     'L3_ffn_sh_down': 8.0}
    for name, (base, spread) in spreads.items():
        noise = np.random.default_rng([zlib.crc32(name.encode()), seed]).standard_normal(out[name].shape)
        drawn = base * np.exp(spread * noise) if base else spread * noise
        out[name] = jnp.asarray(drawn.astype(out[name].dtype))
    for name, factor in factors.items():
        out[name] = (out[name] * factor).astype(out[name].dtype)
    return out
```

```python
from contextlib import ExitStack

import concourse.bass as bass
from concourse import mybir

F32 = mybir.dt.float32
BF16 = mybir.dt.bfloat16
I32 = mybir.dt.int32
ALU = mybir.AluOpType
ACT = mybir.ActivationFunctionType
AX = mybir.AxisListType.X

P = 128
D = 128
NBATCH = 2
SEQ = 1024
TPB = SEQ // P
NT = NBATCH * TPB
BLK = 512
TB = BLK // P
NBLK = NT // TB
SBUF_COLS = 53184
LN_EPS = 1e-5


class Pack:

    def __init__(self):
        self.at, self.n, self.ends = {}, 0, {}

    def add(self, name, cols):
        self.at[name] = (self.n, cols)
        self.n += cols

    def end(self, part):
        self.ends[part] = self.n


def layout():
    k = Pack()
    for name, cols in (("ident", P), ("triU", P), ("triL", P), ("ones", P), ("idx8", 8), ("idx16", 16)):
        k.add(name, cols)
    for name, cols in (("m0_zdt", 260), ("m0_xbc", 512), ("m0_cw", 16), ("m0_cb", 4), ("m0_dtb", 4),
                       ("m0_alog", 4), ("m0_D", 4), ("m0_nw", 2), ("m0_out", 256),
                       ("f0_w1", 512), ("f0_b1", 4), ("f0_w2", 512), ("f0_b2", P), ("f0_rt", 16),
                       ("f0_sel", 512)):
        k.add(name, cols)
    k.end(0)
    for name, cols in (("a1_q", P), ("a1_kvb", 257), ("a1_g", P), ("a1_b", P), ("lvlT", 7 * P),
                       ("lvl1", P), ("f1_rt", 8), ("f1_rb", 8), ("f1_w1", 9 * 256), ("f1_w3", 9 * 256),
                       ("f1_w2", 9 * 256)):
        k.add(name, cols)
    k.end(1)
    for name, cols in (("a2_g", 1), ("a2_b", 1), ("a2_qkv", 384), ("a2_bqkv", 384), ("a2_gate", P),
                       ("a2_bgate", P), ("a2_proj", P), ("a2_bproj", P), ("a2_bd", 36),
                       ("negU", P), ("negL", P), ("cos", TPB * 64), ("sin", TPB * 64),
                       ("f2_n1", P), ("f2_qkv", 192), ("f2_wo", P), ("f2_n2", 1), ("f2_rt", 8), ("f2_rb", 8),
                       ("f2_b1", 32), ("f2_b2", 32), ("f2_b3", P)):
        k.add(name, cols)
    k.end(2)
    for name, cols in (("m3_nw", 1), ("m3_zdt", 130), ("m3_xbc", 384), ("m3_cwf", 12), ("m3_cwb", 12),
                       ("m3_cbf", 3), ("m3_cbb", 3), ("m3_dtbf", 2), ("m3_dtbb", 2), ("m3_alogf", 2),
                       ("m3_alogb", 2), ("m3_Df", 2), ("m3_Db", 2), ("m3_gn", 2), ("m3_outp", P),
                       ("m3_opw", P), ("m3_opb", P),
                       ("f3_rt", 16), ("f3_rb", 16), ("f3_gate", 9 * P), ("f3_up", 9 * P),
                       ("f3_down", 9 * P), ("f3_sel", 8 * P)):
        k.add(name, cols)
    k.end(3)
    for name in ("f2_w1", "f2_w2", "f2_w3"):
        k.add(name, 4096)
    k.end(4)
    return k


class Line:

    def __init__(self, engine, sem, name):
        self.e, self.sem, self.name, self.count, self.seen = engine, sem, name, 0, {}

    def mark(self, ins):
        self.count += 1
        ins.then_inc(self.sem, 1)
        return (self.name, self.sem, self.count)

    def wait(self, *marks):
        for name, sem, value in marks:
            if self.seen.get(name, 0) < value:
                self.e.wait_ge(sem, value)
                self.seen[name] = value

    def then(self, ins):
        m = self.mark(ins)
        self.wait(m)
        return m


class Ring:

    def __init__(self, views):
        self.views = list(views)
        self.free = list(range(len(self.views)))
        self.last_use = [()] * len(self.views)

    def next(self):
        i = self.free.pop(0)
        return i, self.views[i]

    def done(self, i, *marks):
        self.last_use[i] = marks
        self.free.append(i)


class Arena:

    def __init__(self):
        self.rooms = []

    def start(self, *rooms):
        self.rooms = [list(r) for r in rooms]

    def f32(self, cols):
        for room in self.rooms:
            tensor, a, end = room
            if a + cols <= end:
                room[1] = a + cols
                return tensor[:, a:a + cols]
        raise AssertionError(("no room for", cols, [r[2] - r[1] for r in self.rooms]))

    def bf16(self, cols):
        return self.f32(cols // 2).bitcast(BF16)


def interleave(*streams):
    live = list(streams)
    while live:
        left = []
        for gen, n in live:
            ended = False
            for _ in range(n):
                if next(gen, None) is None:
                    ended = True
                    break
            if not ended:
                left.append((gen, n))
        live = left


def in_turn(*gens):
    for g in gens:
        yield from g


def lanes(ap, n, w):
    return ap.unsqueeze(2).to_broadcast([ap.shape[0], n, w])


def again(ap, n):
    return ap.unsqueeze(1).to_broadcast([ap.shape[0], n, ap.shape[1]])


def split(ap, n):
    return ap.rearrange("p (a b) -> p a b", a=n)


class Shared:
    pass


def core(nc, ctx, x_dram, w_dram, out_dram):
    k = Shared()
    k.nc = nc

    def line(engine, name):
        return Line(engine, ctx.enter_context(nc.semaphore("done_" + name)), name)

    k.pe, k.dve, k.act = line(nc.tensor, "pe"), line(nc.vector, "dve"), line(nc.scalar, "act")
    k.pool, k.sp = line(nc.gpsimd, "pool"), line(nc.sync, "sp")
    k.pack = layout()
    ends = k.pack.ends
    k.wide = ends[4] - ends[3]
    assert ends[3] - ends[2] <= ends[1] - ends[0]
    n_arena = SBUF_COLS - ends[2] - NT * P * 5
    k.w_all = ctx.enter_context(nc.sbuf_tensor("weights", [P, ends[2]], F32))
    k.x = ctx.enter_context(nc.sbuf_tensor("x", [P, NT, D], F32))
    k.xn = ctx.enter_context(nc.sbuf_tensor("xn", [P, NT, D], F32))
    k.xnT = ctx.enter_context(nc.sbuf_tensor("xnT", [P, NT * P], F32))
    k.s = ctx.enter_context(nc.sbuf_tensor("s", [P, NT, D], F32))
    k.g = ctx.enter_context(nc.sbuf_tensor("g", [P, NT, D], F32))
    k.arena_all = ctx.enter_context(nc.sbuf_tensor("arena", [P, n_arena], F32))
    k.arena = Arena()
    k.n_arena = n_arena
    k.ps = ctx.enter_context(nc.psum_tensor("banks", [P, 8, BLK], F32))
    k.banks = Ring([k.ps[:, b, :] for b in range(8)])
    k.x_in = [ctx.enter_context(nc.semaphore(f"x_in{i}")) for i in range(NBLK)]
    k.w_in = [ctx.enter_context(nc.semaphore(f"w_in{i}")) for i in range(5)]
    k.out_sem = ctx.enter_context(nc.semaphore("out_written"))
    k.x_dram, k.w_dram, k.out_dram = x_dram, w_dram, out_dram
    k.x_ready = [None] * NBLK
    k.xn_ready = [None] * NBLK
    k.xnT_ready = [None] * NBLK
    k.s_ready = [None] * NT
    k.g_ready = [None] * NT
    return k


def weight(k, name, rows=slice(0, P)):
    a, n = k.pack.at[name]
    ends = k.pack.ends
    if a >= ends[3]:
        a += k.n_arena - ends[4]
        return k.arena_all[rows, a:a + n]
    if a >= ends[2]:
        a += ends[0] - ends[2]
    return k.w_all[rows, a:a + n]


def load_part(k, part, dst):
    a, b = k.pack.ends[part - 1] if part else 0, k.pack.ends[part]
    mid = (a + b) // 2
    for lo, hi in ((a, mid), (mid, b)):
        k.sp.e.dma_start(dst[:, lo - a:hi - a], k.w_dram[:, lo:hi]).then_inc(k.w_in[part], 16)


def late_loads(k, part):
    k.sp.wait(*[(o.name, o.sem, o.count) for o in (k.pe, k.dve, k.act, k.pool) if o.count])
    n = k.n_arena
    ends = k.pack.ends
    dst = k.w_all[:, ends[0]:ends[0] + ends[3] - ends[2]] if part == 3 else k.arena_all[:, n - k.wide:n]
    load_part(k, part, dst)


def loads(k):
    src = k.x_dram.rearrange("b (t p) d -> p (b t) d", p=P)
    for i in range(NBLK):
        t = slice(i * TB, (i + 1) * TB)
        k.act.e.dma_start(k.x[:, t, :], src[:, t, :]).then_inc(k.x_in[i], 16)
        k.x_ready[i] = (f"x_in{i}", k.x_in[i], 16)
    ends = [0] + [k.pack.ends[i] for i in range(3)]
    for part in range(3):
        load_part(k, part, k.w_all[:, ends[part]:ends[part + 1]])


def weights_ready(k, layer):
    mark = (f"w_in{layer}", k.w_in[layer], 32)
    for line in (k.pe, k.dve, k.act, k.pool):
        line.wait(mark)


def barrier(k):
    lines = (k.pe, k.dve, k.act, k.pool)
    marks = [(o.name, o.sem, o.count) for o in lines if o.count]
    for line in lines:
        line.wait(*marks)


def open_arena(k, layer):
    barrier(k)
    ends = k.pack.ends
    whole = (k.arena_all, 0, k.n_arena)
    below_experts = (k.arena_all, 0, k.n_arena - k.wide)
    part0 = (k.w_all, k.pack.at["m0_zdt"][0], ends[0])
    part1 = (k.w_all, ends[0] + ends[3] - ends[2], ends[1])
    k.arena.start(*{0: (whole,), 1: (part0, below_experts), 2: (part0, part1, below_experts),
                       3: (part0, whole)}[layer])


def matmul(k, out, lhsT, rhs, start=True, stop=True):
    return k.pe.e.matmul(out, lhsT, rhs, start=start, stop=stop, skip_group_check=True)


def rsqrt(k, y, v, t):
    dve = k.dve
    dve.then(dve.e.tensor_scalar(y.bitcast(I32), v.bitcast(I32), -0.5, 1597463007.0, ALU.mult, ALU.add))
    for _ in range(3):
        dve.then(dve.e.scalar_tensor_tensor(t, v, -0.5, y, ALU.mult, ALU.mult))
        dve.then(dve.e.tensor_tensor(t, t, y, ALU.mult))
        m = dve.then(dve.e.scalar_tensor_tensor(y, t, 1.5, y, ALU.add, ALU.mult))
    return m


def layernorm(k):
    pe, dve, act = k.pe, k.dve, k.act
    st = k.arena.f32(NT * 6).rearrange("p (t c) -> p t c", c=6)
    mv = k.arena.f32(NT * 2).rearrange("p (t c) -> p t c", c=2)
    var, rs, tmp = k.arena.f32(NT), k.arena.f32(NT), k.arena.f32(NT)
    for i in range(NBLK):
        g = slice(i * TB, (i + 1) * TB)
        dve.wait(k.x_ready[i])
        for t in range(i * TB, (i + 1) * TB):
            m = dve.mark(dve.e.bn_stats(st[:, t, :], k.x[:, t, :]))
        dve.wait(m)
        for t in range(i * TB, (i + 1) * TB):
            m = dve.mark(dve.e.bn_aggr(mv[:, t, :], st[:, t, :]))
        dve.wait(m)
        dve.then(dve.e.tensor_scalar(var[:, g], mv[:, g, 1], LN_EPS, None, ALU.add))
        rsqrt(k, rs[:, g], var[:, g], tmp[:, g])
        for t in range(i * TB, (i + 1) * TB):
            m = dve.mark(dve.e.tensor_scalar(k.xn[:, t, :], k.x[:, t, :], mv[:, t, 0:1], rs[:, t:t + 1],
                                             ALU.subtract, ALU.mult))
        k.xn_ready[i] = m
        b, bank = k.banks.next()
        pe.wait(*k.banks.last_use[b])
        pe.wait(m)
        for q in range(TB):
            tr = pe.e.transpose(bank[:, q * P:(q + 1) * P], k.xn[:, i * TB + q, :], weight(k, "ident"))
        act.wait(pe.mark(tr))
        m = act.mark(act.e.activation(k.xnT[:, i * BLK:(i + 1) * BLK], bank, ACT.Copy))
        k.banks.done(b, m)
        k.xnT_ready[i] = m


def close_layer(k, last=False):
    dve, pool = k.dve, k.pool
    for i in range(NBLK):
        g = slice(i * TB, (i + 1) * TB)
        for t in range(i * TB, (i + 1) * TB):
            dve.wait(k.s_ready[t], k.g_ready[t])
        dve.then(dve.e.tensor_tensor(k.s[:, g, :], k.s[:, g, :], k.g[:, g, :], ALU.mult))
        m = dve.then(dve.e.tensor_tensor(k.x[:, g, :], k.x[:, g, :], k.s[:, g, :], ALU.add))
        k.x_ready[i] = m
        if last:
            k.sp.wait(m)
            dst = k.out_dram.rearrange("b (t p) d -> p (b t) d", p=P)
            k.sp.e.dma_start(dst[:, g, :], k.x[:, g, :]).then_inc(k.out_sem, 16)
    if last:
        k.sp.e.wait_ge(k.out_sem, 16 * NBLK)



def route(k, E, lg, gates, idx, masked_softmax=False, tiles=NT):
    dve, act = k.dve, k.act
    a = k.arena
    shape = lambda: a.f32(tiles * E).rearrange("p (t e) -> p t e", e=E)
    eq, oh1, oh2, l2 = shape(), shape(), shape(), shape()
    m1, m2, mi, ex, sm = (a.f32(tiles) for _ in range(5))
    full = lambda v: lanes(v, tiles, E)
    idxs = again(idx, tiles)

    def first(l, m, oh):
        dve.then(dve.e.tensor_reduce(m, l, AX, ALU.max))
        dve.then(dve.e.tensor_tensor(eq, l, full(m), ALU.is_equal))
        dve.then(dve.e.scalar_tensor_tensor(eq, eq, -64.0, idxs, ALU.mult, ALU.add))
        dve.then(dve.e.tensor_reduce(mi, eq, AX, ALU.min))
        return dve.then(dve.e.tensor_tensor(oh, eq, full(mi), ALU.is_equal))

    first(lg, m1, oh1)
    yield 1
    dve.then(dve.e.scalar_tensor_tensor(l2, oh1, -3e38, lg, ALU.mult, ALU.add))
    first(l2, m2, oh2)
    yield 1
    if masked_softmax:
        dve.then(dve.e.tensor_tensor(oh1, lg, full(m2), ALU.is_ge))
        m = dve.then(dve.e.tensor_tensor(l2, lg, full(m1), ALU.subtract))
        act.wait(m)
        m = act.mark(act.e.activation(l2, l2, ACT.Exp))
        dve.wait(m)
        dve.then(dve.e.tensor_tensor(l2, l2, oh1, ALU.mult))
        dve.then(dve.e.tensor_reduce(sm, l2, AX, ALU.add))
        dve.then(dve.e.reciprocal(sm, sm))
        k.gates_ready = dve.then(dve.e.tensor_tensor(gates, l2, full(sm), ALU.mult))
    else:
        m = dve.then(dve.e.tensor_tensor(ex, m2, m1, ALU.subtract))
        act.wait(m)
        m = act.mark(act.e.activation(ex, ex, ACT.Exp))
        dve.wait(m)
        dve.then(dve.e.tensor_scalar(sm, ex, 1.0, None, ALU.add))
        dve.then(dve.e.reciprocal(sm, sm))
        dve.then(dve.e.tensor_tensor(ex, ex, sm, ALU.mult))
        dve.then(dve.e.tensor_tensor(oh1, oh1, full(sm), ALU.mult))
        dve.then(dve.e.tensor_tensor(oh2, oh2, full(ex), ALU.mult))
        k.gates_ready = dve.then(dve.e.tensor_tensor(gates, oh1, oh2, ALU.add))
    yield 1


def gates_across(k, E, gates, gT, t0=0, tiles=NT):
    pe, act = k.pe, k.act
    for i in range(tiles // TB):
        b, bank = k.banks.next()
        pe.wait(*k.banks.last_use[b])
        pe.wait(k.gates_ready)
        for q in range(TB):
            tr = pe.e.transpose(bank[0:E, q * P:(q + 1) * P], gates[:, i * TB + q, :], weight(k, "ident"))
        act.wait(pe.mark(tr))
        k.gT_ready = act.mark(act.e.activation(gT[0:E, t0 * P + i * BLK:t0 * P + (i + 1) * BLK], bank[0:E, :], ACT.Copy))
        k.banks.done(b, k.gT_ready)
        yield 1


def mamba(k, cfg, batch, buf):
    pe, dve, act, pool = k.pe, k.dve, k.act, k.pool
    H, rows, back = cfg["H"], cfg["rows"], cfg["back"]
    DI = 64 * H
    NX = DI // P
    NCH = NX + 2
    src, src_ready = cfg["xT"], cfg["xT_ready"]
    tri = weight(k, "triL") if back else weight(k, "triU")
    ones = weight(k, "ones")
    tiles = [batch * TPB + t for t in (range(TPB - 1, -1, -1) if back else range(TPB))]
    lo = batch * TPB
    hs = lambda a: a.rearrange("p (t h) -> p t h", h=H)

    for line in (dve, act, pool):
        line.wait(*buf.get("done", ()))
    dt, u, s, z, acc = (buf["small"][name] for name in ("dt", "u", "s", "z", "acc"))
    dA, cA, ecA, seg, etot = (buf["small"][name] for name in ("dA", "cA", "ecA", "seg", "etot"))
    b, bank = k.banks.next()
    pe.wait(*k.banks.last_use[b])
    pe.wait(*[src_ready[t // TB] for t in tiles])
    for t in sorted(tiles):
        mm = matmul(k, bank[:, (t - lo) * H:(t - lo + 1) * H], src[rows, t * P:(t + 1) * P],
                     cfg["zdt"][:, DI:DI + H])
    dve.wait(pe.mark(mm))
    m = dve.then(dve.e.tensor_tensor(hs(dt), hs(bank[:, 0:TPB * H]), again(cfg["dtb"], TPB), ALU.add))
    k.banks.done(b, m)
    dve.then(dve.e.tensor_scalar(u, dt, -1.0, None, ALU.mult))
    m = dve.then(dve.e.tensor_tensor(u, u, dt, ALU.min))
    act.wait(m)
    m = act.mark(act.e.activation(u, u, ACT.Exp))
    dve.wait(m)
    yield 1
    dve.then(dve.e.tensor_scalar(s, u, 2.0, None, ALU.add))
    dve.then(dve.e.reciprocal(s, s))
    dve.then(dve.e.tensor_tensor(s, s, u, ALU.mult))
    dve.then(dve.e.tensor_tensor(z, s, s, ALU.mult))
    dve.then(dve.e.tensor_scalar(acc, z, 1.0 / 17, 1.0 / 15, ALU.mult, ALU.add))
    for odd in (13, 11, 9, 7, 5, 3, 1):
        dve.then(dve.e.tensor_tensor(acc, acc, z, ALU.mult))
        dve.then(dve.e.tensor_scalar(acc, acc, 1.0 / odd, None, ALU.add))
    dve.then(dve.e.scalar_tensor_tensor(acc, acc, 2.0, s, ALU.mult, ALU.mult))
    dve.then(dve.e.scalar_tensor_tensor(dt, dt, 0.0, acc, ALU.max, ALU.add))
    yield 1
    m = act.mark(act.e.activation(cfg["A"], cfg["alog"], ACT.Exp))
    dve.wait(m)
    m = dve.then(dve.e.scalar_tensor_tensor(hs(dA), hs(dt), -1.0, again(cfg["A"], TPB), ALU.mult, ALU.mult))
    b, bank = k.banks.next()
    pe.wait(*k.banks.last_use[b])
    pe.wait(m)
    n = TPB * H
    matmul(k, bank[:, 0:n], tri, dA)
    mm = matmul(k, bank[:, n:2 * n], ones, dA)
    dve.wait(pe.mark(mm))
    dve.then(dve.e.tensor_copy(cA, bank[:, 0:n]))
    m = dve.then(dve.e.tensor_copy(etot, bank[:, n:2 * n]))
    k.banks.done(b, m)
    dve.then(dve.e.tensor_tensor(seg, etot, cA, ALU.subtract))
    m = dve.then(dve.e.tensor_scalar(seg, seg, 0.0, None, ALU.min))
    act.wait(m)
    act.mark(act.e.activation(ecA, cA, ACT.Exp))
    act.mark(act.e.activation(seg, seg, ACT.Exp))
    m = act.mark(act.e.activation(etot, etot, ACT.Exp))
    dve.wait(m)
    pool.wait(m)
    state = buf["state"]
    state_mark = dve.then(dve.e.memset(state[0], 0.0))
    cur = 0
    pre, cv = buf["pre"], buf["cv"]
    tap = (lambda j: 3 - j) if back else (lambda j: j)
    halo = slice(512, 515) if back else slice(0, 3)
    edge = slice(0, 3) if back else slice(512, 515)
    data = slice(0, 512) if back else slice(3, 515)
    m = None
    for ch in range(NCH):
        m = dve.mark(dve.e.memset(pre[ch][:, halo], 0.0))
    halo_mark = m
    state_used = ()
    yield 1

    for nb in range(TPB // TB):
        block = tiles[nb * TB:(nb + 1) * TB]
        c0 = min(block) * P
        conv_marks = []
        for ch in range(NCH):
            b, bank = k.banks.next()
            pe.wait(*k.banks.last_use[b])
            mm = matmul(k, bank, cfg["xbc"][:, ch * P:(ch + 1) * P], src[rows, c0:c0 + BLK])
            act.wait(pe.mark(mm), halo_mark)
            m = act.mark(act.e.activation(pre[ch][:, data], bank, ACT.Copy))
            k.banks.done(b, m)
            dve.wait(m, *buf.get("cv_used", ()))
            o = cv[ch]
            dve.then(dve.e.tensor_scalar(o, pre[ch][:, tap(0):tap(0) + BLK], cfg["cw"][:, 4 * ch:4 * ch + 1],
                                         cfg["cb"][:, ch:ch + 1], ALU.mult, ALU.add))
            for j in (1, 2, 3):
                m = dve.then(dve.e.scalar_tensor_tensor(
                    o, pre[ch][:, tap(j):tap(j) + BLK], cfg["cw"][:, 4 * ch + j:4 * ch + j + 1], o,
                    ALU.mult, ALU.add))
            halo_mark = dve.then(dve.e.tensor_copy(pre[ch][:, halo], pre[ch][:, edge]))
            act.wait(m)
            conv_marks.append(act.mark(act.e.activation(o, o, ACT.Silu)))
            yield 1
        for t in block:
            q = (t * P - c0) // P
            tt = t - lo
            cols = slice(q * P, (q + 1) * P)
            hcol = lambda a: a[:, tt * H:(tt + 1) * H]
            b, bank = k.banks.next()
            pe.wait(*k.banks.last_use[b])
            pe.wait(conv_marks[NCH - 1])
            for ch in range(NX + 1):
                tr = pe.e.transpose(bank[:, ch * P:(ch + 1) * P], cv[ch][:, cols], weight(k, "ident"))
            xi, xb = buf["xb"].next()
            act.wait(*buf["xb"].last_use[xi])
            act.wait(pe.mark(tr))
            m_xb = act.mark(act.e.activation(xb, bank[:, 0:DI + P], ACT.Copy))
            k.banks.done(b, m_xb)
            b, bank = k.banks.next()
            pe.wait(*k.banks.last_use[b])
            mm = matmul(k, bank[:, 0:DI], src[rows, t * P:(t + 1) * P], cfg["zdt"][:, 0:DI])
            matmul(k, bank[:, DI:DI + P], cv[NX][:, cols], cv[NX + 1][:, cols])
            b2, dbank = k.banks.next()
            pe.wait(*k.banks.last_use[b2])
            for h in range(H):
                col = dA[:, tt * H + h:tt * H + h + 1]
                mm = matmul(k, dbank[:, h * P:(h + 1) * P], col.to_broadcast([P, P]), tri)
            m = pe.mark(mm)
            act.wait(m)
            zi, sz = buf["sz"].next()
            act.wait(*buf["sz"].last_use[zi])
            m_z = act.mark(act.e.activation(sz, bank[:, 0:DI], ACT.Silu))
            dve.wait(m, m_z)
            ci, cb = buf["cb"].next()
            dve.wait(*buf["cb"].last_use[ci])
            m = dve.mark(dve.e.tensor_tensor(cb, bank[:, DI:DI + P], tri, ALU.mult))
            k.banks.done(b, m)
            di, dec = buf["dec"].next()
            dve.wait(*buf["dec"].last_use[di])
            for h in range(H):
                m = dve.mark(dve.e.tensor_scalar(dec[:, h * P:(h + 1) * P], dbank[:, h * P:(h + 1) * P],
                                                 cA[:, tt * H + h:tt * H + h + 1], 0.0,
                                                 ALU.subtract, ALU.min))
            k.banks.done(b2, m)
            act.wait(m)
            m = act.mark(act.e.activation(dec, dec, ACT.Exp))
            yield 1
            dve.wait(m_xb)
            xdi, xd = buf["xd"].next()
            dve.wait(*buf["xd"].last_use[xdi])
            xh = xb[:, 0:DI].rearrange("p (h c) -> p h c", h=H)
            m_xd = dve.then(dve.e.tensor_tensor(split(xd[:, 0:DI], H), xh, lanes(hcol(dt), H, 64), ALU.mult))
            m_xs = dve.mark(dve.e.tensor_tensor(split(xd[:, DI:2 * DI], H), split(xd[:, 0:DI], H),
                                                lanes(hcol(seg), H, 64), ALU.mult))
            dve.wait(m)
            m_M = dve.mark(dve.e.tensor_tensor(split(dec, H), split(dec, H), again(cb, H), ALU.mult))
            buf["cb"].done(ci, m_M)
            b, ybank = k.banks.next()
            pe.wait(*k.banks.last_use[b])
            b2, sbank = k.banks.next()
            pe.wait(*k.banks.last_use[b2])
            pe.wait(state_mark, m_xs)
            matmul(k, ybank[:, DI:2 * DI], cv[NX + 1][:, cols], state[cur])
            mm = matmul(k, sbank[:, 0:DI], xb[:, DI:DI + P], xd[:, DI:2 * DI])
            m_st = pe.mark(mm)
            pe.wait(m_M)
            for h in range(H):
                mm = matmul(k, ybank[:, h * 64:(h + 1) * 64], dec[:, h * P:(h + 1) * P],
                             xd[:, h * 64:(h + 1) * 64])
            m_y = pe.mark(mm)
            buf["xd"].done(xdi, m_y)
            buf["dec"].done(di, m_y)
            dve.wait(m_st, *state_used)
            nxt = 1 - cur
            dve.then(dve.e.tensor_tensor(split(state[nxt], H), split(state[cur], H),
                                         lanes(hcol(etot), H, 64), ALU.mult))
            state_mark = dve.mark(dve.e.tensor_tensor(state[nxt], state[nxt], sbank[:, 0:DI], ALU.add))
            k.banks.done(b2, state_mark)
            state_used = (m_y,)
            cur = nxt
            yi, y = buf["y"].next()
            dve.wait(*buf["y"].last_use[yi])
            pool.wait(*buf["y"].last_use[yi])
            y1, y2 = y[:, 0:DI], y[:, DI:2 * DI]
            pool.wait(m_xb)
            m_D = pool.mark(pool.e.tensor_tensor(split(y1, H), xh, lanes(cfg["Dh"], H, 64), ALU.mult))
            buf["xb"].done(xi, m_y, m_D, m_xs)
            dve.wait(m_y)
            dve.then(dve.e.tensor_tensor(split(y2, H), split(ybank[:, DI:2 * DI], H),
                                         lanes(hcol(ecA), H, 64), ALU.mult))
            m = dve.then(dve.e.tensor_tensor(y2, y2, ybank[:, 0:DI], ALU.add))
            k.banks.done(b, m)
            yield 1
            dve.wait(m_D)
            dve.then(dve.e.tensor_tensor(y2, y2, y1, ALU.add))
            dve.wait(m_z)
            m_yz = dve.then(dve.e.tensor_tensor(y2, y2, sz, ALU.mult))
            buf["sz"].done(zi, m_yz)
            act.wait(m_yz)
            m_sq = act.mark(act.e.activation(y1, y2, ACT.Square, accum_out=buf["ss"][:, tt:tt + 1]))
            b, bank = k.banks.next()
            pe.wait(*k.banks.last_use[b])
            pe.wait(m_yz)
            for c in range(NX):
                tr = pe.e.transpose(bank[:, c * P:(c + 1) * P], y2[:, c * P:(c + 1) * P], weight(k, "ident"))
            m = pe.mark(tr)
            buf["y"].done(yi, m, m_sq)
            ti, yT = buf["yT"].next()
            act.wait(*buf["yT"].last_use[ti])
            act.wait(m)
            m = act.mark(act.e.activation(yT, bank[:, 0:DI], ACT.Copy))
            k.banks.done(b, m)
            b, bank = k.banks.next()
            pe.wait(*k.banks.last_use[b])
            pe.wait(m)
            for c in range(NX):
                mm = matmul(k, bank[:, 0:P], yT[:, c * P:(c + 1) * P], cfg["out"][:, c * P:(c + 1) * P],
                             start=(c == 0), stop=(c == NX - 1))
            m = pe.mark(mm)
            buf["yT"].done(ti, m)
            act.wait(m)
            m = act.mark(act.e.activation(buf["so"][:, tt, :], bank[:, 0:P], ACT.Copy))
            k.banks.done(b, m)
            buf["so_mark"] = m
            yield 1
        buf["cv_used"] = (m_y, buf["so_mark"])
    dve.wait(buf["so_mark"])
    dve.then(dve.e.tensor_scalar(buf["ss"], buf["ss"], 1.0 / DI, 1e-5, ALU.mult, ALU.add))
    rsqrt(k, buf["rs"], buf["ss"], buf["tmp"])
    buf["done"] = [(o.name, o.sem, o.count) for o in (pe, dve, act, pool)]
    yield 1


def mamba_buffers(k, H):
    a = k.arena
    DI = 64 * H
    NCH = DI // P + 2
    n = TPB * H
    return dict(
        small={name: a.f32(n) for name in ("dt", "u", "s", "z", "acc", "dA", "cA", "ecA", "seg", "etot")},
        state=[a.f32(DI), a.f32(DI)],
        pre=[a.f32(516) for _ in range(NCH)], cv=[a.f32(BLK) for _ in range(NCH)],
        xb=Ring([a.f32(DI + P) for _ in range(2)]), sz=Ring([a.f32(DI) for _ in range(2)]),
        cb=Ring([a.f32(P) for _ in range(2)]), dec=Ring([a.f32(H * P) for _ in range(2)]),
        xd=Ring([a.f32(2 * DI) for _ in range(2)]), y=Ring([a.f32(2 * DI) for _ in range(2)]),
        yT=Ring([a.f32(DI) for _ in range(2)]), ss=a.f32(TPB), rs=a.f32(TPB), tmp=a.f32(TPB),
        so=a.f32(TPB * D).rearrange("p (t d) -> p t d", d=D))


def layer0_mixer(k, batch, buf):
    dve = k.dve
    cfg = dict(H=4, rows=slice(0, P), back=False, xT=k.xnT, xT_ready=k.xnT_ready,
               zdt=weight(k, "m0_zdt"), xbc=weight(k, "m0_xbc"), cw=weight(k, "m0_cw"), cb=weight(k, "m0_cb"),
               dtb=weight(k, "m0_dtb"), alog=weight(k, "m0_alog"), A=k.m0_A[batch], Dh=weight(k, "m0_D"),
               out=k.m0_out)
    yield from mamba(k, cfg, batch, buf)
    for tt in range(TPB):
        t = batch * TPB + tt
        k.s_ready[t] = dve.mark(dve.e.tensor_scalar(k.s[:, t, :], buf["so"][:, tt, :],
                                                       buf["rs"][:, tt:tt + 1], None, ALU.mult))
    yield 1


def layer0_ffn(k):
    pe, dve, act = k.pe, k.dve, k.act
    a = k.arena
    E, NC = 8, 4
    csq, cinv, tmp8 = a.f32(8), a.f32(8), a.f32(8)
    m = dve.mark(dve.e.tensor_tensor(csq, weight(k, "f0_rt")[:, 0:8], weight(k, "f0_rt")[:, 0:8], ALU.mult))
    b, bank = k.banks.next()
    pe.wait(*k.banks.last_use[b])
    pe.wait(m)
    dve.wait(pe.mark(matmul(k, bank[:, 0:8], weight(k, "ones"), csq)))
    m = dve.then(dve.e.tensor_scalar(csq, bank[:, 0:8], 1e-24, None, ALU.max))
    k.banks.done(b, m)
    rsqrt(k, cinv, csq, tmp8)
    yield 1
    xsq, xinv, tmp = a.f32(NT), a.f32(NT), a.f32(NT)
    junk = a.f32(P)
    for t in range(NT):
        act.wait(k.xn_ready[t // TB])
        m = act.then(act.e.activation(junk, k.xn[:, t, :], ACT.Square, accum_out=xsq[:, t:t + 1]))
    dve.wait(m)
    dve.then(dve.e.tensor_scalar(xsq, xsq, 1e-24, None, ALU.max))
    rsqrt(k, xinv, xsq, tmp)
    yield 1
    lg = a.f32(NT * E).rearrange("p (t e) -> p t e", e=E)
    b, bank = k.banks.next()
    pe.wait(*k.banks.last_use[b])
    pe.wait(*k.xnT_ready)
    for t in range(NT):
        mm = matmul(k, bank[:, 16 * t:16 * t + 16], k.xnT[:, t * P:(t + 1) * P], weight(k, "f0_rt"))
    dve.wait(pe.mark(mm))
    dots = bank[:, 0:16 * NT].rearrange("p (t e) -> p t e", e=16)
    dve.then(dve.e.tensor_tensor(lg, dots[:, :, 0:8], again(cinv, NT), ALU.mult))
    dve.then(dve.e.tensor_tensor(lg, lg, lanes(xinv, NT, E), ALU.mult))
    m = dve.then(dve.e.tensor_tensor(lg, lg, dots[:, :, 8:16], ALU.add))
    k.banks.done(b, m)
    yield 1
    gates = a.f32(NT * E).rearrange("p (t e) -> p t e", e=E)
    yield from route(k, E, lg, gates, weight(k, "idx8"), masked_softmax=True)
    gT = a.f32(NT * P)
    yield from gates_across(k, E, gates, gT)
    hid = Ring([a.f32(BLK) for _ in range(3)])
    pe.wait(k.gT_ready)
    for i in range(NBLK):
        cols = slice(i * BLK, (i + 1) * BLK)
        ob, obank = k.banks.next()
        pe.wait(*k.banks.last_use[ob])

        def down(c, hi, h, m_h):
            pe.wait(m_h)
            for q in range(TB):
                mm = matmul(k, obank[:, q * P:(q + 1) * P], h[:, q * P:(q + 1) * P],
                             weight(k, "f0_w2")[:, c * P:(c + 1) * P], start=(c == 0 and q == 0), stop=False)
            hid.done(hi, pe.mark(mm))

        late = None
        for c in range(NC):
            b, bank = k.banks.next()
            pe.wait(*k.banks.last_use[b])
            m_g = pe.mark(matmul(k, bank, weight(k, "f0_w1")[:, c * P:(c + 1) * P], k.xnT[:, cols]))
            b2, cbank = k.banks.next()
            pe.wait(*k.banks.last_use[b2])
            m_c = pe.mark(matmul(k, cbank, weight(k, "f0_sel")[0:E, c * P:(c + 1) * P], gT[0:E, cols]))
            hi, h = hid.next()
            act.wait(*hid.last_use[hi])
            act.wait(m_g)
            m = act.mark(act.e.activation(h, bank, ACT.Gelu, bias=weight(k, "f0_b1")[:, c:c + 1]))
            k.banks.done(b, m)
            dve.wait(m, m_c)
            m = dve.mark(dve.e.tensor_tensor(h, h, cbank, ALU.mult))
            k.banks.done(b2, m)
            if late:
                down(*late)
            late = (c, hi, h, m)
            yield 1
        down(*late)
        for q in range(TB):
            mm = matmul(k, obank[:, q * P:(q + 1) * P], gT[0:E, i * BLK + q * P:i * BLK + (q + 1) * P],
                         weight(k, "f0_b2", slice(0, E)), start=False, stop=True)
        act.wait(pe.mark(mm))
        m = act.mark(act.e.activation(k.g[:, i * TB:(i + 1) * TB, :], split(obank, TB), ACT.Silu))
        k.banks.done(ob, m)
        for t in range(i * TB, (i + 1) * TB):
            k.g_ready[t] = m
        yield 1


def wide_experts(k, cfg, blocks):
    pe, dve, act = k.pe, k.dve, k.act
    NF, w1, w2, w3, bufs = cfg["NF"], cfg["w1"], cfg["w2"], cfg["w3"], cfg["bufs"]
    for i in blocks:
        xT = cfg["blocks"][i]
        ai, acc = bufs["acc"].next()
        dve.wait(*bufs["acc"].last_use[ai])
        accs = split(acc, TB)
        acc_mark = cfg["begin"](i, acc)
        pe.wait(cfg["xT_ready"][i])
        late = None

        def down(e, f, h, hi, m_h, obank, ob):
            nonlocal acc_mark
            pe.wait(m_h)
            for q in range(TB):
                mm = matmul(k, obank[:, q * P:(q + 1) * P], h[:, q * P:(q + 1) * P],
                             w3[:, (e * NF + f) * P:(e * NF + f + 1) * P], start=(f == 0 and q == 0),
                             stop=(f == NF - 1))
            m = pe.mark(mm)
            bufs["hid"].done(hi, m)
            if f < NF - 1:
                return
            dve.wait(m)
            if acc_mark is not None:
                dve.wait(acc_mark)
            if e < cfg["shared"]:
                r = dve.mark(dve.e.tensor_copy(acc, obank))
            else:
                dve.wait(k.gates_ready)
                for q in range(TB):
                    g = cfg["gates"][:, i * TB + q - cfg["t0"], e - cfg["shared"]:e - cfg["shared"] + 1]
                    r = dve.mark(dve.e.scalar_tensor_tensor(accs[:, q, :], obank[:, q * P:(q + 1) * P], g,
                                                            accs[:, q, :], ALU.mult, ALU.add))
            acc_mark = r
            k.banks.done(ob, r)

        for e in range(cfg["E"]):
            for f in range(NF):
                c = (e * NF + f) * P
                if f == 0:
                    ob, obank = k.banks.next()
                    pe.wait(*k.banks.last_use[ob])
                b, bank = k.banks.next()
                pe.wait(*k.banks.last_use[b])
                m_g = pe.mark(matmul(k, bank, w1[:, c:c + P], xT))
                b2, bank2 = k.banks.next()
                pe.wait(*k.banks.last_use[b2])
                m_u = pe.mark(matmul(k, bank2, w2[:, c:c + P], xT))
                si, sg = bufs["sg"].next()
                act.wait(*bufs["sg"].last_use[si])
                act.wait(m_g)
                bias = cfg["b1"][:, e * NF + f:e * NF + f + 1] if cfg["b1"] is not None else 0.0
                m = act.mark(act.e.activation(sg, bank, ACT.Silu, bias=bias))
                k.banks.done(b, m)
                hi, h = bufs["hid"].next()
                dve.wait(*bufs["hid"].last_use[hi])
                dve.wait(m, m_u)
                if cfg["b2"] is None:
                    m = dve.mark(dve.e.tensor_tensor(h, sg, bank2, ALU.mult))
                else:
                    m = dve.mark(dve.e.scalar_tensor_tensor(h, bank2, cfg["b2"][:, e * NF + f:e * NF + f + 1],
                                                            sg, ALU.add, ALU.mult))
                k.banks.done(b2, m)
                bufs["sg"].done(si, m)
                if late:
                    down(*late)
                late = (e, f, h, hi, m, obank, ob)
                yield 1
        down(*late)
        cfg["end"](i, acc, acc_mark, ai)
        yield 1


def wide_buffers(k):
    a = k.arena
    return dict(hid=Ring([a.f32(BLK) for _ in range(3)]), sg=Ring([a.f32(BLK) for _ in range(2)]),
                acc=Ring([a.f32(BLK) for _ in range(2)]))


def layer1_mixer(k):
    pe, dve, act, pool = k.pe, k.dve, k.act, k.pool
    a = k.arena
    k_tok = a.f32(NT * D).rearrange("p (t d) -> p t d", d=D)
    vb = a.f32(NT * D).rearrange("p (t d) -> p t d", d=D)
    ksq, rk, beta, tmp = a.f32(NT), a.f32(NT), a.f32(NT), a.f32(NT)
    v_marks = []
    for t in range(NT):
        b, bank = k.banks.next()
        pe.wait(*k.banks.last_use[b])
        pe.wait(k.xnT_ready[t // TB])
        m = pe.mark(matmul(k, bank[:, 0:257], k.xnT[:, t * P:(t + 1) * P], weight(k, "a1_kvb")))
        act.wait(m)
        m = act.mark(act.e.activation(vb[:, t, :], bank[:, 128:256], ACT.Silu))
        v_marks.append(m)
        dve.wait(m)
        dve.mark(dve.e.tensor_copy(k_tok[:, t, :], bank[:, 0:128]))
        m = dve.mark(dve.e.tensor_copy(beta[:, t:t + 1], bank[:, 256:257]))
        k.banks.done(b, m)
        act.wait(m)
        ji, junk = k.junk.next()
        act.wait(*k.junk.last_use[ji])
        m_k = act.mark(act.e.activation(junk, k_tok[:, t, :], ACT.Square, accum_out=ksq[:, t:t + 1]))
        k.junk.done(ji, m_k)
        yield 1
    dve.wait(m_k)
    dve.then(dve.e.tensor_scalar(ksq, ksq, 1e-24, None, ALU.max))
    rsqrt(k, rk, ksq, tmp)
    m = act.then(act.e.activation(beta, beta, ACT.Exp, scale=-1.0))
    dve.wait(m)
    dve.then(dve.e.tensor_scalar(beta, beta, 1.0, None, ALU.add))
    beta_mark = dve.then(dve.e.reciprocal(beta, beta))
    yield 1

    state = [[a.f32(D) for _ in range(2)] for _ in range(NBATCH)]
    cur, state_mark, state_used = [0, 0], [None, None], [(), ()]
    for n in range(NBATCH):
        state_mark[n] = dve.mark(dve.e.memset(state[n][0], 0.0))
    kb, qT, kbT, kT = (a.f32(BLK) for _ in range(4))
    AT, PT, T, TT, U, lv = (a.f32(BLK) for _ in range(6))
    lv2 = a.f32(BLK)
    u_slots = Ring([a.f32(D) for _ in range(2)])
    o_all = split(U, TB)
    st, mv = a.f32(6 * TB).rearrange("p (t c) -> p t c", c=6), a.f32(2 * TB).rearrange("p (t c) -> p t c", c=2)
    var, rs, tmp4 = a.f32(TB), a.f32(TB), a.f32(TB)
    quarters = [slice(q * P, (q + 1) * P) for q in range(TB)]
    group_used = ()
    for i in (0, 2, 1, 3):
        n = i // 2
        dve.wait(*v_marks[i * TB:(i + 1) * TB], *group_used)
        act.wait(*group_used)
        pool.wait(*group_used)
        for q in range(TB):
            t = i * TB + q
            m = dve.then(dve.e.tensor_scalar(k_tok[:, t, :], k_tok[:, t, :], rk[:, t:t + 1], None, ALU.mult))
            m = dve.mark(dve.e.tensor_scalar(kb[:, quarters[q]], k_tok[:, t, :], beta[:, t:t + 1], None, ALU.mult))
            m = dve.mark(dve.e.tensor_scalar(vb[:, t, :], vb[:, t, :], beta[:, t:t + 1], None, ALU.mult))
        pe.wait(m)
        for dst, src in ((kT, lambda q: k_tok[:, i * TB + q, :]), (kbT, lambda q: kb[:, quarters[q]])):
            b, bank = k.banks.next()
            pe.wait(*k.banks.last_use[b])
            for q in range(TB):
                tr = pe.e.transpose(bank[:, quarters[q]], src(q), weight(k, "ident"))
            act.wait(pe.mark(tr))
            m = act.mark(act.e.activation(dst, bank, ACT.Copy))
            k.banks.done(b, m)
        b, bank = k.banks.next()
        pe.wait(*k.banks.last_use[b])
        act.wait(pe.mark(matmul(k, bank, weight(k, "a1_q"), k.xnT[:, i * BLK:(i + 1) * BLK])))
        m = act.mark(act.e.activation(qT, bank, ACT.Copy, scale=float(D) ** -0.5))
        k.banks.done(b, m)
        pe.wait(m)
        yield 1
        b, bank = k.banks.next()
        pe.wait(*k.banks.last_use[b])
        for q in range(TB):
            mm = matmul(k, bank[:, quarters[q]], kT[:, quarters[q]], kbT[:, quarters[q]])
        act.wait(pe.mark(mm))
        m_AT = act.mark(act.e.activation(AT, bank, ACT.Copy))
        k.banks.done(b, m_AT)
        b, bank = k.banks.next()
        pe.wait(*k.banks.last_use[b])
        for q in range(TB):
            mm = matmul(k, bank[:, quarters[q]], kbT[:, quarters[q]], kT[:, quarters[q]])
        dve.wait(pe.mark(mm))
        m = dve.then(dve.e.tensor_tensor(split(T, TB), split(bank, TB), again(weight(k, "lvl1"), TB), ALU.mult))
        k.banks.done(b, m)
        b, bank = k.banks.next()
        pe.wait(*k.banks.last_use[b])
        for q in range(TB):
            mm = matmul(k, bank[:, quarters[q]], kT[:, quarters[q]], qT[:, quarters[q]])
        dve.wait(pe.mark(mm))
        m_PT = dve.mark(dve.e.tensor_tensor(split(PT, TB), split(bank, TB), again(weight(k, "triU"), TB), ALU.mult))
        k.banks.done(b, m_PT)
        idn = again(weight(k, "ident"), TB)
        dve.then(dve.e.scalar_tensor_tensor(split(T, TB), split(T, TB), -1.0, idn, ALU.mult, ALU.add))
        dve.wait(m_AT)
        dve.then(dve.e.tensor_tensor(split(TT, TB), split(AT, TB), again(weight(k, "lvlT")[:, 0:P], TB), ALU.mult))
        m_T = dve.then(dve.e.scalar_tensor_tensor(split(TT, TB), split(TT, TB), -1.0, idn, ALU.mult, ALU.add))
        yield 1
        pool.wait(m_AT)
        level_used = [None, None]
        for level in range(1, 7):
            mask = weight(k, "lvlT")[:, level * P:(level + 1) * P]
            lvb = (lv, lv2)[level % 2]
            if level_used[level % 2]:
                pool.wait(level_used[level % 2])
            m = pool.mark(pool.e.tensor_tensor(split(lvb, TB), split(AT, TB), again(mask, TB), ALU.mult))
            b, bank = k.banks.next()
            pe.wait(*k.banks.last_use[b])
            pe.wait(m, m_T)
            for q in range(TB):
                mm = matmul(k, bank[:, quarters[q]], lvb[:, quarters[q]], T[:, quarters[q]])
            m = pe.mark(mm)
            level_used[level % 2] = m
            act.wait(m)
            m = act.mark(act.e.activation(U, bank, ACT.Copy))
            k.banks.done(b, m)
            pe.wait(m)
            yield 1
            last = level == 6
            if not last:
                b, bank = k.banks.next()
                pe.wait(*k.banks.last_use[b])
                for q in range(TB):
                    mm = matmul(k, bank[:, quarters[q]], TT[:, quarters[q]], U[:, quarters[q]])
                m1 = pe.mark(mm)
            b2, bank2 = k.banks.next()
            pe.wait(*k.banks.last_use[b2])
            for q in range(TB):
                mm = matmul(k, bank2[:, quarters[q]], U[:, quarters[q]], TT[:, quarters[q]])
            m2 = pe.mark(mm)
            dve.wait(m2)
            if not last:
                m = dve.mark(dve.e.tensor_tensor(T, T, bank, ALU.subtract))
                k.banks.done(b, m)
            m_T = dve.mark(dve.e.tensor_tensor(TT, TT, bank2, ALU.subtract))
            k.banks.done(b2, m_T)
            yield 1
        pe.wait(m_T)
        b, bank = k.banks.next()
        pe.wait(*k.banks.last_use[b])
        for q in range(TB):
            mm = matmul(k, bank[:, quarters[q]], kb[:, quarters[q]], TT[:, quarters[q]])
        act.wait(pe.mark(mm))
        m_W = act.mark(act.e.activation(T, bank, ACT.Copy))
        k.banks.done(b, m_W)
        b, bank = k.banks.next()
        pe.wait(*k.banks.last_use[b])
        for q in range(TB):
            mm = matmul(k, bank[:, quarters[q]], TT[:, quarters[q]], vb[:, i * TB + q, :])
        act.wait(pe.mark(mm))
        m_V = act.mark(act.e.activation(AT, bank, ACT.Copy))
        k.banks.done(b, m_V)
        dve.wait(m_V)
        pe.wait(m_W, m_PT)
        yield 1
        for q in range(TB):
            t = i * TB + q
            S = state[n][cur[n]]
            b, bank = k.banks.next()
            pe.wait(*k.banks.last_use[b])
            pe.wait(state_mark[n])
            m = pe.mark(matmul(k, bank[:, 0:P], T[:, quarters[q]], S))
            ui, Uc = u_slots.next()
            dve.wait(*u_slots.last_use[ui])
            dve.wait(m)
            m_U = dve.mark(dve.e.tensor_tensor(Uc, AT[:, quarters[q]], bank[:, 0:P], ALU.subtract))
            k.banks.done(b, m_U)
            b, obank = k.banks.next()
            pe.wait(*k.banks.last_use[b])
            matmul(k, obank[:, 0:P], qT[:, quarters[q]], S, start=True, stop=False)
            b2, sbank = k.banks.next()
            pe.wait(*k.banks.last_use[b2])
            pe.wait(m_U)
            m_s = pe.mark(matmul(k, sbank[:, 0:P], k_tok[:, t, :], Uc))
            m_o = pe.mark(matmul(k, obank[:, 0:P], PT[:, quarters[q]], Uc, start=False, stop=True))
            u_slots.done(ui, m_o)
            nxt = 1 - cur[n]
            dve.wait(m_s, *state_used[n])
            state_mark[n] = dve.mark(dve.e.tensor_tensor(state[n][nxt], S, sbank[:, 0:P], ALU.add))
            k.banks.done(b2, state_mark[n])
            state_used[n] = (m_o,)
            cur[n] = nxt
            act.wait(m_o)
            m = act.mark(act.e.activation(o_all[:, q, :], obank[:, 0:P], ACT.Copy))
            k.banks.done(b, m)
            dve.wait(m)
            m = dve.mark(dve.e.bn_stats(st[:, q, :], o_all[:, q, :]))
            yield 1
        dve.wait(m)
        for q in range(TB):
            m = dve.mark(dve.e.bn_aggr(mv[:, q, :], st[:, q, :]))
        dve.wait(m)
        dve.then(dve.e.tensor_scalar(var, mv[:, :, 1], LN_EPS, None, ALU.add))
        rsqrt(k, rs, var, tmp4)
        for q in range(TB):
            t = i * TB + q
            m = dve.mark(dve.e.tensor_scalar(o_all[:, q, :], o_all[:, q, :], mv[:, q, 0:1], rs[:, q:q + 1],
                                             ALU.subtract, ALU.mult))
        pool.wait(m)
        sl = slice(i * TB, (i + 1) * TB)
        m = pool.mark(pool.e.tensor_tensor(o_all, o_all, again(weight(k, "a1_g"), TB), ALU.mult))
        pool.wait(m)
        m = pool.mark(pool.e.tensor_tensor(k.s[:, sl, :], o_all, again(weight(k, "a1_b"), TB), ALU.add))
        for t in range(i * TB, (i + 1) * TB):
            k.s_ready[t] = m
        group_used = (m_o, m)
        yield 1


def layer1_ffn(k):
    pe, dve, act = k.pe, k.dve, k.act
    a = k.arena
    lg = a.f32(NT * 8).rearrange("p (t e) -> p t e", e=8)
    gates = a.f32(NT * 8).rearrange("p (t e) -> p t e", e=8)
    b, bank = k.banks.next()
    pe.wait(*k.banks.last_use[b])
    pe.wait(*k.xnT_ready)
    for t in range(NT):
        mm = matmul(k, bank[:, 8 * t:8 * t + 8], k.xnT[:, t * P:(t + 1) * P], weight(k, "f1_rt"))
    dve.wait(pe.mark(mm))
    m = dve.then(dve.e.tensor_tensor(lg, bank[:, 0:8 * NT].rearrange("p (t e) -> p t e", e=8),
                                     again(weight(k, "f1_rb"), NT), ALU.add))
    k.banks.done(b, m)
    yield from route(k, 8, lg, gates, weight(k, "idx8"))
    bufs = wide_buffers(k)

    def end(i, acc, m, ai):
        act.wait(m)
        m = act.mark(act.e.activation(k.g[:, i * TB:(i + 1) * TB, :], split(acc, TB), ACT.Silu))
        bufs["acc"].done(ai, m)
        for t in range(i * TB, (i + 1) * TB):
            k.g_ready[t] = m

    blocks = [k.xnT[:, i * BLK:(i + 1) * BLK] for i in range(NBLK)]
    cfg = dict(E=9, NF=2, shared=1, blocks=blocks, xT_ready=k.xnT_ready, w1=weight(k, "f1_w1"),
               w2=weight(k, "f1_w3"), w3=weight(k, "f1_w2"), b1=None, b2=None, gates=gates, t0=0, bufs=bufs,
               begin=lambda i, acc: None, end=end)
    yield from wide_experts(k, cfg, range(NBLK))


def layer2_mixer(k):
    pe, dve, act, pool = k.pe, k.dve, k.act, k.pool
    a = k.arena
    st, mv = a.f32(6 * NT).rearrange("p (t c) -> p t c", c=6), a.f32(2 * NT).rearrange("p (t c) -> p t c", c=2)
    var, rs, tmp = a.f32(NT), a.f32(NT), a.f32(NT)
    bd = weight(k, "a2_bd")
    for t in range(NT):
        dve.wait(k.xn_ready[t // TB])
        m = dve.mark(dve.e.bn_stats(st[:, t, :], k.xn[:, t, :]))
    dve.wait(m)
    for t in range(NT):
        m = dve.mark(dve.e.bn_aggr(mv[:, t, :], st[:, t, :]))
    dve.wait(m)
    dve.then(dve.e.tensor_scalar(var, mv[:, :, 1], LN_EPS, None, ALU.add))
    rsqrt(k, rs, var, tmp)
    yield 1
    qk_pad = [a.f32(8 * P) for _ in range(2)]
    v9 = [a.f32(144).rearrange("p (h c) -> p h c", c=9) for _ in range(2)]
    for n in range(2):
        dve.mark(dve.e.memset(qk_pad[n], 0.0))
        m = dve.mark(dve.e.memset(v9[n], 1.0))
    dve.wait(m)
    pads = Ring(list(zip(qk_pad, v9)))
    xh = Ring([a.f32(P) for _ in range(2)])
    xlT = Ring([a.f32(P) for _ in range(2)])
    gate = Ring([a.f32(P) for _ in range(2)])
    qk = Ring([a.f32(256) for _ in range(2)])
    ex = Ring([a.f32(256) for _ in range(2)])
    qkT = Ring([a.f32(8 * P)])
    sc = Ring([a.f32(BLK) for _ in range(2)])
    att = Ring([a.f32(P) for _ in range(2)])
    gm = a.f32(2)
    den = a.f32(16)
    total, masked = a.f32(144), [a.f32(144) for _ in range(2)]
    masked_used = [(), ()]
    for t in range(NT):
        first = t % TPB == 0
        xi, xc = xh.next()
        dve.wait(*xh.last_use[xi])
        m = dve.mark(dve.e.tensor_scalar(xc, k.xn[:, t, :], mv[:, t, 0:1], rs[:, t:t + 1],
                                         ALU.subtract, ALU.mult))
        b, bank = k.banks.next()
        pe.wait(*k.banks.last_use[b])
        pe.wait(m)
        m = pe.mark(pe.e.transpose(bank[:, 0:P], xc, weight(k, "ident")))
        xh.done(xi, m)
        xi, xT = xlT.next()
        act.wait(*xlT.last_use[xi])
        act.wait(m)
        m = act.mark(act.e.activation(xT, bank[:, 0:P], ACT.Identity, bias=weight(k, "a2_b"), scale=weight(k, "a2_g")))
        k.banks.done(b, m)
        b, bank = k.banks.next()
        pe.wait(*k.banks.last_use[b])
        pe.wait(m, k.xnT_ready[t // TB])
        matmul(k, bank[:, 0:384], xT, weight(k, "a2_qkv"))
        m = pe.mark(matmul(k, bank[:, 384:512], k.xnT[:, t * P:(t + 1) * P], weight(k, "a2_gate")))
        xlT.done(xi, m)
        gi, gt = gate.next()
        dve.wait(*gate.last_use[gi])
        dve.wait(m)
        m = dve.mark(dve.e.tensor_tensor(gt, bank[:, 384:512], weight(k, "a2_bgate"), ALU.add))
        act.wait(m)
        m_e = act.mark(act.e.activation(gt, gt, ACT.Exp, scale=-1.0))
        qi, qkc = qk.next()
        dve.wait(*qk.last_use[qi])
        m = dve.mark(dve.e.tensor_tensor(qkc, bank[:, 0:256], weight(k, "a2_bqkv")[:, 0:256], ALU.add))
        pi, (pad, v) = pads.next()
        dve.wait(*pads.last_use[pi])
        act.wait(*pads.last_use[pi])
        m_v = dve.mark(dve.e.tensor_tensor(v[:, :, 0:8], bank[:, 256:384].rearrange("p (h c) -> p h c", c=8),
                                           weight(k, "a2_bqkv")[:, 256:384].rearrange("p (h c) -> p h c", c=8), ALU.add))
        k.banks.done(b, m_v)
        yield 1
        dve.wait(m_e)
        dve.then(dve.e.tensor_scalar(gt, gt, 1.0, None, ALU.add))
        dve.then(dve.e.reciprocal(gt, gt))
        dve.then(dve.e.tensor_reduce(gm[:, 0:1], gt, AX, ALU.add))
        dve.then(dve.e.tensor_scalar(gm[:, 0:1], gm[:, 0:1], 1.0 / D, 1e-5, ALU.mult, ALU.add))
        dve.then(dve.e.reciprocal(gm[:, 0:1], gm[:, 0:1]))
        qk2 = qkc.rearrange("p (s d) -> p s d", s=2)
        dve.then(dve.e.scalar_tensor_tensor(qk2, again(gt, 2), gm[:, 0:1], qk2, ALU.mult, ALU.mult))
        gate.done(gi, (dve.name, dve.sem, dve.count))
        ei, e = ex.next()
        dve.wait(*ex.last_use[ei])
        m = dve.mark(dve.e.tensor_scalar(e, qkc, 0.0, None, ALU.min))
        act.wait(m)
        m = act.mark(act.e.activation(e, e, ACT.Exp))
        dve.wait(m)
        m_pad = dve.mark(dve.e.scalar_tensor_tensor(
            pad.rearrange("p (h c) -> p h c", c=32)[:, :, 0:8], qkc.rearrange("p (h c) -> p h c", c=8), 0.0,
            e.rearrange("p (h c) -> p h c", c=8), ALU.max, ALU.add))
        qk.done(qi, m_pad)
        ex.done(ei, m_pad)
        ti, tT = qkT.next()
        act.wait(*qkT.last_use[ti])
        dve.wait(*qkT.last_use[ti])
        pe.wait(m_pad)
        for half, line in ((0, act), (1, dve)):
            b, bank = k.banks.next()
            pe.wait(*k.banks.last_use[b])
            for g in range(4):
                tr = pe.e.transpose(bank[:, g * P:(g + 1) * P], pad[:, (4 * half + g) * P:(4 * half + g + 1) * P],
                                    weight(k, "ident"))
            line.wait(pe.mark(tr))
            dst = tT[:, half * BLK:(half + 1) * BLK]
            m = act.mark(act.e.activation(dst, bank, ACT.Copy)) if half == 0 else \
                dve.mark(dve.e.tensor_copy(dst, bank))
            k.banks.done(b, m)
            pe.wait(m)
        yield 1
        ob, obank = k.banks.next()
        pe.wait(*k.banks.last_use[ob])
        if not first:
            pe.wait(state_mark)
            for g in range(4):
                mm = matmul(k, obank[:, 36 * g:36 * g + 36], tT[:, g * P:(g + 1) * P],
                             masked[t % 2][:, 36 * g:36 * g + 36], start=(g == 0), stop=False)
            masked_used[t % 2] = (pe.mark(mm),)
        pe.wait(m_v)
        b, bank = k.banks.next()
        pe.wait(*k.banks.last_use[b])
        for g in range(4):
            mm = matmul(k, bank[:, 36 * g:36 * g + 36], pad[:, (4 + g) * P:(5 + g) * P],
                         v[:, 4 * g:4 * g + 4, :].rearrange("p h c -> p (h c)"))
        m = pe.mark(mm)
        dve.wait(m)
        if first:
            m = dve.then(dve.e.tensor_copy(total, bank[:, 0:144]))
        else:
            m = dve.then(dve.e.tensor_tensor(total, total, bank[:, 0:144], ALU.add))
        k.banks.done(b, m)
        dve.wait(*masked_used[(t + 1) % 2])
        state_mark = dve.mark(dve.e.tensor_tensor(split(masked[(t + 1) % 2], 4), split(total, 4), again(bd, 4), ALU.mult))
        late = None

        def values(j, si, s, m):
            pe.wait(m)
            for g in range(4):
                h = 4 * g + j
                mm = matmul(k, obank[:, 9 * h:9 * h + 9], s[:, g * P:(g + 1) * P], v[:, h, :],
                             start=(first and h == 0), stop=True)
            m = pe.mark(mm)
            sc.done(si, m)
            return m

        for j in range(4):
            b, bank = k.banks.next()
            pe.wait(*k.banks.last_use[b])
            r = slice(32 * j, 32 * j + 8)
            for g in range(4):
                mm = matmul(k, bank[:, g * P:(g + 1) * P], tT[r, BLK + g * P:BLK + (g + 1) * P],
                             tT[r, g * P:(g + 1) * P])
            si, s = sc.next()
            dve.wait(*sc.last_use[si])
            dve.wait(pe.mark(mm))
            m = dve.mark(dve.e.tensor_tensor(split(s, 4), split(bank, 4), again(weight(k, "triU"), 4), ALU.mult))
            k.banks.done(b, m)
            if late:
                values(*late)
            late = (j, si, s, m)
            if j % 2:
                yield 1
        m = values(*late)
        qkT.done(ti, m)
        pads.done(pi, m)
        dve.wait(m)
        o = obank[:, 0:144].rearrange("p (h c) -> p h c", c=9)
        dve.then(dve.e.tensor_scalar(den, o[:, :, 8], 1e-5, None, ALU.add))
        dve.then(dve.e.reciprocal(den, den))
        ai, at = att.next()
        dve.wait(*att.last_use[ai])
        m = dve.mark(dve.e.tensor_tensor(at.rearrange("p (h c) -> p h c", c=8), o[:, :, 0:8], lanes(den, 16, 8), ALU.mult))
        k.banks.done(ob, m)
        b, bank = k.banks.next()
        pe.wait(*k.banks.last_use[b])
        pe.wait(m)
        m = pe.mark(pe.e.transpose(bank[:, 0:P], at, weight(k, "ident")))
        att.done(ai, m)
        xi, xT = xlT.next()
        act.wait(*xlT.last_use[xi])
        act.wait(m)
        m = act.mark(act.e.activation(xT, bank[:, 0:P], ACT.Copy))
        k.banks.done(b, m)
        yield 1
        b, bank = k.banks.next()
        pe.wait(*k.banks.last_use[b])
        pe.wait(m)
        m = pe.mark(matmul(k, bank[:, 0:P], xT, weight(k, "a2_proj")))
        xlT.done(xi, m)
        dve.wait(m)
        m = dve.mark(dve.e.tensor_tensor(k.s[:, t, :], bank[:, 0:P], weight(k, "a2_bproj"), ALU.add))
        k.banks.done(b, m)
        k.s_ready[t] = m
        yield 1


def bf16_parts(k, src, parts, rest, line):
    m = None
    for i in range(3):
        for dst in parts[i]:
            m = line.mark(line.e.tensor_copy(dst, src))
        line.wait(m)
        if i < 2:
            line.then(line.e.tensor_tensor(rest, src, parts[i][0], ALU.subtract))
            src = rest
    return m


def layer2_attention(k, n, buf):
    pe, dve, act, pool = k.pe, k.dve, k.act, k.pool
    lo = n * TPB
    x2, kT, v9, h = buf["x2"], buf["kT"], buf["v9"], buf["h"]
    kst, qst = buf["kst"], buf["qst"]
    for tt in range(TPB):
        t = lo + tt
        r1, r2 = x2[:, 0:P], x2[:, P:2 * P]
        dve.wait(*buf["x2_used"])
        dve.then(dve.e.tensor_scalar(r1, k.xn[:, t, :], buf["rs"][:, t:t + 1], None, ALU.mult))
        dve.then(dve.e.tensor_tensor(r1, r1, weight(k, "f2_n1"), ALU.mult))
        pair = r1.rearrange("p (c two) -> p two c", two=2)
        cos, sin = (weight(k, w)[:, 64 * tt:64 * tt + 64] for w in ("cos", "sin"))
        t1, t2 = x2[:, 2 * P:2 * P + 64], x2[:, 2 * P + 64:3 * P]
        dve.mark(dve.e.tensor_tensor(r2[:, 0:64], pair[:, 0, :], cos, ALU.mult))
        dve.mark(dve.e.tensor_tensor(r2[:, 64:128], pair[:, 0, :], sin, ALU.mult))
        dve.mark(dve.e.tensor_tensor(t1, pair[:, 1, :], sin, ALU.mult))
        dve.then(dve.e.tensor_tensor(t2, pair[:, 1, :], cos, ALU.mult))
        dve.mark(dve.e.tensor_tensor(r2[:, 0:64], r2[:, 0:64], t1, ALU.subtract))
        m = dve.then(dve.e.tensor_tensor(r2[:, 64:128], r2[:, 64:128], t2, ALU.add))
        b, bank = k.banks.next()
        pe.wait(*k.banks.last_use[b])
        pe.wait(m)
        m = pe.mark(pe.e.transpose(bank[:, 0:P], r2, weight(k, "ident")))
        buf["x2_used"] = (m,)
        xi, xT = buf["xT"].next()
        act.wait(*buf["xT"].last_use[xi])
        act.wait(m)
        m = act.mark(act.e.activation(xT, bank[:, 0:P], ACT.Copy))
        k.banks.done(b, m)
        b, bank = k.banks.next()
        pe.wait(*k.banks.last_use[b])
        pe.wait(m)
        m = pe.mark(matmul(k, bank[:, 0:192], xT, weight(k, "f2_qkv")))
        buf["xT"].done(xi, m)
        dve.wait(m)
        qf = buf["q"][:, tt * P:(tt + 1) * P]
        dve.mark(dve.e.tensor_copy(qf, bank[:, 0:128]))
        dve.mark(dve.e.tensor_copy(v9[:, tt, :, 0:8], bank[:, 160:192].rearrange("p (g c) -> p g c", c=8)))
        kf = x2[:, 0:32]
        m = dve.then(dve.e.tensor_copy(kf, bank[:, 128:160]))
        k.banks.done(b, m)
        k4 = kf.rearrange("p (g c) -> p g c", c=8)
        dve.wait(*buf["kst_used"])
        slot = lambda i, half: kst[:, :, half, 8 * i:8 * i + 8]
        m = bf16_parts(k, k4, [[slot(i, hf) for i in where for hf in range(2)]
                                 for where in ((0, 2, 5), (1, 4), (3,))],
                            x2[:, 32:64].rearrange("p (g c) -> p g c", c=8), dve)
        b, bank = k.banks.next()
        pe.wait(*k.banks.last_use[b])
        bank16 = bank.bitcast(BF16)
        pe.wait(m)
        for g in range(4):
            tr = pe.e.transpose(bank16[:, g * P:(g + 1) * P], kst[:, g, :, :].rearrange("p a c -> p (a c)"), buf["id16"])
        m = pe.mark(tr)
        buf["kst_used"] = (m,)
        act.wait(m)
        m = act.mark(act.e.activation(kT[:, :, tt * P:(tt + 1) * P], split(bank16[:, 0:4 * P], 4), ACT.Copy))
        k.banks.done(b, m)
        kT_mark = m
        yield 1
    pe.wait(kT_mark)
    for tt in range(TPB):
        t = lo + tt
        L = (tt + 1) * P
        dve.wait(*buf["qst_used"])
        q16 = buf["q"][:, tt * P:(tt + 1) * P].rearrange("p (h c) -> p h c", c=8)
        slot = lambda i: qst[:, :, 8 * i:8 * i + 8]
        m = bf16_parts(k, q16, [[slot(0), slot(1), slot(3)], [slot(2), slot(4)], [slot(5)]],
                            x2[:, 0:P].rearrange("p (h c) -> p h c", c=8), dve)

        def turn(m, qi, qT):
            b, bank = k.banks.next()
            pe.wait(*k.banks.last_use[b])
            bank16 = bank.bitcast(BF16)
            pe.wait(m)
            for p in range(8):
                tr = pe.e.transpose(bank16[:, p * P:(p + 1) * P],
                                    qst[:, 2 * p:2 * p + 2, :].rearrange("p a c -> p (a c)"), buf["id16"])
            m = pe.mark(tr)
            act.wait(m)
            r = act.mark(act.e.activation(qT, bank16, ACT.Copy))
            k.banks.done(b, r)
            return m, r

        qi, qT = buf["qT"].next()
        act.wait(*buf["qT"].last_use[qi])
        m_tr, m = turn(m, qi, qT)
        pe.wait(m)
        yield 1
        pm = buf["pm"]
        pieces = [(c, min(c + BLK, L)) for c in range(0, L, BLK)]
        per_bank = BLK // L if L <= BLK else 1
        for heads in [range(h0, h0 + 2 * per_bank, 2) for h00 in range(0, 16, 2 * per_bank)
                      for h0 in (h00, h00 + 1)]:
            for pc, (c0, c1) in enumerate(pieces):
                w = c1 - c0
                b, bank = k.banks.next()
                pe.wait(*k.banks.last_use[b])
                for j, hh in enumerate(heads):
                    r = slice(64 * (hh % 2), 64 * (hh % 2) + 48)
                    mm = matmul(k, bank[:, j * w:(j + 1) * w], qT[r, hh // 2 * P:hh // 2 * P + P],
                                 kT[r, hh // 4, c0:c1], start=(j == 0), stop=False)
                    if c1 == L:
                        mm = matmul(k, bank[:, (j + 1) * w - P:(j + 1) * w], buf["id16"], buf["negU"],
                                     start=False, stop=True)
                dve.wait(pe.mark(mm))
                m = dve.mark(dve.e.tensor_reduce(pm[:, heads[0]:heads[-1] + 1:2, pc],
                                                 bank[:, 0:per_bank * w].rearrange("p (h c) -> p h c", c=w), AX, ALU.max))
                k.banks.done(b, m)
            if heads[0] % 2:
                yield 1
        buf["qT"].done(qi, (pe.name, pe.sem, pe.count))
        dve.wait(m)
        mx = buf["mx"]
        if len(pieces) == 2:
            dve.then(dve.e.tensor_tensor(mx, pm[:, :, 0], pm[:, :, 1], ALU.max))
            dve.then(dve.e.tensor_scalar(mx, mx, -1.0, None, ALU.mult))
        else:
            dve.then(dve.e.tensor_scalar(mx, pm[:, :, 0], -1.0, None, ALU.mult))
        dve.wait(m_tr)
        m = bf16_parts(k, mx.unsqueeze(2), [[qst[:, :, 48 + i:49 + i]] for i in range(3)],
                            buf["mx2"].unsqueeze(2), dve)
        qi, qT = buf["qT"].next()
        act.wait(*buf["qT"].last_use[qi])
        m_tr, m = turn(m, qi, qT)
        buf["qst_used"] = (m_tr,)
        pe.wait(m)
        yield 1
        ob, obank = k.banks.next()
        pe.wait(*k.banks.last_use[ob])
        late = None

        def values(g2, j, half, pi, pr, m):
            pe.wait(m)
            for q in range(4):
                g = g2 + q // 2
                hh = 4 * g + 2 * (q % 2) + half
                mm = matmul(k, obank[:, 9 * hh:9 * hh + 9], pr[:, q * P:(q + 1) * P], v9[:, j, g, :],
                             start=(g2 == 0 and j == 0 and half == 0 and q == 0), stop=(j == tt))
            m = pe.mark(mm)
            buf["pr"].done(pi, m)
            return m

        for g2, j, half in [(g2, j, half) for g2 in (0, 2) for j in range(tt + 1) for half in range(2)]:
            if True:
                b, bank = k.banks.next()
                pe.wait(*k.banks.last_use[b])
                r = slice(64 * half, 64 * half + 51)
                for q in range(2):
                    g = g2 + q
                    mm = matmul(k, bank[:, 2 * q * P:(2 * q + 2) * P], kT[r, g, j * P:(j + 1) * P],
                                 qT[r, 2 * g * P:(2 * g + 2) * P], start=(q == 0), stop=False)
                if j == tt:
                    mm = matmul(k, bank, buf["id16"], buf["negL"], start=False, stop=True)
                pi, pr = buf["pr"].next()
                act.wait(*buf["pr"].last_use[pi])
                act.wait(pe.mark(mm))
                m = act.mark(act.e.activation(pr, bank, ACT.Exp, scale=8.0 ** -0.5))
                k.banks.done(b, m)
                if late:
                    values(*late)
                late = (g2, j, half, pi, pr, m)
                if half:
                    yield 1
        buf["qT"].done(qi, (pe.name, pe.sem, pe.count))
        m = values(*late)
        dve.wait(m)
        o = obank[:, 0:144].rearrange("p (h c) -> p h c", c=9)
        dve.then(dve.e.reciprocal(buf["den"], o[:, :, 8]))
        ai, at = buf["att"].next()
        dve.wait(*buf["att"].last_use[ai])
        m = dve.mark(dve.e.tensor_tensor(at.rearrange("p (h c) -> p h c", c=8), o[:, :, 0:8],
                                         lanes(buf["den"], 16, 8), ALU.mult))
        k.banks.done(ob, m)
        b, bank = k.banks.next()
        pe.wait(*k.banks.last_use[b])
        pe.wait(m)
        m = pe.mark(pe.e.transpose(bank[:, 0:P], at, weight(k, "ident")))
        buf["att"].done(ai, m)
        xi, xT = buf["xT"].next()
        act.wait(*buf["xT"].last_use[xi])
        act.wait(m)
        m = act.mark(act.e.activation(xT, bank[:, 0:P], ACT.Copy))
        k.banks.done(b, m)
        b, bank = k.banks.next()
        pe.wait(*k.banks.last_use[b])
        pe.wait(m)
        m = pe.mark(matmul(k, bank[:, 0:P], xT, weight(k, "f2_wo")))
        buf["xT"].done(xi, m)
        dve.wait(m)
        m = dve.then(dve.e.tensor_tensor(h[:, t, :], bank[:, 0:P], k.xn[:, t, :], ALU.add))
        k.banks.done(b, m)
        ji, junk = k.junk.next()
        act.wait(*k.junk.last_use[ji])
        act.wait(m)
        m = act.mark(act.e.activation(junk, h[:, t, :], ACT.Square, accum_out=buf["hsq"][:, t:t + 1]))
        k.junk.done(ji, m)
        yield 1
    buf["h_done"][n] = m


def layer2_moe(k, n, buf):
    pe, dve, act = k.pe, k.dve, k.act
    sl = slice(n * TPB, (n + 1) * TPB)
    h, hs, hT = buf["h"], buf["hsq"], buf["hT"]
    dve.wait(buf["h_done"][n])
    dve.then(dve.e.tensor_scalar(hs[:, sl], hs[:, sl], 1.0 / D, 1e-6, ALU.mult, ALU.add))
    rsqrt(k, buf["hrs"][:, sl], hs[:, sl], buf["htmp"][:, sl])
    ready = [None] * NBLK
    for i in range(2 * n, 2 * n + 2):
        b, bank = k.banks.next()
        pe.wait(*k.banks.last_use[b])
        for q in range(TB):
            t = i * TB + q
            xi, xh = buf["xh"].next()
            dve.wait(*buf["xh"].last_use[xi])
            m = dve.mark(dve.e.tensor_scalar(xh, h[:, t, :], buf["hrs"][:, t:t + 1], None, ALU.mult))
            pe.wait(m)
            m = pe.mark(pe.e.transpose(bank[:, q * P:(q + 1) * P], xh, weight(k, "ident")))
            buf["xh"].done(xi, m)
        act.wait(m, *buf["hT_used"])
        m = act.mark(act.e.activation(hT[:, (i % 2) * BLK:(i % 2 + 1) * BLK], bank, ACT.Copy, scale=weight(k, "f2_n2")))
        k.banks.done(b, m)
        ready[i] = m
        yield 1
    lg, gates, gT = buf["lg"], buf["gates"], buf["gT"]
    b, bank = k.banks.next()
    pe.wait(*k.banks.last_use[b])
    pe.wait(m)
    for q in range(TPB):
        mm = matmul(k, bank[:, 8 * q:8 * q + 8], hT[:, q * P:(q + 1) * P], weight(k, "f2_rt"))
    dve.wait(pe.mark(mm))
    m = dve.then(dve.e.tensor_tensor(lg, bank[:, 0:8 * TPB].rearrange("p (t e) -> p t e", e=8),
                                     again(weight(k, "f2_rb"), TPB), ALU.add))
    k.banks.done(b, m)
    yield from route(k, 8, lg, gates, weight(k, "idx8"), tiles=TPB)
    yield from gates_across(k, 8, gates, gT, tiles=TPB)
    bufs = buf["wide"]
    gT_ready = k.gT_ready

    def begin(i, acc):
        b, bank = k.banks.next()
        pe.wait(*k.banks.last_use[b])
        pe.wait(gT_ready)
        for q in range(TB):
            c = ((i % 2) * TB + q) * P
            mm = matmul(k, bank[:, q * P:(q + 1) * P], gT[0:8, c:c + P], weight(k, "f2_b3", slice(0, 8)))
        dve.wait(pe.mark(mm))
        m = dve.mark(dve.e.tensor_tensor(split(acc, TB), split(bank, TB), h[:, i * TB:(i + 1) * TB, :], ALU.add))
        k.banks.done(b, m)
        return m

    def end(i, acc, m, ai):
        act.wait(m)
        m = act.mark(act.e.activation(k.g[:, i * TB:(i + 1) * TB, :], split(acc, TB), ACT.Silu))
        bufs["acc"].done(ai, m)
        for t in range(i * TB, (i + 1) * TB):
            k.g_ready[t] = m

    two = [hT[:, (i % 2) * BLK:(i % 2 + 1) * BLK] for i in range(NBLK)]
    cfg = dict(E=8, NF=4, shared=0, blocks=two, xT_ready=ready, w1=weight(k, "f2_w1"), w2=weight(k, "f2_w2"),
               w3=weight(k, "f2_w3"), b1=weight(k, "f2_b1"), b2=weight(k, "f2_b2"), gates=gates, t0=n * TPB, bufs=bufs,
               begin=begin, end=end)
    yield from wide_experts(k, cfg, range(2 * n, 2 * n + 2))
    buf["hT_used"] = ((pe.name, pe.sem, pe.count),)


def layer2_ffn(k):
    dve, act, pool = k.dve, k.act, k.pool
    a = k.arena
    q_or_gT = a.f32(TPB * P)
    buf = dict(q=q_or_gT, gT=q_or_gT, x2=a.f32(3 * P), x2_used=(), kst_used=(), qst_used=(), hT_used=(), h_done=[None, None],
               kT=a.bf16(4 * SEQ).rearrange("p (g c) -> p g c", g=4),
               v9=a.f32(TPB * 36).rearrange("p (t g c) -> p t g c", g=4, c=9),
               kst=a.bf16(4 * P).rearrange("p (g a c) -> p g a c", g=4, a=2),
               qst=a.bf16(16 * 64).rearrange("p (h c) -> p h c", h=16),
               xT=Ring([a.f32(P) for _ in range(2)]),
               id16=a.bf16(P), negU=a.bf16(P), negL=a.bf16(4 * P),
               qT=Ring([a.bf16(8 * P) for _ in range(2)]), pr=Ring([a.f32(BLK) for _ in range(3)]),
               pm=a.f32(32).rearrange("p (h c) -> p h c", c=2), mx=a.f32(16), mx2=a.f32(16), den=a.f32(16),
               att=Ring([a.f32(P) for _ in range(2)]), h=k.h2,
               hsq=a.f32(NT), hrs=a.f32(NT), htmp=a.f32(NT), xh=Ring([a.f32(P) for _ in range(2)]),
               hT=a.f32(TPB * P), lg=a.f32(TPB * 8).rearrange("p (t e) -> p t e", e=8),
               gates=a.f32(TPB * 8).rearrange("p (t e) -> p t e", e=8),
               rs=a.f32(NT), wide=wide_buffers(k))
    dve.mark(dve.e.tensor_copy(buf["id16"], weight(k, "ident")))
    dve.mark(dve.e.tensor_copy(buf["negU"], weight(k, "negU")))
    dve.mark(dve.e.tensor_copy(split(buf["negL"], 4), again(weight(k, "negL"), 4)))
    dve.mark(dve.e.memset(buf["v9"][:, :, :, 8:9], 1.0))
    dve.then(dve.e.memset(buf["kst"], 0.0))
    dve.mark(dve.e.memset(buf["kst"][:, :, :, 48:51], 1.0))
    dve.then(dve.e.memset(buf["qst"], 0.0))
    sq, tmp = a.f32(NT), a.f32(NT)
    for t in range(NT):
        act.wait(k.xn_ready[t // TB])
        ji, junk = k.junk.next()
        act.wait(*k.junk.last_use[ji])
        m = act.mark(act.e.activation(junk, k.xn[:, t, :], ACT.Square, accum_out=sq[:, t:t + 1]))
        k.junk.done(ji, m)
    dve.wait(m)
    dve.then(dve.e.tensor_scalar(sq, sq, 1.0 / D, 1e-6, ALU.mult, ALU.add))
    rsqrt(k, buf["rs"], sq, tmp)
    yield 1
    yield from layer2_attention(k, 0, buf)
    yield from layer2_moe(k, 0, buf)
    yield from layer2_attention(k, 1, buf)
    yield from layer2_moe(k, 1, buf)


def layer3_prepare(k):
    pe, dve, act = k.pe, k.dve, k.act
    a = k.arena
    sq, rs, tmp = a.f32(NT), a.f32(NT), a.f32(NT)
    for t in range(NT):
        act.wait(k.xn_ready[t // TB])
        ji, junk = k.junk.next()
        act.wait(*k.junk.last_use[ji])
        m = act.mark(act.e.activation(junk, k.xn[:, t, :], ACT.Square, accum_out=sq[:, t:t + 1]))
        k.junk.done(ji, m)
    dve.wait(m)
    dve.then(dve.e.tensor_scalar(sq, sq, 1.0 / D, 1e-5, ALU.mult, ALU.add))
    rsqrt(k, rs, sq, tmp)
    k.m3_xT = a.f32(NT * P)
    xh = Ring([a.f32(P) for _ in range(2)])
    k.m3_ready = []
    for i in range(NBLK):
        b, bank = k.banks.next()
        pe.wait(*k.banks.last_use[b])
        for q in range(TB):
            t = i * TB + q
            xi, x = xh.next()
            dve.wait(*xh.last_use[xi])
            m = dve.mark(dve.e.tensor_scalar(x, k.xn[:, t, :], rs[:, t:t + 1], None, ALU.mult))
            pe.wait(m)
            m = pe.mark(pe.e.transpose(bank[:, q * P:(q + 1) * P], x, weight(k, "ident")))
            xh.done(xi, m)
        act.wait(m)
        m = act.mark(act.e.activation(k.m3_xT[:, i * BLK:(i + 1) * BLK], bank, ACT.Copy, scale=weight(k, "m3_nw")))
        k.banks.done(b, m)
        k.m3_ready.append(m)
    k.m3_out = [a.f32(P), a.f32(P)]
    for d in range(2):
        rows = slice(64 * d, 64 * d + 64)
        b, bank = k.banks.next()
        pe.wait(*k.banks.last_use[b])
        m = pe.mark(matmul(k, bank[:, 0:P], weight(k, "m3_outp", rows), weight(k, "m3_opw", rows)))
        dve.wait(m)
        m = dve.mark(dve.e.tensor_scalar(k.m3_out[d], bank[:, 0:P], weight(k, "m3_gn")[:, d:d + 1], None, ALU.mult))
        k.banks.done(b, m)
    pe.wait(m)
    k.m3_A = [a.f32(2), a.f32(2)]


def layer3_direction(k, d, batch, buf):
    dve = k.dve
    n = "fb"[d]
    rows = slice(64 * d, 64 * d + 64)
    cfg = dict(H=2, rows=rows, back=d == 1, xT=k.m3_xT, xT_ready=k.m3_ready,
               zdt=weight(k, "m3_zdt", rows), xbc=weight(k, "m3_xbc", rows), cw=weight(k, "m3_cw" + n),
               cb=weight(k, "m3_cb" + n), dtb=weight(k, "m3_dtb" + n), alog=weight(k, "m3_alog" + n),
               A=k.m3_A[d], Dh=weight(k, "m3_D" + n), out=k.m3_out[d])
    yield from mamba(k, cfg, batch, buf)
    for tt in range(TPB):
        t = batch * TPB + tt
        if k.m3_first[batch]:
            dve.mark(dve.e.tensor_tensor(k.s[:, t, :], k.xn[:, t, :], weight(k, "m3_opb"), ALU.add))
    dve.wait((dve.name, dve.sem, dve.count))
    for tt in range(TPB):
        t = batch * TPB + tt
        k.s_ready[t] = dve.mark(dve.e.scalar_tensor_tensor(k.s[:, t, :], buf["so"][:, tt, :],
                                                              buf["rs"][:, tt:tt + 1], k.s[:, t, :],
                                                              ALU.mult, ALU.add))
    k.m3_first[batch] = False
    buf["done"].append((dve.name, dve.sem, dve.count))
    yield 1


def layer3_ffn(k):
    pe, dve, act = k.pe, k.dve, k.act
    a = k.arena
    E, NC = 16, 9
    lg = a.f32(NT * E).rearrange("p (t e) -> p t e", e=E)
    b, bank = k.banks.next()
    pe.wait(*k.banks.last_use[b])
    pe.wait(*k.xnT_ready)
    for t in range(NT):
        mm = matmul(k, bank[:, 16 * t:16 * t + 16], k.xnT[:, t * P:(t + 1) * P], weight(k, "f3_rt"))
    dve.wait(pe.mark(mm))
    m = dve.then(dve.e.tensor_tensor(lg, bank[:, 0:E * NT].rearrange("p (t e) -> p t e", e=E),
                                     again(weight(k, "f3_rb"), NT), ALU.add))
    k.banks.done(b, m)
    gates = a.f32(NT * E).rearrange("p (t e) -> p t e", e=E)
    yield from route(k, E, lg, gates, weight(k, "idx16"))
    gT = a.f32(NT * P)
    yield from gates_across(k, E, gates, gT)
    hid, sgs = Ring([a.f32(BLK) for _ in range(3)]), Ring([a.f32(BLK) for _ in range(2)])
    pe.wait(k.gT_ready)
    for i in range(NBLK):
        cols = slice(i * BLK, (i + 1) * BLK)
        ob, obank = k.banks.next()
        pe.wait(*k.banks.last_use[ob])

        def down(c, hi, h, m_h):
            pe.wait(m_h)
            for q in range(TB):
                mm = matmul(k, obank[:, q * P:(q + 1) * P], h[:, q * P:(q + 1) * P],
                             weight(k, "f3_down")[:, c * P:(c + 1) * P], start=(c == 0 and q == 0), stop=(c == NC - 1))
            m = pe.mark(mm)
            hid.done(hi, m)
            return m

        late = None
        for c in range(NC):
            b, bank = k.banks.next()
            pe.wait(*k.banks.last_use[b])
            m_g = pe.mark(matmul(k, bank, weight(k, "f3_gate")[:, c * P:(c + 1) * P], k.xnT[:, cols]))
            b2, bank2 = k.banks.next()
            pe.wait(*k.banks.last_use[b2])
            m_u = pe.mark(matmul(k, bank2, weight(k, "f3_up")[:, c * P:(c + 1) * P], k.xnT[:, cols]))
            si, sg = sgs.next()
            act.wait(*sgs.last_use[si])
            act.wait(m_g)
            m = act.mark(act.e.activation(sg, bank, ACT.Silu))
            k.banks.done(b, m)
            hi, h = hid.next()
            dve.wait(*hid.last_use[hi])
            dve.wait(m, m_u)
            m = dve.mark(dve.e.tensor_tensor(h, sg, bank2, ALU.mult))
            sgs.done(si, m)
            k.banks.done(b2, m)
            if c < NC - 1:
                b, bank = k.banks.next()
                pe.wait(*k.banks.last_use[b])
                m_c = pe.mark(matmul(k, bank, weight(k, "f3_sel")[0:E, c * P:(c + 1) * P], gT[0:E, cols]))
                dve.wait(m, m_c)
                m = dve.mark(dve.e.tensor_tensor(h, h, bank, ALU.mult))
                k.banks.done(b, m)
            if late:
                down(*late)
            late = (c, hi, h, m)
            yield 1
        m = down(*late)
        act.wait(m)
        m = act.mark(act.e.activation(k.g[:, i * TB:(i + 1) * TB, :], split(obank, TB), ACT.Silu))
        k.banks.done(ob, m)
        for t in range(i * TB, (i + 1) * TB):
            k.g_ready[t] = m
        yield 1


def program(nc, x_dram, w_dram, out_dram, dbg=None):
    with ExitStack() as ctx:
        k = core(nc, ctx, x_dram, w_dram, out_dram)
        loads(k)
        open_arena(k, 0)
        weights_ready(k, 0)
        layernorm(k)
        k.m0_A = [k.arena.f32(4), k.arena.f32(4)]
        k.m0_out = k.arena.f32(256)
        for c in range(2):
            m = k.dve.mark(k.dve.e.tensor_scalar(k.m0_out[:, c * P:(c + 1) * P], weight(k, "m0_out")[:, c * P:(c + 1) * P],
                                                 weight(k, "m0_nw")[:, c:c + 1], None, ALU.mult))
        k.pe.wait(m)
        interleave((layer0_mixer(k, 0, mamba_buffers(k, 4)), 1), (layer0_mixer(k, 1, mamba_buffers(k, 4)), 1),
                   (layer0_ffn(k), 1))
        close_layer(k)
        open_arena(k, 1)
        late_loads(k, 4)
        weights_ready(k, 1)
        k.junk = Ring([k.arena.f32(P) for _ in range(2)])
        layernorm(k)
        interleave((layer1_mixer(k), 1), (layer1_ffn(k), 1))
        close_layer(k)
        open_arena(k, 2)
        late_loads(k, 3)
        weights_ready(k, 2)
        weights_ready(k, 4)
        k.junk = Ring([k.arena.f32(P) for _ in range(2)])
        k.h2 = k.g
        layernorm(k)
        interleave((layer2_mixer(k), 1), (layer2_ffn(k), 3))
        close_layer(k)
        open_arena(k, 3)
        weights_ready(k, 3)
        k.junk = Ring([k.arena.f32(P) for _ in range(2)])
        layernorm(k)
        layer3_prepare(k)
        k.m3_first = [True, True]
        bufs = [mamba_buffers(k, 2), mamba_buffers(k, 2)]
        interleave((in_turn(*(layer3_direction(k, 0, n, bufs[0]) for n in range(NBATCH))), 1),
                   (in_turn(*(layer3_direction(k, 1, n, bufs[1]) for n in range(NBATCH))), 1), (layer3_ffn(k), 1))
        close_layer(k, last=True)


def constants():
    import numpy as np
    f = np.float32
    c = {}
    i = np.arange(P)
    c["ident"] = np.eye(P, dtype=f)
    c["triU"] = (i[:, None] <= i[None, :]).astype(f)
    c["triL"] = (i[:, None] >= i[None, :]).astype(f)
    c["ones"] = np.ones((P, P), f)
    c["idx8"] = np.broadcast_to(np.arange(8, dtype=f) + 64, (P, 8))
    c["idx16"] = np.broadcast_to(np.arange(16, dtype=f) + 64, (P, 16))
    lv = []
    for n in range(7):
        s = 1 << n
        lv.append(((i[:, None] // (2 * s) == i[None, :] // (2 * s)) & (i[:, None] % (2 * s) < s)
                   & (i[None, :] % (2 * s) >= s)).astype(f))
    c["lvlT"] = np.concatenate(lv, axis=1)
    c["lvl1"] = np.ascontiguousarray(lv[0].T)
    c["negU"] = np.where(i[None, :] > i[:, None], f(-1e9), f(0)).astype(f)
    c["negL"] = np.ascontiguousarray(c["negU"].T)
    bd = np.zeros((P, 36), f)
    for h in range(4):
        bd[32 * h:32 * h + 8, 9 * h:9 * h + 9] = 1
    c["a2_bd"] = bd
    half = D // 2
    theta = (f(1.0) / np.power(f(10000.0), (np.arange(half, dtype=f) / f(half)))).astype(f)
    ang = (np.arange(SEQ, dtype=f)[:, None] * theta[None, :]).astype(f)
    for name, fn in (("cos", np.cos), ("sin", np.sin)):
        c[name] = fn(ang).astype(f).reshape(TPB, P, half).transpose(1, 0, 2).reshape(P, TPB * half)
    sel = np.zeros((P, 4, P), f)
    for e in range(8):
        sel[e, e // 2, 64 * (e % 2):64 * (e % 2) + 64] = 1
    c["f0_sel"] = sel.reshape(P, 4 * P)
    sel = np.zeros((P, 8, P), f)
    for e in range(16):
        sel[e, e // 2, 64 * (e % 2):64 * (e % 2) + 64] = 1
    c["f3_sel"] = sel.reshape(P, 8 * P)
    return c


def weights(inputs):
    import numpy as np
    a = {n: np.asarray(v) for n, v in inputs.items()}

    def every(v):
        return np.broadcast_to(v.reshape(1, -1), (P, v.size))

    def chunks(v):
        return v.reshape(-1, P, v.shape[-1]).transpose(1, 0, 2).reshape(P, -1)

    def low(v):
        out = np.zeros((P, v.shape[1]), v.dtype)
        out[:v.shape[0]] = v
        return out

    w = {}
    W = a["L0_attn_W_in"].T
    w["m0_zdt"] = np.concatenate([W[:, 0:256], W[:, 768:772]], axis=1)
    w["m0_xbc"] = W[:, 256:768]
    w["m0_cw"] = chunks(a["L0_attn_conv_w"])
    w["m0_cb"] = a["L0_attn_conv_b"].reshape(4, P).T
    w["m0_dtb"], w["m0_alog"], w["m0_D"] = every(a["L0_attn_dt_bias"]), every(a["L0_attn_A_log"]), every(a["L0_attn_D"])
    w["m0_nw"] = a["L0_attn_norm_weight"].reshape(2, P).T
    w["m0_out"] = chunks(a["L0_attn_W_out"].T)
    w["f0_w1"] = a["L0_ffn_w1"].transpose(1, 0, 2).reshape(P, 512)
    w["f0_b1"] = a["L0_ffn_b1"].reshape(4, P).T
    w["f0_w2"] = chunks(a["L0_ffn_w2"].reshape(512, P))
    w["f0_b2"] = low(a["L0_ffn_b2"])
    w["f0_rt"] = np.concatenate([a["L0_ffn_centroids"].T, a["L0_ffn_w_route"].T], axis=1)

    w["a1_q"] = a["L1_attn_Wq"]
    w["a1_kvb"] = np.concatenate([a["L1_attn_Wk"], a["L1_attn_Wv"], a["L1_attn_Wb"].reshape(P, 1)], axis=1)
    w["a1_g"], w["a1_b"] = every(a["L1_attn_ln_g"]), every(a["L1_attn_ln_b"])
    w["f1_rt"], w["f1_rb"] = a["L1_ffn_router_w"].T, every(a["L1_ffn_experts_bias"])
    for n, m in (("w1", "sw1"), ("w3", "sw3")):
        v = np.concatenate([a["L1_ffn_" + m], a["L1_ffn_" + n]], axis=0)
        w["f1_" + n] = v.transpose(1, 0, 2).reshape(P, 9 * 256)
    w["f1_w2"] = chunks(np.concatenate([a["L1_ffn_sw2"], a["L1_ffn_w2"]], axis=0).reshape(9 * 256, P))

    w["a2_g"], w["a2_b"] = a["L2_attn_ln_g"].reshape(P, 1), a["L2_attn_ln_b"].reshape(P, 1)
    w["a2_qkv"], w["a2_bqkv"] = a["L2_attn_w_qkv"], every(a["L2_attn_b_qkv"])
    w["a2_gate"], w["a2_bgate"] = a["L2_attn_w_gate"], every(a["L2_attn_b_gate"])
    w["a2_proj"], w["a2_bproj"] = a["L2_attn_w_proj"], every(a["L2_attn_b_proj"])
    w["f2_n1"], w["f2_n2"] = every(a["L2_ffn_norm1_w"]), a["L2_ffn_norm2_w"].reshape(P, 1)
    w["f2_qkv"] = np.concatenate([a["L2_ffn_Wq"], a["L2_ffn_Wk"], a["L2_ffn_Wv"]], axis=1)
    w["f2_wo"], w["f2_rt"], w["f2_rb"] = a["L2_ffn_Wo"], a["L2_ffn_router_w"], every(a["L2_ffn_router_b"])
    w["f2_b1"], w["f2_b2"] = a["L2_ffn_b1"].reshape(32, P).T, a["L2_ffn_b2"].reshape(32, P).T
    w["f2_b3"] = low(a["L2_ffn_b3"])
    w["f2_w1"] = a["L2_ffn_W1"].transpose(1, 0, 2).reshape(P, 4096)
    w["f2_w2"] = a["L2_ffn_W2"].transpose(1, 0, 2).reshape(P, 4096)
    w["f2_w3"] = chunks(a["L2_ffn_W3"].reshape(4096, P))

    w["m3_nw"] = a["L3_attn_norm_w"].reshape(P, 1)
    both = np.concatenate([a["L3_attn_f_in_w"].T, a["L3_attn_b_in_w"].T], axis=0)
    w["m3_zdt"] = np.concatenate([both[:, 0:128], both[:, 512:514]], axis=1)
    w["m3_xbc"] = both[:, 128:512]
    for d in "fb":
        w["m3_cw" + d] = chunks(a[f"L3_attn_{d}_conv_w"])
        w["m3_cb" + d] = a[f"L3_attn_{d}_conv_b"].reshape(3, P).T
        w["m3_dtb" + d], w["m3_alog" + d] = every(a[f"L3_attn_{d}_dt_bias"]), every(a[f"L3_attn_{d}_A_log"])
        w["m3_D" + d] = every(a[f"L3_attn_{d}_D"])
    w["m3_gn"] = np.stack([a["L3_attn_f_gnorm_w"], a["L3_attn_b_gnorm_w"]], axis=1)
    w["m3_outp"] = np.concatenate([a["L3_attn_f_outp_w"], a["L3_attn_b_outp_w"]], axis=0)
    w["m3_opw"], w["m3_opb"] = a["L3_attn_op_w"].T, every(a["L3_attn_op_b"])
    w["f3_rt"], w["f3_rb"] = a["L3_ffn_router_w"].T, every(a["L3_ffn_router_bias"])
    for n, m, s in (("gate", "gate_proj", "sh_gate"), ("up", "up_proj", "sh_up")):
        v = a["L3_ffn_" + m].transpose(1, 0, 2).reshape(P, 1024)
        w["f3_" + n] = np.concatenate([v, a["L3_ffn_" + s].T], axis=1)
    w["f3_down"] = np.concatenate([chunks(a["L3_ffn_down_proj"].reshape(1024, P)), a["L3_ffn_sh_down"].T], axis=1)
    return w


def kernel(**inputs):
    import numpy as np
    import concourse.bacc as bacc
    from concourse.bass_utils import run_bass_kernel_spmd

    pack = layout()
    parts = {**constants(), **weights(inputs)}
    for name, (_, cols) in pack.at.items():
        assert parts[name].shape == (P, cols), (name, parts[name].shape, cols)
    packed = np.concatenate([parts[name] for name in pack.at], axis=1)
    x = np.ascontiguousarray(inputs["L0_attn_u"])
    nc = bacc.Bacc("TRN2", target_bir_lowering=False, num_devices=1)
    x_dram = nc.dram_tensor("x_in", list(x.shape), F32, kind="ExternalInput").ap()
    w_dram = nc.dram_tensor("w_in", list(packed.shape), F32, kind="ExternalInput").ap()
    out_dram = nc.dram_tensor("x_out", list(x.shape), F32, kind="ExternalOutput").ap()
    program(nc, x_dram, w_dram, out_dram)
    r = run_bass_kernel_spmd(nc, [{"x_in": x, "w_in": packed}], core_ids=[0])
    return r.results[0]["x_out"]
```

```python
from contextlib import ExitStack

import concourse.bass as bass
from concourse import mybir

F32 = mybir.dt.float32
BF16 = mybir.dt.bfloat16
I32 = mybir.dt.int32
ALU = mybir.AluOpType
ACT = mybir.ActivationFunctionType
AX = mybir.AxisListType.X

P = 128
D = 128
NBATCH = 2
SEQ = 1024
TPB = SEQ // P
NT = NBATCH * TPB
BLK = 512
TB = BLK // P
NBLK = NT // TB
SBUF_COLS = 53184
LN_EPS = 1e-5


class Pack:

    def __init__(self):
        self.at, self.n, self.ends = {}, 0, {}

    def add(self, name, cols):
        self.at[name] = (self.n, cols)
        self.n += cols

    def end(self, part):
        self.ends[part] = self.n


def layout():
    k = Pack()
    for name, cols in (("ident", P), ("triU", P), ("triL", P), ("ones", P), ("idx8", 8), ("idx16", 16)):
        k.add(name, cols)
    for name, cols in (("m0_zdt", 260), ("m0_xbc", 512), ("m0_cw", 16), ("m0_cb", 4), ("m0_dtb", 4),
                       ("m0_alog", 4), ("m0_D", 4), ("m0_nw", 2), ("m0_out", 256),
                       ("f0_w1", 512), ("f0_b1", 4), ("f0_w2", 512), ("f0_b2", P), ("f0_rt", 16),
                       ("f0_sel", 512)):
        k.add(name, cols)
    k.end(0)
    for name, cols in (("a1_q", P), ("a1_kvb", 257), ("a1_g", P), ("a1_b", P), ("lvlT", 7 * P),
                       ("lvl1", P), ("f1_rt", 8), ("f1_rb", 8), ("f1_w1", 9 * 256), ("f1_w3", 9 * 256),
                       ("f1_w2", 9 * 256)):
        k.add(name, cols)
    k.end(1)
    for name, cols in (("a2_g", 1), ("a2_b", 1), ("a2_qkv", 384), ("a2_bqkv", 384), ("a2_gate", P),
                       ("a2_bgate", P), ("a2_proj", P), ("a2_bproj", P), ("a2_bd", 36),
                       ("negU", P), ("negL", P), ("cos", TPB * 64), ("sin", TPB * 64),
                       ("f2_n1", P), ("f2_qkv", 192), ("f2_wo", P), ("f2_n2", 1), ("f2_rt", 8), ("f2_rb", 8),
                       ("f2_b1", 32), ("f2_b2", 32), ("f2_b3", P)):
        k.add(name, cols)
    k.end(2)
    for name, cols in (("m3_nw", 1), ("m3_zdt", 130), ("m3_xbc", 384), ("m3_cwf", 12), ("m3_cwb", 12),
                       ("m3_cbf", 3), ("m3_cbb", 3), ("m3_dtbf", 2), ("m3_dtbb", 2), ("m3_alogf", 2),
                       ("m3_alogb", 2), ("m3_Df", 2), ("m3_Db", 2), ("m3_gn", 2), ("m3_outp", P),
                       ("m3_opw", P), ("m3_opb", P),
                       ("f3_rt", 16), ("f3_rb", 16), ("f3_gate", 9 * P), ("f3_up", 9 * P),
                       ("f3_down", 9 * P), ("f3_sel", 8 * P)):
        k.add(name, cols)
    k.end(3)
    for name in ("f2_w1", "f2_w2", "f2_w3"):
        k.add(name, 4096)
    k.end(4)
    return k


class Line:

    def __init__(self, engine, sem, name):
        self.e, self.sem, self.name, self.count, self.seen = engine, sem, name, 0, {}

    def mark(self, ins):
        self.count += 1
        ins.then_inc(self.sem, 1)
        return (self.name, self.sem, self.count)

    def wait(self, *marks):
        for name, sem, value in marks:
            if self.seen.get(name, 0) < value:
                self.e.wait_ge(sem, value)
                self.seen[name] = value

    def then(self, ins):
        m = self.mark(ins)
        self.wait(m)
        return m


class Ring:

    def __init__(self, views):
        self.views = list(views)
        self.free = list(range(len(self.views)))
        self.last_use = [()] * len(self.views)

    def next(self):
        i = self.free.pop(0)
        return i, self.views[i]

    def done(self, i, *marks):
        self.last_use[i] = marks
        self.free.append(i)


class Arena:

    def __init__(self):
        self.rooms = []

    def start(self, *rooms):
        self.rooms = [list(r) for r in rooms]

    def f32(self, cols):
        for room in self.rooms:
            tensor, a, end = room
            if a + cols <= end:
                room[1] = a + cols
                return tensor[:, a:a + cols]
        raise AssertionError(("no room for", cols, [r[2] - r[1] for r in self.rooms]))

    def bf16(self, cols):
        return self.f32(cols // 2).bitcast(BF16)


def interleave(*streams):
    live = [[gen, rate, 0.0] for gen, rate in streams]
    while live:
        for stream in list(live):
            stream[2] += stream[1]
            while stream[2] >= 1:
                stream[2] -= 1
                if next(stream[0], None) is None:
                    live.remove(stream)
                    break


def together(*gens):
    live = list(gens)
    while live:
        for g in list(live):
            if next(g, None) is None:
                live.remove(g)
            else:
                yield 1


def behind(gen, steps):
    for _ in range(steps):
        yield 1
    yield from gen


def first_steps(gen, steps):
    for _ in range(steps):
        yield next(gen)


def in_turn(*gens):
    for g in gens:
        yield from g


def lanes(ap, n, w):
    return ap.unsqueeze(2).to_broadcast([ap.shape[0], n, w])


def again(ap, n):
    return ap.unsqueeze(1).to_broadcast([ap.shape[0], n, ap.shape[1]])


def split(ap, n):
    return ap.rearrange("p (a b) -> p a b", a=n)


class Shared:
    pass


def core(nc, ctx, x_dram, w_dram, out_dram):
    k = Shared()
    k.nc = nc

    def line(engine, name):
        return Line(engine, ctx.enter_context(nc.semaphore("done_" + name)), name)

    k.pe, k.dve, k.act = line(nc.tensor, "pe"), line(nc.vector, "dve"), line(nc.scalar, "act")
    k.pool, k.sp = line(nc.gpsimd, "pool"), line(nc.sync, "sp")
    k.pack = layout()
    ends = k.pack.ends
    k.wide = ends[4] - ends[3]
    assert ends[3] - ends[2] <= ends[1] - ends[0]
    n_arena = SBUF_COLS - ends[2] - NT * P * 5
    k.w_all = ctx.enter_context(nc.sbuf_tensor("weights", [P, ends[2]], F32))
    k.x = ctx.enter_context(nc.sbuf_tensor("x", [P, NT, D], F32))
    k.xn = ctx.enter_context(nc.sbuf_tensor("xn", [P, NT, D], F32))
    k.xnT = ctx.enter_context(nc.sbuf_tensor("xnT", [P, NT * P], F32))
    k.s = ctx.enter_context(nc.sbuf_tensor("s", [P, NT, D], F32))
    k.g = ctx.enter_context(nc.sbuf_tensor("g", [P, NT, D], F32))
    k.arena_all = ctx.enter_context(nc.sbuf_tensor("arena", [P, n_arena], F32))
    k.arena = Arena()
    k.n_arena = n_arena
    k.ps = ctx.enter_context(nc.psum_tensor("banks", [P, 8, BLK], F32))
    k.banks = Ring([k.ps[:, b, :] for b in range(8)])
    k.x_in = [ctx.enter_context(nc.semaphore(f"x_in{i}")) for i in range(NBLK)]
    k.w_in = [ctx.enter_context(nc.semaphore(f"w_in{i}")) for i in range(5)]
    k.out_sem = ctx.enter_context(nc.semaphore("out_written"))
    k.x_dram, k.w_dram, k.out_dram = x_dram, w_dram, out_dram
    k.x_ready = [None] * NBLK
    k.xn_ready = [None] * NBLK
    k.xnT_ready = [None] * NBLK
    k.s_ready = [None] * NT
    k.g_ready = [None] * NT
    return k


def weight(k, name, rows=slice(0, P)):
    a, n = k.pack.at[name]
    ends = k.pack.ends
    if a >= ends[3]:
        a += k.n_arena - ends[4]
        return k.arena_all[rows, a:a + n]
    if a >= ends[2]:
        a += ends[0] - ends[2]
    return k.w_all[rows, a:a + n]


def load_part(k, part, dst):
    a, b = k.pack.ends[part - 1] if part else 0, k.pack.ends[part]
    mid = (a + b) // 2
    for lo, hi in ((a, mid), (mid, b)):
        k.sp.e.dma_start(dst[:, lo - a:hi - a], k.w_dram[:, lo:hi]).then_inc(k.w_in[part], 16)


def late_loads(k, part):
    k.sp.wait(*[(o.name, o.sem, o.count) for o in (k.pe, k.dve, k.act, k.pool) if o.count])
    n = k.n_arena
    ends = k.pack.ends
    dst = k.w_all[:, ends[0]:ends[0] + ends[3] - ends[2]] if part == 3 else k.arena_all[:, n - k.wide:n]
    load_part(k, part, dst)


def loads(k):
    src = k.x_dram.rearrange("b (t p) d -> p (b t) d", p=P)
    for i in range(NBLK):
        t = slice(i * TB, (i + 1) * TB)
        k.act.e.dma_start(k.x[:, t, :], src[:, t, :]).then_inc(k.x_in[i], 16)
        k.x_ready[i] = (f"x_in{i}", k.x_in[i], 16)
    ends = [0] + [k.pack.ends[i] for i in range(3)]
    for part in range(3):
        load_part(k, part, k.w_all[:, ends[part]:ends[part + 1]])


def weights_ready(k, layer):
    mark = (f"w_in{layer}", k.w_in[layer], 32)
    for line in (k.pe, k.dve, k.act, k.pool):
        line.wait(mark)


def barrier(k):
    lines = (k.pe, k.dve, k.act, k.pool)
    marks = [(o.name, o.sem, o.count) for o in lines if o.count]
    for line in lines:
        line.wait(*marks)


def open_arena(k, layer):
    barrier(k)
    ends = k.pack.ends
    whole = (k.arena_all, 0, k.n_arena)
    below_experts = (k.arena_all, 0, k.n_arena - k.wide)
    part0 = (k.w_all, k.pack.at["m0_zdt"][0], ends[0])
    part1 = (k.w_all, ends[0] + ends[3] - ends[2], ends[1])
    parts12 = (k.w_all, ends[0] + ends[3] - ends[2], ends[2])
    k.arena.start(*{0: (whole,), 1: (part0, below_experts), 2: (part0, part1, below_experts),
                    3: (part0, parts12, whole)}[layer])


def matmul(k, out, lhsT, rhs, start=True, stop=True):
    return k.pe.e.matmul(out, lhsT, rhs, start=start, stop=stop, skip_group_check=True)


def rsqrt(k, y, v, t):
    dve = k.dve
    dve.then(dve.e.tensor_scalar(y.bitcast(I32), v.bitcast(I32), -0.5, 1597463007.0, ALU.mult, ALU.add))
    for _ in range(3):
        dve.then(dve.e.scalar_tensor_tensor(t, v, -0.5, y, ALU.mult, ALU.mult))
        dve.then(dve.e.tensor_tensor(t, t, y, ALU.mult))
        m = dve.then(dve.e.scalar_tensor_tensor(y, t, 1.5, y, ALU.add, ALU.mult))
    return m


def halve(k, *views):
    for v in views:
        m = k.dve.mark(k.dve.e.tensor_scalar(v, v, 0.5, None, ALU.mult))
    k.pe.wait(m)
    k.dve.wait(m)


def close_block(k, i):
    g = slice(i * TB, (i + 1) * TB)
    line = k.pool if i >= 2 else k.dve
    for t in range(i * TB, (i + 1) * TB):
        line.wait(k.s_ready[t], k.g_ready[t])
    line.then(line.e.tensor_tensor(k.s[:, g, :], k.s[:, g, :], k.g[:, g, :], ALU.mult))
    k.x_ready[i] = line.then(line.e.tensor_tensor(k.x[:, g, :], k.x[:, g, :], k.s[:, g, :], ALU.add))


def layernorm(k, closes=True):
    pe, dve, act = k.pe, k.dve, k.act
    st = k.arena.f32(NT * 6).rearrange("p (t c) -> p t c", c=6)
    mv = k.arena.f32(NT * 2).rearrange("p (t c) -> p t c", c=2)
    var, rs, tmp = k.arena.f32(NT), k.arena.f32(NT), k.arena.f32(NT)
    if closes:
        for i in range(NBLK):
            close_block(k, i)
    for i in range(NBLK):
        dve.wait(k.x_ready[i])
        for t in range(i * TB, (i + 1) * TB):
            m = dve.mark(dve.e.bn_stats(st[:, t, :], k.x[:, t, :]))
    dve.wait(m)
    for t in range(NT):
        m = dve.mark(dve.e.bn_aggr(mv[:, t, :], st[:, t, :]))
    dve.wait(m)
    dve.then(dve.e.tensor_scalar(var, mv[:, :, 1], LN_EPS, None, ALU.add))
    rsqrt(k, rs, var, tmp)
    for i in range(NBLK):
        for t in range(i * TB, (i + 1) * TB):
            m = dve.mark(dve.e.tensor_scalar(k.xn[:, t, :], k.x[:, t, :], mv[:, t, 0:1], rs[:, t:t + 1],
                                             ALU.subtract, ALU.mult))
        k.xn_ready[i] = m
        b, bank = k.banks.next()
        pe.wait(*k.banks.last_use[b])
        pe.wait(m)
        for q in range(TB):
            tr = pe.e.transpose(bank[:, q * P:(q + 1) * P], k.xn[:, i * TB + q, :], weight(k, "ident"))
        act.wait(pe.mark(tr))
        m = act.mark(act.e.activation(k.xnT[:, i * BLK:(i + 1) * BLK], bank, ACT.Copy))
        k.banks.done(b, m)
        k.xnT_ready[i] = m


def results(k):
    dst = k.out_dram.rearrange("b (t p) d -> p (b t) d", p=P)
    for i in range(NBLK):
        g = slice(i * TB, (i + 1) * TB)
        close_block(k, i)
        k.sp.wait(k.x_ready[i])
        k.sp.e.dma_start(dst[:, g, :], k.x[:, g, :]).then_inc(k.out_sem, 16)
    k.sp.e.wait_ge(k.out_sem, 16 * NBLK)


def route_room(k, E, tiles=NT):
    a = k.arena
    return ([a.f32(tiles * E).rearrange("p (t e) -> p t e", e=E) for _ in range(4)],
            [a.f32(tiles) for _ in range(5)])


def route(k, E, lg, gates, idx, room, masked_softmax=False, tiles=NT):
    dve, act = k.dve, k.act
    (eq, oh1, oh2, l2), (m1, m2, mi, ex, sm) = room
    full = lambda v: lanes(v, tiles, E)
    idxs = again(idx, tiles)

    def first(l, m, oh):
        dve.then(dve.e.tensor_reduce(m, l, AX, ALU.max))
        dve.then(dve.e.tensor_tensor(eq, l, full(m), ALU.is_equal))
        dve.then(dve.e.scalar_tensor_tensor(eq, eq, -64.0, idxs, ALU.mult, ALU.add))
        dve.then(dve.e.tensor_reduce(mi, eq, AX, ALU.min))
        return dve.then(dve.e.tensor_tensor(oh, eq, full(mi), ALU.is_equal))

    first(lg, m1, oh1)
    yield 1
    dve.then(dve.e.scalar_tensor_tensor(l2, oh1, -3e38, lg, ALU.mult, ALU.add))
    first(l2, m2, oh2)
    yield 1
    if masked_softmax:
        dve.then(dve.e.tensor_tensor(oh1, lg, full(m2), ALU.is_ge))
        m = dve.then(dve.e.tensor_tensor(l2, lg, full(m1), ALU.subtract))
        act.wait(m)
        m = act.mark(act.e.activation(l2, l2, ACT.Exp))
        dve.wait(m)
        dve.then(dve.e.tensor_tensor(l2, l2, oh1, ALU.mult))
        dve.then(dve.e.tensor_reduce(sm, l2, AX, ALU.add))
        dve.then(dve.e.reciprocal(sm, sm))
        k.gates_ready = dve.then(dve.e.tensor_tensor(gates, l2, full(sm), ALU.mult))
    else:
        m = dve.then(dve.e.tensor_tensor(ex, m2, m1, ALU.subtract))
        act.wait(m)
        m = act.mark(act.e.activation(ex, ex, ACT.Exp))
        dve.wait(m)
        dve.then(dve.e.tensor_scalar(sm, ex, 1.0, None, ALU.add))
        dve.then(dve.e.reciprocal(sm, sm))
        dve.then(dve.e.tensor_tensor(ex, ex, sm, ALU.mult))
        dve.then(dve.e.tensor_tensor(oh1, oh1, full(sm), ALU.mult))
        dve.then(dve.e.tensor_tensor(oh2, oh2, full(ex), ALU.mult))
        k.gates_ready = dve.then(dve.e.tensor_tensor(gates, oh1, oh2, ALU.add))
    yield 1


def gates_across(k, E, gates, gT, t0=0, tiles=NT):
    pe, act = k.pe, k.act
    for i in range(tiles // TB):
        b, bank = k.banks.next()
        pe.wait(*k.banks.last_use[b])
        pe.wait(k.gates_ready)
        for q in range(TB):
            tr = pe.e.transpose(bank[0:E, q * P:(q + 1) * P], gates[:, i * TB + q, :], weight(k, "ident"))
        act.wait(pe.mark(tr))
        k.gT_ready = act.mark(act.e.activation(gT[0:E, t0 * P + i * BLK:t0 * P + (i + 1) * BLK], bank[0:E, :], ACT.Copy))
        k.banks.done(b, k.gT_ready)
        yield 1


def mamba(k, cfg, batch, buf):
    pe, dve, act, pool = k.pe, k.dve, k.act, k.pool
    H, rows, back = cfg["H"], cfg["rows"], cfg["back"]
    DI = 64 * H
    NX = DI // P
    NCH = NX + 2
    one_bank = 3 * DI <= BLK
    src, src_ready = cfg["xT"], cfg["xT_ready"]
    tri = weight(k, "triL") if back else weight(k, "triU")
    ones = weight(k, "ones")
    tiles = [batch * TPB + t for t in (range(TPB - 1, -1, -1) if back else range(TPB))]
    lo = batch * TPB
    hs = lambda a: a.rearrange("p (t h) -> p t h", h=H)

    for line in (dve, act, pool):
        line.wait(*buf.get("done", ()))
    dt, u, s, z, acc = (buf["small"][name] for name in ("dt", "u", "s", "z", "acc"))
    dA, cA, ecA, seg, etot = (buf["small"][name] for name in ("dA", "cA", "ecA", "seg", "etot"))
    b, bank = k.banks.next()
    pe.wait(*k.banks.last_use[b])
    pe.wait(*[src_ready[t // TB] for t in tiles])
    for t in sorted(tiles):
        mm = matmul(k, bank[:, (t - lo) * H:(t - lo + 1) * H], src[rows, t * P:(t + 1) * P],
                     cfg["zdt"][:, DI:DI + H])
    dve.wait(pe.mark(mm))
    m = dve.then(dve.e.tensor_tensor(hs(dt), hs(bank[:, 0:TPB * H]), again(cfg["dtb"], TPB), ALU.add))
    k.banks.done(b, m)
    dve.then(dve.e.tensor_scalar(u, dt, -1.0, None, ALU.mult))
    m = dve.then(dve.e.tensor_tensor(u, u, dt, ALU.min))
    act.wait(m)
    m = act.mark(act.e.activation(u, u, ACT.Exp))
    dve.wait(m)
    yield 1
    dve.then(dve.e.tensor_scalar(s, u, 2.0, None, ALU.add))
    dve.then(dve.e.reciprocal(s, s))
    dve.then(dve.e.tensor_tensor(s, s, u, ALU.mult))
    dve.then(dve.e.tensor_tensor(z, s, s, ALU.mult))
    dve.then(dve.e.tensor_scalar(acc, z, 1.0 / 17, 1.0 / 15, ALU.mult, ALU.add))
    for odd in (13, 11, 9, 7, 5, 3, 1):
        dve.then(dve.e.tensor_tensor(acc, acc, z, ALU.mult))
        dve.then(dve.e.tensor_scalar(acc, acc, 1.0 / odd, None, ALU.add))
    dve.then(dve.e.scalar_tensor_tensor(acc, acc, 2.0, s, ALU.mult, ALU.mult))
    dve.then(dve.e.scalar_tensor_tensor(dt, dt, 0.0, acc, ALU.max, ALU.add))
    yield 1
    m = act.mark(act.e.activation(cfg["A"], cfg["alog"], ACT.Exp))
    dve.wait(m)
    m = dve.then(dve.e.scalar_tensor_tensor(hs(dA), hs(dt), -1.0, again(cfg["A"], TPB), ALU.mult, ALU.mult))
    b, bank = k.banks.next()
    pe.wait(*k.banks.last_use[b])
    pe.wait(m)
    n = TPB * H
    matmul(k, bank[:, 0:n], tri, dA)
    mm = matmul(k, bank[:, n:2 * n], ones, dA)
    dve.wait(pe.mark(mm))
    dve.then(dve.e.tensor_copy(cA, bank[:, 0:n]))
    m = dve.then(dve.e.tensor_copy(etot, bank[:, n:2 * n]))
    k.banks.done(b, m)
    dve.then(dve.e.tensor_tensor(seg, etot, cA, ALU.subtract))
    m = dve.then(dve.e.tensor_scalar(seg, seg, 0.0, None, ALU.min))
    act.wait(m)
    act.mark(act.e.activation(ecA, cA, ACT.Exp))
    act.mark(act.e.activation(seg, seg, ACT.Exp))
    m = act.mark(act.e.activation(etot, etot, ACT.Exp))
    dve.wait(m)
    pool.wait(m)
    state = buf["state"]
    state_mark = dve.then(dve.e.memset(state[0], 0.0))
    cur = 0
    pre, cv = buf["pre"], buf["cv"]
    tap = (lambda j: 3 - j) if back else (lambda j: j)
    halo = slice(512, 515) if back else slice(0, 3)
    edge = slice(0, 3) if back else slice(512, 515)
    data = slice(0, 512) if back else slice(3, 515)
    m = None
    for ch in range(NCH):
        m = dve.mark(dve.e.memset(pre[ch][:, halo], 0.0))
    halo_mark = m
    state_used = ()
    yield 1

    for nb in range(TPB // TB):
        block = tiles[nb * TB:(nb + 1) * TB]
        c0 = min(block) * P
        chunk = {}

        def front(t):
            q = (t * P - c0) // P
            tt = t - lo
            cols = slice(q * P, (q + 1) * P)
            hcol = lambda a: a[:, tt * H:(tt + 1) * H]
            b2, dbank = k.banks.next()
            pe.wait(*k.banks.last_use[b2])
            for h in range(H):
                col = dA[:, tt * H + h:tt * H + h + 1]
                mm = matmul(k, dbank[:, h * P:(h + 1) * P], col.to_broadcast([P, P]), tri)
            dve.wait(pe.mark(mm))
            di, dec = buf["dec"].next()
            dve.wait(*buf["dec"].last_use[di])
            for h in range(H):
                m_dec = dve.mark(dve.e.tensor_scalar(dec[:, h * P:(h + 1) * P], dbank[:, h * P:(h + 1) * P],
                                                     cA[:, tt * H + h:tt * H + h + 1], 0.0,
                                                     ALU.subtract, ALU.min))
            k.banks.done(b2, m_dec)
            b, bank = k.banks.next()
            pe.wait(*k.banks.last_use[b])
            m = pe.mark(matmul(k, bank[:, 0:DI], src[rows, t * P:(t + 1) * P], cfg["zdt"][:, 0:DI]))
            act.wait(m)
            zi, sz = buf["sz"].next()
            act.wait(*buf["sz"].last_use[zi])
            m_z = act.mark(act.e.activation(sz, bank[:, 0:DI], ACT.Tanh))
            act.wait(m_dec)
            m_dec = act.mark(act.e.activation(dec, dec, ACT.Exp))
            dve.wait(m_z)
            m_z = dve.mark(dve.e.scalar_tensor_tensor(sz, sz, 1.0, bank[:, 0:DI], ALU.add, ALU.mult))
            k.banks.done(b, m_z)
            yield 1
            b, bank = k.banks.next()
            pe.wait(*k.banks.last_use[b])
            pe.wait(conv_mark)
            for ch in range(NX + 1):
                tr = pe.e.transpose(bank[:, ch * P:(ch + 1) * P], cv[ch][:, cols], weight(k, "ident"))
            m_tr = pe.mark(tr)
            b2, cbank = k.banks.next()
            pe.wait(*k.banks.last_use[b2])
            m_cb = pe.mark(matmul(k, cbank[:, 0:P], cv[NX][:, cols], cv[NX + 1][:, cols]))
            xi, xb = buf["xb"].next()
            act.wait(*buf["xb"].last_use[xi])
            act.wait(m_tr)
            m_xb = act.mark(act.e.activation(xb, bank[:, 0:DI + P], ACT.Copy))
            k.banks.done(b, m_xb)
            ci, cb = buf["cb"].next()
            dve.wait(*buf["cb"].last_use[ci])
            dve.wait(m_cb)
            m = dve.mark(dve.e.tensor_tensor(cb, cbank[:, 0:P], tri, ALU.mult))
            k.banks.done(b2, m)
            yield 1
            pool.wait(m_xb)
            xdi, xd = buf["xd"].next()
            pool.wait(*buf["xd"].last_use[xdi])
            xh = xb[:, 0:DI].rearrange("p (h c) -> p h c", h=H)
            m_xd = pool.then(pool.e.tensor_tensor(split(xd[:, 0:DI], H), xh, lanes(hcol(dt), H, 64), ALU.mult))
            m_xs = pool.mark(pool.e.tensor_tensor(split(xd[:, DI:2 * DI], H), split(xd[:, 0:DI], H),
                                                lanes(hcol(seg), H, 64), ALU.mult))
            dve.wait(m_dec, m)
            m_M = dve.mark(dve.e.tensor_tensor(split(dec, H), split(dec, H), again(cb, H), ALU.mult))
            buf["cb"].done(ci, m_M)
            chunk[t] = dict(hcol=hcol, cols=cols, tt=tt, xi=xi, xb=xb, m_xb=m_xb, zi=zi, sz=sz, m_z=m_z, di=di,
                            dec=dec, m_M=m_M, xdi=xdi, xd=xd, m_xs=m_xs, xh=xh)
            yield 1

        def back(t):
            nonlocal state_mark, state_used, cur
            hcol, cols, tt, xi, xb, m_xb, zi, sz, m_z, di, dec, m_M, xdi, xd, m_xs, xh = chunk.pop(t).values()
            b, ybank = k.banks.next()
            pe.wait(*k.banks.last_use[b])
            if one_bank:
                s_view = ybank[:, 2 * DI:3 * DI]
            else:
                b2, sbank = k.banks.next()
                pe.wait(*k.banks.last_use[b2])
                s_view = sbank[:, 0:DI]
            pe.wait(state_mark, m_xs)
            matmul(k, ybank[:, DI:2 * DI], cv[NX + 1][:, cols], state[cur])
            mm = matmul(k, s_view, xb[:, DI:DI + P], xd[:, DI:2 * DI])
            m_st = pe.mark(mm)
            pe.wait(m_M)
            for h in range(H):
                mm = matmul(k, ybank[:, h * 64:(h + 1) * 64], dec[:, h * P:(h + 1) * P],
                             xd[:, h * 64:(h + 1) * 64])
            m_y = pe.mark(mm)
            if one_bank:
                m_st = m_y
            buf["xd"].done(xdi, m_y)
            buf["dec"].done(di, m_y)
            yield 1
            dve.wait(m_st, *state_used)
            nxt = 1 - cur
            dve.then(dve.e.tensor_tensor(split(state[nxt], H), split(state[cur], H),
                                         lanes(hcol(etot), H, 64), ALU.mult))
            state_mark = dve.mark(dve.e.tensor_tensor(state[nxt], state[nxt], s_view, ALU.add))
            if not one_bank:
                k.banks.done(b2, state_mark)
            state_used = (m_y,)
            cur = nxt
            yi, y = buf["y"].next()
            dve.wait(*buf["y"].last_use[yi])
            pool.wait(*buf["y"].last_use[yi])
            y1, y2 = y[:, 0:DI], y[:, DI:2 * DI]
            pool.wait(m_xb)
            m_D = pool.mark(pool.e.tensor_tensor(split(y1, H), xh, lanes(cfg["Dh"], H, 64), ALU.mult))
            buf["xb"].done(xi, m_y, m_D, m_xs)
            dve.wait(m_y)
            dve.then(dve.e.tensor_tensor(split(y2, H), split(ybank[:, DI:2 * DI], H),
                                         lanes(hcol(ecA), H, 64), ALU.mult))
            m = dve.mark(dve.e.tensor_tensor(y2, y2, ybank[:, 0:DI], ALU.add))
            k.banks.done(b, m)
            yield 1
            pool.wait(m, m_D)
            pool.then(pool.e.tensor_tensor(y2, y2, y1, ALU.add))
            pool.wait(m_z)
            m_yz = pool.mark(pool.e.tensor_tensor(y2, y2, sz, ALU.mult))
            buf["sz"].done(zi, m_yz)
            act.wait(m_yz)
            m_sq = act.mark(act.e.activation(y1, y2, ACT.Square, accum_out=buf["ss"][:, tt:tt + 1]))
            yield 1
            b, bank = k.banks.next()
            pe.wait(*k.banks.last_use[b])
            pe.wait(m_yz)
            for c in range(NX):
                tr = pe.e.transpose(bank[:, c * P:(c + 1) * P], y2[:, c * P:(c + 1) * P], weight(k, "ident"))
            m = pe.mark(tr)
            buf["y"].done(yi, m, m_sq)
            ti, yT = buf["yT"].next()
            act.wait(*buf["yT"].last_use[ti])
            act.wait(m)
            m = act.mark(act.e.activation(yT, bank[:, 0:DI], ACT.Copy))
            k.banks.done(b, m)
            yield 1
            b, bank = k.banks.next()
            pe.wait(*k.banks.last_use[b])
            pe.wait(m)
            for c in range(NX):
                mm = matmul(k, bank[:, 0:P], yT[:, c * P:(c + 1) * P], cfg["out"][:, c * P:(c + 1) * P],
                             start=(c == 0), stop=(c == NX - 1))
            m = pe.mark(mm)
            buf["yT"].done(ti, m)
            act.wait(m)
            m = act.mark(act.e.activation(buf["so"][:, tt, :], bank[:, 0:P], ACT.Copy))
            k.banks.done(b, m)
            buf["so_mark"] = m
            buf["cv_used"] = (m_y, m)
            yield 1

        fronts = [front(t) for t in block]
        next(fronts[0])
        yield 1
        late = []
        for ch in range(NCH):
            b, bank = k.banks.next()
            pe.wait(*k.banks.last_use[b])
            mm = matmul(k, bank, cfg["xbc"][:, ch * P:(ch + 1) * P], src[rows, c0:c0 + BLK])
            act.wait(pe.mark(mm), halo_mark)
            m = act.mark(act.e.activation(pre[ch][:, data], bank, ACT.Copy))
            k.banks.done(b, m)
            act.wait(m, *buf.get("cv_used", ()))
            o = cv[ch]
            m = act.mark(act.e.activation(o, pre[ch][:, tap(0):tap(0) + BLK], ACT.Identity,
                                          bias=cfg["cb"][:, ch:ch + 1], scale=cfg["cw"][:, 4 * ch:4 * ch + 1]))
            dve.wait(m)
            for j in (1, 2, 3):
                m = dve.then(dve.e.scalar_tensor_tensor(
                    o, pre[ch][:, tap(j):tap(j) + BLK], cfg["cw"][:, 4 * ch + j:4 * ch + j + 1], o,
                    ALU.mult, ALU.add))
            halo_mark = dve.then(dve.e.tensor_copy(pre[ch][:, halo], pre[ch][:, edge]))
            act.wait(halo_mark)
            m = act.mark(act.e.activation(pre[ch][:, data], o, ACT.Tanh))
            late.append((ch, m))
            yield 1
            if len(late) > 1 or ch == NCH - 1:
                for c, m in late if ch == NCH - 1 else [late.pop(0)]:
                    dve.wait(m)
                    halo_mark = dve.mark(dve.e.scalar_tensor_tensor(cv[c], pre[c][:, data], 1.0, cv[c],
                                                                    ALU.add, ALU.mult))
        conv_mark = halo_mark
        yield from fronts[0]
        for i, t in enumerate(block):
            yield from together(back(t), *fronts[i + 1:i + 2])
    dve.wait(buf["so_mark"])
    dve.then(dve.e.tensor_scalar(buf["ss"], buf["ss"], 1.0 / DI, 1e-5, ALU.mult, ALU.add))
    rsqrt(k, buf["rs"], buf["ss"], buf["tmp"])
    buf["done"] = [(o.name, o.sem, o.count) for o in (pe, dve, act, pool)]
    yield 1


def mamba_buffers(k, H, so=None):
    a = k.arena
    DI = 64 * H
    NCH = DI // P + 2
    n = TPB * H
    one = 2 if H == 2 else 1
    return dict(
        small={name: a.f32(n) for name in ("dt", "u", "s", "z", "acc", "dA", "cA", "ecA", "seg", "etot")},
        state=[a.f32(DI), a.f32(DI)],
        pre=[a.f32(516) for _ in range(NCH)], cv=[a.f32(BLK) for _ in range(NCH)],
        xb=Ring([a.f32(DI + P) for _ in range(2)]), sz=Ring([a.f32(DI) for _ in range(2)]),
        cb=Ring([a.f32(P) for _ in range(2)]), dec=Ring([a.f32(H * P) for _ in range(2)]),
        xd=Ring([a.f32(2 * DI) for _ in range(2)]), y=Ring([a.f32(2 * DI) for _ in range(3 - one)]),
        yT=Ring([a.f32(DI) for _ in range(3 - one)]), ss=a.f32(TPB), rs=a.f32(TPB), tmp=a.f32(TPB),
        so=a.f32(TPB * D).rearrange("p (t d) -> p t d", d=D) if so is None else so)


def layer0_mixer(k, batch, buf):
    dve = k.dve
    cfg = dict(H=4, rows=slice(0, P), back=False, xT=k.xnT, xT_ready=k.xnT_ready,
               zdt=weight(k, "m0_zdt"), xbc=weight(k, "m0_xbc"), cw=weight(k, "m0_cw"), cb=weight(k, "m0_cb"),
               dtb=weight(k, "m0_dtb"), alog=weight(k, "m0_alog"), A=k.m0_A[batch], Dh=weight(k, "m0_D"),
               out=k.m0_out)
    yield from mamba(k, cfg, batch, buf)
    for tt in range(TPB):
        t = batch * TPB + tt
        k.s_ready[t] = dve.mark(dve.e.tensor_scalar(k.s[:, t, :], buf["so"][:, tt, :],
                                                       buf["rs"][:, tt:tt + 1], None, ALU.mult))
    yield 1


def layer0_ffn(k):
    pe, dve, act = k.pe, k.dve, k.act
    a = k.arena
    E, NC = 8, 4
    csq, cinv, tmp8 = a.f32(8), a.f32(8), a.f32(8)
    m = dve.mark(dve.e.tensor_tensor(csq, weight(k, "f0_rt")[:, 0:8], weight(k, "f0_rt")[:, 0:8], ALU.mult))
    b, bank = k.banks.next()
    pe.wait(*k.banks.last_use[b])
    pe.wait(m)
    dve.wait(pe.mark(matmul(k, bank[:, 0:8], weight(k, "ones"), csq)))
    m = dve.then(dve.e.tensor_scalar(csq, bank[:, 0:8], 1e-24, None, ALU.max))
    k.banks.done(b, m)
    rsqrt(k, cinv, csq, tmp8)
    yield 1
    xsq, xinv, tmp = a.f32(NT), a.f32(NT), a.f32(NT)
    junk = a.f32(P)
    for t in range(NT):
        act.wait(k.xn_ready[t // TB])
        m = act.then(act.e.activation(junk, k.xn[:, t, :], ACT.Square, accum_out=xsq[:, t:t + 1]))
    dve.wait(m)
    dve.then(dve.e.tensor_scalar(xsq, xsq, 1e-24, None, ALU.max))
    rsqrt(k, xinv, xsq, tmp)
    yield 1
    lg = a.f32(NT * E).rearrange("p (t e) -> p t e", e=E)
    b, bank = k.banks.next()
    pe.wait(*k.banks.last_use[b])
    pe.wait(*k.xnT_ready)
    for t in range(NT):
        mm = matmul(k, bank[:, 16 * t:16 * t + 16], k.xnT[:, t * P:(t + 1) * P], weight(k, "f0_rt"))
    dve.wait(pe.mark(mm))
    dots = bank[:, 0:16 * NT].rearrange("p (t e) -> p t e", e=16)
    dve.then(dve.e.tensor_tensor(lg, dots[:, :, 0:8], again(cinv, NT), ALU.mult))
    dve.then(dve.e.tensor_tensor(lg, lg, lanes(xinv, NT, E), ALU.mult))
    m = dve.then(dve.e.tensor_tensor(lg, lg, dots[:, :, 8:16], ALU.add))
    k.banks.done(b, m)
    yield 1
    gates = a.f32(NT * E).rearrange("p (t e) -> p t e", e=E)
    yield from route(k, E, lg, gates, weight(k, "idx8"), route_room(k, E), masked_softmax=True)
    across = Ring([a.f32(BLK) for _ in range(2)])
    hid = Ring([a.f32(BLK) for _ in range(4)])
    for i in range(NBLK):
        gi, gT = across.next()
        act.wait(*across.last_use[gi])
        yield from gates_across(k, E, gates[:, i * TB:(i + 1) * TB, :], gT, tiles=TB)
        pe.wait(k.gT_ready)
        cols = slice(i * BLK, (i + 1) * BLK)
        ob, obank = k.banks.next()
        pe.wait(*k.banks.last_use[ob])

        def down(c, hi, h, m_h):
            pe.wait(m_h)
            for q in range(TB):
                mm = matmul(k, obank[:, q * P:(q + 1) * P], h[:, q * P:(q + 1) * P],
                             weight(k, "f0_w2")[:, c * P:(c + 1) * P], start=(c == 0 and q == 0), stop=False)
            hid.done(hi, pe.mark(mm))

        late = []
        for c0 in range(0, NC, 2):
            pair = []
            for c in (c0, c0 + 1):
                b, bank = k.banks.next()
                pe.wait(*k.banks.last_use[b])
                m_g = pe.mark(matmul(k, bank, weight(k, "f0_w1")[:, c * P:(c + 1) * P], k.xnT[:, cols]))
                hi, h = hid.next()
                act.wait(*hid.last_use[hi])
                act.wait(m_g)
                m = act.mark(act.e.activation(h, bank, ACT.Gelu, bias=weight(k, "f0_b1")[:, c:c + 1]))
                k.banks.done(b, m)
                pair.append((c, hi, h, m))
            for c, hi, h, m in pair:
                b, cbank = k.banks.next()
                pe.wait(*k.banks.last_use[b])
                m_c = pe.mark(matmul(k, cbank, weight(k, "f0_sel")[0:E, c * P:(c + 1) * P], gT[0:E, :]))
                dve.wait(m, m_c)
                m = dve.mark(dve.e.tensor_tensor(h, h, cbank, ALU.mult))
                k.banks.done(b, m)
                late.append((c, hi, h, m))
            yield 1
            while len(late) > 2 or (late and c0 == NC - 2):
                down(*late.pop(0))
        for q in range(TB):
            mm = matmul(k, obank[:, q * P:(q + 1) * P], gT[0:E, q * P:(q + 1) * P],
                         weight(k, "f0_b2", slice(0, E)), start=False, stop=True)
        m = pe.mark(mm)
        across.done(gi, m)
        act.wait(m)
        m = act.mark(act.e.activation(k.g[:, i * TB:(i + 1) * TB, :], split(obank, TB), ACT.Silu))
        k.banks.done(ob, m)
        for t in range(i * TB, (i + 1) * TB):
            k.g_ready[t] = m
        yield 1


def wide_experts(k, cfg, blocks):
    pe, dve, act = k.pe, k.dve, k.act
    NF, w1, w2, w3, bufs = cfg["NF"], cfg["w1"], cfg["w2"], cfg["w3"], cfg["bufs"]
    LAG = 2
    for i in blocks:
        xT = cfg["blocks"][i]
        acc = k.g[:, i * TB:(i + 1) * TB, :]
        acc_mark = cfg["begin"](i, acc)
        pe.wait(cfg["xT_ready"][i])
        late = []

        def down(e, f, h, hi, m_h, obank, ob):
            nonlocal acc_mark
            pe.wait(m_h)
            for q in range(TB):
                mm = matmul(k, obank[:, q * P:(q + 1) * P], h[:, q * P:(q + 1) * P],
                             w3[:, (e * NF + f) * P:(e * NF + f + 1) * P], start=(f == 0 and q == 0),
                             stop=(f == NF - 1))
            m = pe.mark(mm)
            bufs["hid"].done(hi, m)
            if f < NF - 1:
                return
            dve.wait(m)
            if acc_mark is not None:
                dve.wait(acc_mark)
            if e < cfg["shared"]:
                r = dve.mark(dve.e.tensor_copy(acc, split(obank, TB)))
            else:
                dve.wait(k.gates_ready)
                for q in range(TB):
                    g = cfg["gates"][:, i * TB + q - cfg["t0"], e - cfg["shared"]:e - cfg["shared"] + 1]
                    r = dve.mark(dve.e.scalar_tensor_tensor(acc[:, q, :], obank[:, q * P:(q + 1) * P], g,
                                                            acc[:, q, :], ALU.mult, ALU.add))
            acc_mark = r
            k.banks.done(ob, r)

        for e in range(cfg["E"]):
            for f in range(NF):
                c = (e * NF + f) * P
                if f == 0:
                    ob, obank = k.banks.next()
                    pe.wait(*k.banks.last_use[ob])
                b, bank = k.banks.next()
                pe.wait(*k.banks.last_use[b])
                m_g = pe.mark(matmul(k, bank, w1[:, c:c + P], xT))
                b2, bank2 = k.banks.next()
                pe.wait(*k.banks.last_use[b2])
                m_u = pe.mark(matmul(k, bank2, w2[:, c:c + P], xT))
                si, sg = bufs["sg"].next()
                act.wait(*bufs["sg"].last_use[si])
                act.wait(m_g)
                hi, h = bufs["hid"].next()
                dve.wait(*bufs["hid"].last_use[hi])
                if cfg["b1"] is None:
                    m = act.mark(act.e.activation(sg, bank, ACT.Silu))
                    k.banks.done(b, m)
                    dve.wait(m, m_u)
                    m = dve.mark(dve.e.tensor_tensor(h, sg, bank2, ALU.mult))
                else:
                    half_b1 = cfg["b1"][:, e * NF + f:e * NF + f + 1]
                    act.mark(act.e.activation(sg, bank, ACT.Tanh, bias=half_b1, scale=0.5))
                    act.wait(*bufs["hid"].last_use[hi])
                    m = act.mark(act.e.activation(h, bank, ACT.Identity, bias=half_b1, scale=0.5))
                    k.banks.done(b, m)
                    dve.wait(m)
                    dve.then(dve.e.scalar_tensor_tensor(h, sg, 1.0, h, ALU.add, ALU.mult))
                    dve.wait(m_u)
                    m = dve.mark(dve.e.scalar_tensor_tensor(h, bank2, cfg["b2"][:, e * NF + f:e * NF + f + 1],
                                                            h, ALU.add, ALU.mult))
                k.banks.done(b2, m)
                bufs["sg"].done(si, m)
                late.append((e, f, h, hi, m, obank, ob))
                if len(late) > LAG:
                    down(*late.pop(0))
                yield 1
        for chunk in late:
            down(*chunk)
        cfg["end"](i, acc, acc_mark)
        yield 1


def wide_buffers(k):
    a = k.arena
    return dict(hid=Ring([a.f32(BLK) for _ in range(4)]), sg=Ring([a.f32(BLK) for _ in range(2)]))


def layer1_keys(k):
    pe, dve, act, pool = k.pe, k.dve, k.act, k.pool
    a = k.arena
    k_tok = a.f32(NT * D).rearrange("p (t d) -> p t d", d=D)
    vb = k.s
    ksq, rk, beta, tmp = a.f32(NT), a.f32(NT), a.f32(NT), a.f32(NT)
    v_marks = []
    for t in range(NT):
        b, bank = k.banks.next()
        pe.wait(*k.banks.last_use[b])
        pe.wait(k.xnT_ready[t // TB])
        m = pe.mark(matmul(k, bank[:, 0:257], k.xnT[:, t * P:(t + 1) * P], weight(k, "a1_kvb")))
        act.wait(m)
        m = act.mark(act.e.activation(vb[:, t, :], bank[:, 128:256], ACT.Silu))
        v_marks.append(m)
        dve.wait(m)
        dve.mark(dve.e.tensor_copy(k_tok[:, t, :], bank[:, 0:128]))
        m = dve.mark(dve.e.tensor_copy(beta[:, t:t + 1], bank[:, 256:257]))
        k.banks.done(b, m)
        act.wait(m)
        ji, junk = k.junk.next()
        act.wait(*k.junk.last_use[ji])
        m_k = act.mark(act.e.activation(junk, k_tok[:, t, :], ACT.Square, accum_out=ksq[:, t:t + 1]))
        k.junk.done(ji, m_k)
        yield 1
    dve.wait(m_k)
    dve.then(dve.e.tensor_scalar(ksq, ksq, 1e-24, None, ALU.max))
    rsqrt(k, rk, ksq, tmp)
    m = act.then(act.e.activation(beta, beta, ACT.Exp, scale=-1.0))
    dve.wait(m)
    dve.then(dve.e.tensor_scalar(beta, beta, 1.0, None, ALU.add))
    beta_mark = dve.then(dve.e.reciprocal(beta, beta))
    k.a1 = (k_tok, vb, rk, beta, v_marks)
    yield 1


def layer1_mixer(k, n):
    pe, dve, act, pool = k.pe, k.dve, k.act, k.pool
    a = k.arena
    k_tok, vb, rk, beta, v_marks = k.a1
    state = [a.f32(D) for _ in range(2)]
    cur, state_used = 0, ()
    state_mark = dve.mark(dve.e.memset(state[0], 0.0))
    kb, qT, kbT, kT = (a.f32(BLK) for _ in range(4))
    AT, PT, T, TT, U = (a.f32(BLK) for _ in range(5))
    lv, lv2 = kbT, kT
    u_slots = Ring([a.f32(D) for _ in range(2)])
    o_all = split(U, TB)
    st, mv = a.f32(6 * TB).rearrange("p (t c) -> p t c", c=6), a.f32(2 * TB).rearrange("p (t c) -> p t c", c=2)
    var, rs, tmp4 = a.f32(TB), a.f32(TB), a.f32(TB)
    quarters = [slice(q * P, (q + 1) * P) for q in range(TB)]
    group_used = ()
    for i in (2 * n, 2 * n + 1):
        dve.wait(*v_marks[i * TB:(i + 1) * TB], *group_used)
        act.wait(*group_used)
        pool.wait(*group_used)
        for q in range(TB):
            t = i * TB + q
            m = dve.then(dve.e.tensor_scalar(k_tok[:, t, :], k_tok[:, t, :], rk[:, t:t + 1], None, ALU.mult))
            m = dve.mark(dve.e.tensor_scalar(kb[:, quarters[q]], k_tok[:, t, :], beta[:, t:t + 1], None, ALU.mult))
            m = dve.mark(dve.e.tensor_scalar(vb[:, t, :], vb[:, t, :], beta[:, t:t + 1], None, ALU.mult))
        pe.wait(m)
        for dst, src in ((kT, lambda q: k_tok[:, i * TB + q, :]), (kbT, lambda q: kb[:, quarters[q]])):
            b, bank = k.banks.next()
            pe.wait(*k.banks.last_use[b])
            for q in range(TB):
                tr = pe.e.transpose(bank[:, quarters[q]], src(q), weight(k, "ident"))
            act.wait(pe.mark(tr))
            m = act.mark(act.e.activation(dst, bank, ACT.Copy))
            k.banks.done(b, m)
        b, bank = k.banks.next()
        pe.wait(*k.banks.last_use[b])
        act.wait(pe.mark(matmul(k, bank, weight(k, "a1_q"), k.xnT[:, i * BLK:(i + 1) * BLK])))
        m = act.mark(act.e.activation(qT, bank, ACT.Copy, scale=float(D) ** -0.5))
        k.banks.done(b, m)
        pe.wait(m)
        yield 1
        b, bank = k.banks.next()
        pe.wait(*k.banks.last_use[b])
        for q in range(TB):
            mm = matmul(k, bank[:, quarters[q]], kT[:, quarters[q]], kbT[:, quarters[q]])
        act.wait(pe.mark(mm))
        m_AT = act.mark(act.e.activation(AT, bank, ACT.Copy))
        k.banks.done(b, m_AT)
        b, bank = k.banks.next()
        pe.wait(*k.banks.last_use[b])
        for q in range(TB):
            mm = matmul(k, bank[:, quarters[q]], kbT[:, quarters[q]], kT[:, quarters[q]])
        dve.wait(pe.mark(mm))
        m = dve.then(dve.e.tensor_tensor(split(T, TB), split(bank, TB), again(weight(k, "lvl1"), TB), ALU.mult))
        k.banks.done(b, m)
        b, bank = k.banks.next()
        pe.wait(*k.banks.last_use[b])
        for q in range(TB):
            mm = matmul(k, bank[:, quarters[q]], kT[:, quarters[q]], qT[:, quarters[q]])
        dve.wait(pe.mark(mm))
        m_PT = dve.mark(dve.e.tensor_tensor(split(PT, TB), split(bank, TB), again(weight(k, "triU"), TB), ALU.mult))
        k.banks.done(b, m_PT)
        idn = again(weight(k, "ident"), TB)
        dve.then(dve.e.scalar_tensor_tensor(split(T, TB), split(T, TB), -1.0, idn, ALU.mult, ALU.add))
        dve.wait(m_AT)
        dve.then(dve.e.tensor_tensor(split(TT, TB), split(AT, TB), again(weight(k, "lvlT")[:, 0:P], TB), ALU.mult))
        m_T = dve.then(dve.e.scalar_tensor_tensor(split(TT, TB), split(TT, TB), -1.0, idn, ALU.mult, ALU.add))
        yield 1
        pool.wait(m_AT, m_T, m_PT)
        level_used = [None, None]
        for level in range(1, 7):
            mask = weight(k, "lvlT")[:, level * P:(level + 1) * P]
            lvb = (lv, lv2)[level % 2]
            if level_used[level % 2]:
                pool.wait(level_used[level % 2])
            m = pool.mark(pool.e.tensor_tensor(split(lvb, TB), split(AT, TB), again(mask, TB), ALU.mult))
            b, bank = k.banks.next()
            pe.wait(*k.banks.last_use[b])
            pe.wait(m, m_T)
            for q in range(TB):
                mm = matmul(k, bank[:, quarters[q]], lvb[:, quarters[q]], T[:, quarters[q]])
            m = pe.mark(mm)
            level_used[level % 2] = m
            act.wait(m)
            m = act.mark(act.e.activation(U, bank, ACT.Copy))
            k.banks.done(b, m)
            pe.wait(m)
            yield 1
            last = level == 6
            if not last:
                b, bank = k.banks.next()
                pe.wait(*k.banks.last_use[b])
                for q in range(TB):
                    mm = matmul(k, bank[:, quarters[q]], TT[:, quarters[q]], U[:, quarters[q]])
                m1 = pe.mark(mm)
            b2, bank2 = k.banks.next()
            pe.wait(*k.banks.last_use[b2])
            for q in range(TB):
                mm = matmul(k, bank2[:, quarters[q]], U[:, quarters[q]], TT[:, quarters[q]])
            m2 = pe.mark(mm)
            dve.wait(m2)
            if not last:
                m = dve.mark(dve.e.tensor_tensor(T, T, bank, ALU.subtract))
                k.banks.done(b, m)
            m_T = dve.mark(dve.e.tensor_tensor(TT, TT, bank2, ALU.subtract))
            k.banks.done(b2, m_T)
            yield 1
        pe.wait(m_T)
        b, bank = k.banks.next()
        pe.wait(*k.banks.last_use[b])
        for q in range(TB):
            mm = matmul(k, bank[:, quarters[q]], kb[:, quarters[q]], TT[:, quarters[q]])
        act.wait(pe.mark(mm))
        m_W = act.mark(act.e.activation(T, bank, ACT.Copy))
        k.banks.done(b, m_W)
        b, bank = k.banks.next()
        pe.wait(*k.banks.last_use[b])
        for q in range(TB):
            mm = matmul(k, bank[:, quarters[q]], TT[:, quarters[q]], vb[:, i * TB + q, :])
        act.wait(pe.mark(mm))
        m_V = act.mark(act.e.activation(AT, bank, ACT.Copy))
        k.banks.done(b, m_V)
        dve.wait(m_V)
        pe.wait(m_W, m_PT)
        yield 1
        for q in range(TB):
            t = i * TB + q
            S = state[cur]
            b, bank = k.banks.next()
            pe.wait(*k.banks.last_use[b])
            pe.wait(state_mark)
            m = pe.mark(matmul(k, bank[:, 0:P], T[:, quarters[q]], S))
            ui, Uc = u_slots.next()
            dve.wait(*u_slots.last_use[ui])
            dve.wait(m)
            m_U = dve.mark(dve.e.tensor_tensor(Uc, AT[:, quarters[q]], bank[:, 0:P], ALU.subtract))
            k.banks.done(b, m_U)
            b, obank = k.banks.next()
            pe.wait(*k.banks.last_use[b])
            matmul(k, obank[:, 0:P], qT[:, quarters[q]], S, start=True, stop=False)
            b2, sbank = k.banks.next()
            pe.wait(*k.banks.last_use[b2])
            pe.wait(m_U)
            m_s = pe.mark(matmul(k, sbank[:, 0:P], k_tok[:, t, :], Uc))
            m_o = pe.mark(matmul(k, obank[:, 0:P], PT[:, quarters[q]], Uc, start=False, stop=True))
            u_slots.done(ui, m_o)
            nxt = 1 - cur
            dve.wait(m_s, *state_used)
            state_mark = dve.mark(dve.e.tensor_tensor(state[nxt], S, sbank[:, 0:P], ALU.add))
            k.banks.done(b2, state_mark)
            state_used = (m_o,)
            cur = nxt
            act.wait(m_o)
            m = act.mark(act.e.activation(o_all[:, q, :], obank[:, 0:P], ACT.Copy))
            k.banks.done(b, m)
            dve.wait(m)
            m = dve.mark(dve.e.bn_stats(st[:, q, :], o_all[:, q, :]))
            yield 1
        dve.wait(m)
        for q in range(TB):
            m = dve.mark(dve.e.bn_aggr(mv[:, q, :], st[:, q, :]))
        dve.wait(m)
        dve.then(dve.e.tensor_scalar(var, mv[:, :, 1], LN_EPS, None, ALU.add))
        rsqrt(k, rs, var, tmp4)
        for q in range(TB):
            t = i * TB + q
            m = dve.mark(dve.e.tensor_scalar(o_all[:, q, :], o_all[:, q, :], mv[:, q, 0:1], rs[:, q:q + 1],
                                             ALU.subtract, ALU.mult))
        pool.wait(m)
        sl = slice(i * TB, (i + 1) * TB)
        m = pool.mark(pool.e.tensor_tensor(o_all, o_all, again(weight(k, "a1_g"), TB), ALU.mult))
        pool.wait(m)
        m = pool.mark(pool.e.tensor_tensor(k.s[:, sl, :], o_all, again(weight(k, "a1_b"), TB), ALU.add))
        for t in range(i * TB, (i + 1) * TB):
            k.s_ready[t] = m
        group_used = (m_o, m)
        yield 1


def layer1_ffn(k):
    pe, dve, act = k.pe, k.dve, k.act
    a = k.arena
    lg = a.f32(NT * 8).rearrange("p (t e) -> p t e", e=8)
    gates = a.f32(NT * 8).rearrange("p (t e) -> p t e", e=8)
    b, bank = k.banks.next()
    pe.wait(*k.banks.last_use[b])
    pe.wait(*k.xnT_ready)
    for t in range(NT):
        mm = matmul(k, bank[:, 8 * t:8 * t + 8], k.xnT[:, t * P:(t + 1) * P], weight(k, "f1_rt"))
    dve.wait(pe.mark(mm))
    m = dve.then(dve.e.tensor_tensor(lg, bank[:, 0:8 * NT].rearrange("p (t e) -> p t e", e=8),
                                     again(weight(k, "f1_rb"), NT), ALU.add))
    k.banks.done(b, m)
    yield from route(k, 8, lg, gates, weight(k, "idx8"), route_room(k, 8))
    bufs = wide_buffers(k)

    def end(i, acc, m):
        act.wait(m)
        m = act.mark(act.e.activation(acc, acc, ACT.Silu))
        for t in range(i * TB, (i + 1) * TB):
            k.g_ready[t] = m

    blocks = [k.xnT[:, i * BLK:(i + 1) * BLK] for i in range(NBLK)]
    cfg = dict(E=9, NF=2, shared=1, blocks=blocks, xT_ready=k.xnT_ready, w1=weight(k, "f1_w1"),
               w2=weight(k, "f1_w3"), w3=weight(k, "f1_w2"), b1=None, b2=None, gates=gates, t0=0, bufs=bufs,
               begin=lambda i, acc: None, end=end)
    yield from wide_experts(k, cfg, range(NBLK))


def layer2_mixer(k):
    pe, dve, act, pool = k.pe, k.dve, k.act, k.pool
    a = k.arena
    st, mv = a.f32(6 * NT).rearrange("p (t c) -> p t c", c=6), a.f32(2 * NT).rearrange("p (t c) -> p t c", c=2)
    var, rs, tmp = a.f32(NT), a.f32(NT), a.f32(NT)
    bd = weight(k, "a2_bd")
    for t in range(NT):
        dve.wait(k.xn_ready[t // TB])
        m = dve.mark(dve.e.bn_stats(st[:, t, :], k.xn[:, t, :]))
    dve.wait(m)
    for t in range(NT):
        m = dve.mark(dve.e.bn_aggr(mv[:, t, :], st[:, t, :]))
    dve.wait(m)
    dve.then(dve.e.tensor_scalar(var, mv[:, :, 1], LN_EPS, None, ALU.add))
    rsqrt(k, rs, var, tmp)
    yield 1
    qk_pad = [a.f32(8 * P) for _ in range(2)]
    v9 = [a.f32(144 + 24) for _ in range(2)]
    for n in range(2):
        dve.mark(dve.e.memset(qk_pad[n], 0.0))
        m = dve.mark(dve.e.memset(v9[n], 1.0))
    dve.wait(m)
    pads = Ring(list(zip(qk_pad, v9)))
    xh = Ring([a.f32(P)])
    xlT = Ring([a.f32(P) for _ in range(2)])
    gate = Ring([a.f32(P)])
    qk = Ring([a.f32(256) for _ in range(2)])
    ex = Ring([a.f32(256)])
    qkT = Ring([a.f32(8 * P)])
    sc = Ring([a.f32(BLK) for _ in range(2)])
    att = Ring([a.f32(P) for _ in range(2)])
    gm = a.f32(2)
    den = a.f32(16)
    total, masked = a.f32(144), [a.f32(144 + 24) for _ in range(2)]
    for state in masked:
        m = dve.mark(dve.e.memset(state, 0.0))
    dve.wait(m)
    masked_used = [(), ()]
    for t in range(NT):
        first = t % TPB == 0
        xi, xc = xh.next()
        dve.wait(*xh.last_use[xi])
        m = dve.mark(dve.e.tensor_scalar(xc, k.xn[:, t, :], mv[:, t, 0:1], rs[:, t:t + 1],
                                         ALU.subtract, ALU.mult))
        yield 1
        b, bank = k.banks.next()
        pe.wait(*k.banks.last_use[b])
        pe.wait(m)
        m = pe.mark(pe.e.transpose(bank[:, 0:P], xc, weight(k, "ident")))
        xh.done(xi, m)
        xi, xT = xlT.next()
        act.wait(*xlT.last_use[xi])
        act.wait(m)
        m = act.mark(act.e.activation(xT, bank[:, 0:P], ACT.Identity, bias=weight(k, "a2_b"), scale=weight(k, "a2_g")))
        k.banks.done(b, m)
        yield 1
        b, bank = k.banks.next()
        pe.wait(*k.banks.last_use[b])
        pe.wait(m, k.xnT_ready[t // TB])
        matmul(k, bank[:, 0:384], xT, weight(k, "a2_qkv"))
        m = pe.mark(matmul(k, bank[:, 384:512], k.xnT[:, t * P:(t + 1) * P], weight(k, "a2_gate")))
        k.xnT_used = (t, m)
        xlT.done(xi, m)
        gi, gt = gate.next()
        dve.wait(*gate.last_use[gi])
        dve.wait(m)
        m = dve.mark(dve.e.tensor_tensor(gt, bank[:, 384:512], weight(k, "a2_bgate"), ALU.add))
        act.wait(m)
        m_e = act.mark(act.e.activation(gt, gt, ACT.Exp, scale=-1.0))
        qi, qkc = qk.next()
        dve.wait(*qk.last_use[qi])
        m = dve.mark(dve.e.tensor_tensor(qkc, bank[:, 0:256], weight(k, "a2_bqkv")[:, 0:256], ALU.add))
        pi, (pad, v) = pads.next()
        dve.wait(*pads.last_use[pi])
        act.wait(*pads.last_use[pi])
        m_v = dve.mark(dve.e.tensor_tensor(v[:, 0:144].rearrange("p (h c) -> p h c", c=9)[:, :, 0:8], bank[:, 256:384].rearrange("p (h c) -> p h c", c=8),
                                           weight(k, "a2_bqkv")[:, 256:384].rearrange("p (h c) -> p h c", c=8), ALU.add))
        k.banks.done(b, m_v)
        yield 1
        dve.wait(m_e)
        dve.then(dve.e.tensor_scalar(gt, gt, 1.0, None, ALU.add))
        dve.then(dve.e.reciprocal(gt, gt))
        dve.then(dve.e.tensor_reduce(gm[:, 0:1], gt, AX, ALU.add))
        dve.then(dve.e.tensor_scalar(gm[:, 0:1], gm[:, 0:1], 1.0 / D, 1e-5, ALU.mult, ALU.add))
        dve.then(dve.e.reciprocal(gm[:, 0:1], gm[:, 0:1]))
        qk2 = qkc.rearrange("p (s d) -> p s d", s=2)
        dve.then(dve.e.scalar_tensor_tensor(qk2, again(gt, 2), gm[:, 0:1], qk2, ALU.mult, ALU.mult))
        gate.done(gi, (dve.name, dve.sem, dve.count))
        ei, e = ex.next()
        dve.wait(*ex.last_use[ei])
        m = dve.mark(dve.e.tensor_scalar(e, qkc, 0.0, None, ALU.min))
        act.wait(m)
        m = act.mark(act.e.activation(e, e, ACT.Exp))
        dve.wait(m)
        m_pad = dve.mark(dve.e.scalar_tensor_tensor(
            pad.rearrange("p (h c) -> p h c", c=32)[:, :, 0:8], qkc.rearrange("p (h c) -> p h c", c=8), 0.0,
            e.rearrange("p (h c) -> p h c", c=8), ALU.max, ALU.add))
        qk.done(qi, m_pad)
        ex.done(ei, m_pad)
        yield 1
        ti, tT = qkT.next()
        act.wait(*qkT.last_use[ti])
        dve.wait(*qkT.last_use[ti])
        pe.wait(m_pad)
        for half, line in ((0, act), (1, dve)):
            b, bank = k.banks.next()
            pe.wait(*k.banks.last_use[b])
            for g in range(4):
                tr = pe.e.transpose(bank[:, g * P:(g + 1) * P], pad[:, (4 * half + g) * P:(4 * half + g + 1) * P],
                                    weight(k, "ident"))
            line.wait(pe.mark(tr))
            dst = tT[:, half * BLK:(half + 1) * BLK]
            m = act.mark(act.e.activation(dst, bank, ACT.Copy)) if half == 0 else \
                dve.mark(dve.e.tensor_copy(dst, bank))
            k.banks.done(b, m)
            pe.wait(m)
        yield 1
        ob, obank = k.banks.next()
        pe.wait(*k.banks.last_use[ob])
        if not first:
            pe.wait(state_mark)
            for j in range(4):
                for g in range(4):
                    c = 36 * g + 9 * j
                    mm = matmul(k, obank[32 * g:32 * g + 32, j * P:(j + 1) * P], masked[t % 2][:, c:c + 32],
                                tT[:, g * P:(g + 1) * P], start=(j == 0), stop=False)
            masked_used[t % 2] = (pe.mark(mm),)
        pe.wait(m_v)
        b, bank = k.banks.next()
        pe.wait(*k.banks.last_use[b])
        for g in range(4):
            mm = matmul(k, bank[:, 36 * g:36 * g + 36], pad[:, (4 + g) * P:(5 + g) * P],
                         v[:, 36 * g:36 * g + 36])
        m = pe.mark(mm)
        dve.wait(m)
        if first:
            m = dve.then(dve.e.tensor_copy(total, bank[:, 0:144]))
        else:
            m = dve.then(dve.e.tensor_tensor(total, total, bank[:, 0:144], ALU.add))
        k.banks.done(b, m)
        dve.wait(*masked_used[(t + 1) % 2])
        state_mark = dve.mark(dve.e.tensor_tensor(split(masked[(t + 1) % 2][:, 0:144], 4), split(total, 4), again(bd, 4), ALU.mult))
        four = [k.banks.next() for _ in range(4)]
        for b, _ in four:
            pe.wait(*k.banks.last_use[b])
        for g in range(4):
            for j, (b, bank) in enumerate(four):
                r = slice(32 * j, 32 * j + 8)
                mm = matmul(k, bank[:, g * P:(g + 1) * P], tT[r, BLK + g * P:BLK + (g + 1) * P],
                            tT[r, g * P:(g + 1) * P])
        m = pe.mark(mm)
        dve.wait(m)
        parts = []
        for b, bank in four[:2]:
            si, s = sc.next()
            dve.wait(*sc.last_use[si])
            m = dve.mark(dve.e.tensor_tensor(split(s, 4), split(bank, 4), again(weight(k, "triU"), 4), ALU.mult))
            k.banks.done(b, m)
            parts.append((si, s, m))
        yield 1
        for j in range(4):
            si, s, m = parts.pop(0)
            pe.wait(m)
            for g in range(4):
                c = 9 * (4 * g + j)
                mm = matmul(k, obank[32 * g:32 * g + 32, j * P:(j + 1) * P], v[:, c:c + 32],
                            s[:, g * P:(g + 1) * P], start=(first and j == 0), stop=True)
            m = pe.mark(mm)
            sc.done(si, m)
            if j < 2:
                b, bank = four[j + 2]
                si, s = sc.next()
                dve.wait(*sc.last_use[si])
                m = dve.mark(dve.e.tensor_tensor(split(s, 4), split(bank, 4), again(weight(k, "triU"), 4), ALU.mult))
                k.banks.done(b, m)
                parts.append((si, s, m))
            if j % 2:
                yield 1
        qkT.done(ti, m)
        pads.done(pi, m)
        act.wait(m)
        si, osb = sc.next()
        act.wait(*sc.last_use[si])
        m = act.mark(act.e.activation(osb, obank, ACT.Copy))
        k.banks.done(ob, m)
        yield 1
        ai, at = att.next()
        dve.wait(*att.last_use[ai])
        pe.wait(m)
        m_tr, m = sums_to_tokens(k, osb, at, den, eps=1e-5)
        sc.done(si, m_tr)
        yield 1
        b, bank = k.banks.next()
        pe.wait(*k.banks.last_use[b])
        pe.wait(m)
        m = pe.mark(pe.e.transpose(bank[:, 0:P], at, weight(k, "ident")))
        att.done(ai, m)
        xi, xT = xlT.next()
        act.wait(*xlT.last_use[xi])
        act.wait(m)
        m = act.mark(act.e.activation(xT, bank[:, 0:P], ACT.Copy))
        k.banks.done(b, m)
        yield 1
        b, bank = k.banks.next()
        pe.wait(*k.banks.last_use[b])
        pe.wait(m)
        m = pe.mark(matmul(k, bank[:, 0:P], xT, weight(k, "a2_proj")))
        xlT.done(xi, m)
        dve.wait(m)
        m = dve.mark(dve.e.tensor_tensor(k.s[:, t, :], bank[:, 0:P], weight(k, "a2_bproj"), ALU.add))
        k.banks.done(b, m)
        k.s_ready[t] = m
        yield 1


def sums_to_tokens(k, osb, at, den, eps=None):
    pe, dve = k.pe, k.dve
    b, bank = k.banks.next()
    pe.wait(*k.banks.last_use[b])
    for r in range(4):
        tr = pe.e.transpose(bank[:, r * P:(r + 1) * P], osb[:, r * P:(r + 1) * P], weight(k, "ident"))
    m_tr = pe.mark(tr)
    dve.wait(m_tr)
    o = bank.rearrange("p (r g c) -> p r g c", r=4, g=4)
    den = den.rearrange("p (g r) -> p r g", g=4)
    if eps is None:
        dve.then(dve.e.reciprocal(den, o[:, :, :, 8]))
    else:
        dve.then(dve.e.tensor_scalar(den, o[:, :, :, 8], eps, None, ALU.add))
        dve.then(dve.e.reciprocal(den, den))
    m = dve.mark(dve.e.tensor_tensor(at.rearrange("p (g r c) -> p r g c", g=4, r=4), o[:, :, :, 0:8],
                                     den.unsqueeze(3).to_broadcast([P, 4, 4, 8]), ALU.mult))
    k.banks.done(b, m)
    return m_tr, m


def bf16_parts(k, src, parts, rest, line):
    m = None
    for i in range(3):
        for dst in parts[i]:
            m = line.mark(line.e.tensor_copy(dst, src))
        line.wait(m)
        if i < 2:
            line.then(line.e.tensor_tensor(rest, src, parts[i][0], ALU.subtract))
            src = rest
    return m


def attention_keys(k, n, lane, buf):
    pe, dve, act = k.pe, k.dve, k.act
    lo = n * TPB
    pi, room = buf["pr"].next()
    dve.wait(*buf["pr"].last_use[pi])
    act.wait(*buf["pr"].last_use[pi])
    x2, xT, used = room[:, 0:3 * P], room[:, 5 * P:6 * P], dict(x2=(), kst=(), xT=())
    kst = room[:, 3 * P:5 * P].bitcast(BF16).rearrange("p (g a c) -> p g a c", g=4, a=2)
    dve.then(dve.e.memset(kst, 0.0))
    dve.mark(dve.e.memset(kst[:, :, :, 48:51], 1.0))
    kT = buf["kT"]
    v4 = buf["v9"][:, 0:36 * TPB].rearrange("p (t g c) -> p t g c", g=4, c=9)
    dve.wait(*[m for m in [buf["values_used"]] if m])
    for tt in range(lane, TPB, 4):
        t = lo + tt
        r1, r2 = x2[:, 0:P], x2[:, P:2 * P]
        dve.wait(*used["x2"])
        dve.then(dve.e.tensor_scalar(r1, k.xn[:, t, :], buf["rs"][:, t:t + 1], None, ALU.mult))
        dve.then(dve.e.tensor_tensor(r1, r1, weight(k, "f2_n1"), ALU.mult))
        pair = r1.rearrange("p (c two) -> p two c", two=2)
        cos, sin = (weight(k, w)[:, 64 * tt:64 * tt + 64] for w in ("cos", "sin"))
        t1, t2 = x2[:, 2 * P:2 * P + 64], x2[:, 2 * P + 64:3 * P]
        dve.mark(dve.e.tensor_tensor(r2[:, 0:64], pair[:, 0, :], cos, ALU.mult))
        dve.mark(dve.e.tensor_tensor(r2[:, 64:128], pair[:, 0, :], sin, ALU.mult))
        dve.mark(dve.e.tensor_tensor(t1, pair[:, 1, :], sin, ALU.mult))
        dve.then(dve.e.tensor_tensor(t2, pair[:, 1, :], cos, ALU.mult))
        dve.mark(dve.e.tensor_tensor(r2[:, 0:64], r2[:, 0:64], t1, ALU.subtract))
        m = dve.then(dve.e.tensor_tensor(r2[:, 64:128], r2[:, 64:128], t2, ALU.add))
        yield 1
        b, bank = k.banks.next()
        pe.wait(*k.banks.last_use[b])
        pe.wait(m)
        m = pe.mark(pe.e.transpose(bank[:, 0:P], r2, weight(k, "ident")))
        used["x2"] = (m,)
        act.wait(*used["xT"])
        act.wait(m)
        m = act.mark(act.e.activation(xT, bank[:, 0:P], ACT.Copy))
        k.banks.done(b, m)
        yield 1
        b, bank = k.banks.next()
        pe.wait(*k.banks.last_use[b])
        pe.wait(m)
        m = pe.mark(matmul(k, bank[:, 0:192], xT, weight(k, "f2_qkv")))
        used["xT"] = (m,)
        dve.wait(m)
        qf = k.h2[:, t, :]
        dve.mark(dve.e.tensor_copy(qf, bank[:, 0:128]))
        dve.mark(dve.e.tensor_copy(v4[:, tt, :, 0:8], bank[:, 160:192].rearrange("p (g c) -> p g c", c=8)))
        kf = x2[:, 0:32]
        m = dve.then(dve.e.tensor_copy(kf, bank[:, 128:160]))
        k.banks.done(b, m)
        k4 = kf.rearrange("p (g c) -> p g c", c=8)
        dve.wait(*used["kst"])
        slot = lambda i, half: kst[:, :, half, 8 * i:8 * i + 8]
        m = bf16_parts(k, k4, [[slot(i, hf) for i in where for hf in range(2)]
                                 for where in ((0, 2, 5), (1, 4), (3,))],
                            x2[:, 32:64].rearrange("p (g c) -> p g c", c=8), dve)
        yield 1
        b, bank = k.banks.next()
        pe.wait(*k.banks.last_use[b])
        bank16 = bank.bitcast(BF16)
        pe.wait(m)
        for g in range(4):
            tr = pe.e.transpose(bank16[:, g * P:(g + 1) * P], kst[:, g, :, :].rearrange("p a c -> p (a c)"), buf["id16"])
        m = pe.mark(tr)
        used["kst"] = (m,)
        act.wait(m)
        m = act.mark(act.e.activation(kT[:, :, tt * P:(tt + 1) * P], split(bank16[:, 0:4 * P], 4), ACT.Copy))
        k.banks.done(b, m)
        buf["kT_ready"][lane] = m
        yield 1
    buf["pr"].done(pi, used["kst"][0], (dve.name, dve.sem, dve.count))


def attention_queries(k, n, tt, buf):
    pe, dve, act = k.pe, k.dve, k.act
    kT, qst = buf["kT"], buf["qst"]
    t = n * TPB + tt
    L = (tt + 1) * P
    dve.wait(*buf["qst_used"])
    q16 = k.h2[:, t, :].rearrange("p (h c) -> p h c", c=8)
    slot = lambda i: qst[:, :, 8 * i:8 * i + 8]
    m = bf16_parts(k, q16, [[slot(0), slot(1), slot(3)], [slot(2), slot(4)], [slot(5)]],
                        buf["qrest"].rearrange("p (h c) -> p h c", c=8), dve)

    yield 1

    def turn(m, qi, qT):
        b, bank = k.banks.next()
        pe.wait(*k.banks.last_use[b])
        bank16 = bank.bitcast(BF16)
        pe.wait(m)
        for p in range(8):
            tr = pe.e.transpose(bank16[:, p * P:(p + 1) * P],
                                qst[:, 2 * p:2 * p + 2, :].rearrange("p a c -> p (a c)"), buf["id16"])
        m = pe.mark(tr)
        act.wait(m)
        r = act.mark(act.e.activation(qT, bank16, ACT.Copy))
        k.banks.done(b, r)
        return m, r

    qi, qT = buf["qT"].next()
    act.wait(*buf["qT"].last_use[qi])
    m_tr, m = turn(m, qi, qT)
    yield 1
    pe.wait(m)
    pm = buf["pm"]
    pieces = [(c, min(c + BLK, L)) for c in range(0, L, BLK)]
    per_bank = BLK // L if L <= BLK else 1
    for h0 in range(0, 16, 2 * per_bank):
        for pc, (c0, c1) in enumerate(pieces):
            w = c1 - c0
            two = [k.banks.next() for _ in range(2)]
            for b, _ in two:
                pe.wait(*k.banks.last_use[b])
            for j in range(per_bank):
                for odd, (b, bank) in enumerate(two):
                    hh = h0 + 2 * j + odd
                    r = slice(64 * odd, 64 * odd + 48)
                    mm = matmul(k, bank[:, j * w:(j + 1) * w], qT[r, hh // 2 * P:hh // 2 * P + P],
                                kT[r, hh // 4, c0:c1], start=(j == 0), stop=False)
            if c1 < L:
                m = pe.mark(mm)
            for odd, (b, bank) in enumerate(two):
                if c1 == L:
                    for j in range(per_bank):
                        mm = matmul(k, bank[:, (j + 1) * w - P:(j + 1) * w], buf["id16"], buf["negU"],
                                    start=False, stop=True)
                    m = pe.mark(mm)
                dve.wait(m)
                m = dve.mark(dve.e.tensor_reduce(pm[:, h0 + odd:h0 + odd + 2 * per_bank - 1:2, pc],
                                                 bank[:, 0:per_bank * w].rearrange("p (h c) -> p h c", c=w), AX, ALU.max))
                k.banks.done(b, m)
        yield 1
    firsts_used = (pe.name, pe.sem, pe.count)
    dve.wait(m)
    mx = buf["mx"]
    if len(pieces) == 2:
        dve.then(dve.e.tensor_tensor(mx, pm[:, :, 0], pm[:, :, 1], ALU.max))
        dve.then(dve.e.tensor_scalar(mx, mx, -1.0, None, ALU.mult))
    else:
        dve.then(dve.e.tensor_scalar(mx, pm[:, :, 0], -1.0, None, ALU.mult))
    dve.wait(m_tr)
    m = bf16_parts(k, mx.unsqueeze(2), [[qst[:, :, 48 + i:49 + i]] for i in range(3)],
                        buf["mx2"].unsqueeze(2), dve)
    yield 1
    act.wait(firsts_used)
    m_tr, m = turn(m, qi, qT)
    buf["qst_used"] = (m_tr,)
    buf["queries"][tt % 2] = (qi, qT, m)
    yield 1


def attention_output(k, n, tt, buf):
    pe, dve, act = k.pe, k.dve, k.act
    kT, v9, h = buf["kT"], buf["v9"], buf["h"]
    t = n * TPB + tt
    qi, qT, m = buf["queries"][tt % 2]
    pe.wait(m)
    ob, obank = k.banks.next()
    pe.wait(*k.banks.last_use[ob])

    def values(j, parts):
        for _, _, m in parts:
            pe.wait(m)
        for g in range(4):
            pr = parts[g // 2][1]
            mm = matmul(k, obank[32 * g:32 * g + 32, :], v9[:, 36 * j + 9 * g:36 * j + 9 * g + 32],
                        pr[:, (g % 2) * BLK:(g % 2 + 1) * BLK], start=(j == 0), stop=(j == tt))
        m = pe.mark(mm)
        for pi, _, _ in parts:
            buf["pr"].done(pi, m)
        return m

    late = None
    for j in range(tt + 1):
        parts = []
        for g2 in (0, 2):
            two = [k.banks.next() for _ in range(2)]
            for b, _ in two:
                pe.wait(*k.banks.last_use[b])
            for q in range(2):
                for odd, (b, bank) in enumerate(two):
                    r = slice(64 * odd, 64 * odd + 51)
                    g = g2 + q
                    mm = matmul(k, bank[:, 2 * q * P:(2 * q + 2) * P], kT[r, g, j * P:(j + 1) * P],
                                qT[r, 2 * g * P:(2 * g + 2) * P], start=(q == 0), stop=False)
            if j < tt:
                m = pe.mark(mm)
            pi, pr = buf["pr"].next()
            act.wait(*buf["pr"].last_use[pi])
            for odd, (b, bank) in enumerate(two):
                if j == tt:
                    m = pe.mark(matmul(k, bank, buf["id16"], buf["negL"], start=False, stop=True))
                act.wait(m)
                dst = pr.rearrange("p (g pair odd c) -> p odd g pair c", g=2, pair=2, odd=2)[:, odd]
                r = act.mark(act.e.activation(dst, bank.rearrange("p (g pair c) -> p g pair c", g=2, pair=2),
                                              ACT.Exp, scale=8.0 ** -0.5))
                k.banks.done(b, r)
            parts.append((pi, pr, r))
            yield 1
        if late:
            values(*late)
        late = (j, parts)
    buf["qT"].done(qi, m)
    m = values(*late)
    buf["values_used"] = m
    act.wait(m)
    oi, pr = buf["pr"].next()
    osb = pr[:, 0:BLK]
    act.wait(*buf["pr"].last_use[oi])
    m = act.mark(act.e.activation(osb, obank, ACT.Copy))
    k.banks.done(ob, m)
    yield 1
    ai, at = buf["att"].next()
    dve.wait(*buf["att"].last_use[ai])
    pe.wait(m)
    m_tr, m = sums_to_tokens(k, osb, at, buf["den"])
    buf["pr"].done(oi, m_tr)
    yield 1
    b, bank = k.banks.next()
    pe.wait(*k.banks.last_use[b])
    pe.wait(m)
    m = pe.mark(pe.e.transpose(bank[:, 0:P], at, weight(k, "ident")))
    buf["att"].done(ai, m)
    xi, xT = buf["xT"].next()
    act.wait(*buf["xT"].last_use[xi])
    act.wait(m)
    m = act.mark(act.e.activation(xT, bank[:, 0:P], ACT.Copy))
    k.banks.done(b, m)
    yield 1
    b, bank = k.banks.next()
    pe.wait(*k.banks.last_use[b])
    pe.wait(m)
    m = pe.mark(matmul(k, bank[:, 0:P], xT, weight(k, "f2_wo")))
    buf["xT"].done(xi, m)
    dve.wait(m)
    m = dve.then(dve.e.tensor_tensor(h[:, t, :], bank[:, 0:P], k.xn[:, t, :], ALU.add))
    k.banks.done(b, m)
    ji, junk = k.junk.next()
    act.wait(*k.junk.last_use[ji])
    act.wait(m)
    m = act.mark(act.e.activation(junk, h[:, t, :], ACT.Square, accum_out=buf["hsq"][:, t:t + 1]))
    k.junk.done(ji, m)
    yield 1
    buf["h_done"][t] = m


def layer2_attention(k, n, buf):
    yield from together(*(attention_keys(k, n, lane, buf) for lane in range(4)))
    k.pe.wait(*buf["kT_ready"])
    yield from attention_queries(k, n, 0, buf)
    for tt in range(TPB):
        both = [attention_output(k, n, tt, buf)]
        if tt + 1 < TPB:
            both.append(attention_queries(k, n, tt + 1, buf))
        yield from together(*both)


def layer2_moe(k, i, buf):
    pe, dve, act = k.pe, k.dve, k.act
    sl = slice(i * TB, (i + 1) * TB)
    h, hs = buf["h"], buf["hsq"]
    hT = k.xnT[:, i * BLK:(i + 1) * BLK]
    while k.xnT_used[0] < (i + 1) * TB - 1 or buf["h_done"][(i + 1) * TB - 1] is None:
        yield 1
    dve.wait(buf["h_done"][(i + 1) * TB - 1])
    dve.then(dve.e.tensor_scalar(hs[:, sl], hs[:, sl], 1.0 / D, 1e-6, ALU.mult, ALU.add))
    rsqrt(k, buf["hrs"][:, sl], hs[:, sl], buf["htmp"][:, sl])
    act.wait(k.xnT_used[1])
    yield 1
    b, bank = k.banks.next()
    pe.wait(*k.banks.last_use[b])
    for q in range(TB):
        t = i * TB + q
        xi, xh = buf["xh"].next()
        dve.wait(*buf["xh"].last_use[xi])
        m = dve.mark(dve.e.tensor_scalar(xh, h[:, t, :], buf["hrs"][:, t:t + 1], None, ALU.mult))
        pe.wait(m)
        m = pe.mark(pe.e.transpose(bank[:, q * P:(q + 1) * P], xh, weight(k, "ident")))
        buf["xh"].done(xi, m)
    act.wait(m)
    m_hT = act.mark(act.e.activation(hT, bank, ACT.Copy, scale=weight(k, "f2_n2")))
    k.banks.done(b, m_hT)
    yield 1
    lg, gates, gT = buf["lg"], buf["gates"], buf["gT"]
    b, bank = k.banks.next()
    pe.wait(*k.banks.last_use[b])
    pe.wait(m_hT)
    for q in range(TB):
        mm = matmul(k, bank[:, 8 * q:8 * q + 8], hT[:, q * P:(q + 1) * P], weight(k, "f2_rt"))
    dve.wait(pe.mark(mm))
    m = dve.then(dve.e.tensor_tensor(lg, bank[:, 0:8 * TB].rearrange("p (t e) -> p t e", e=8),
                                     again(weight(k, "f2_rb"), TB), ALU.add))
    k.banks.done(b, m)
    yield from route(k, 8, lg, gates, weight(k, "idx8"), buf["room"], tiles=TB)
    bufs = buf["wide"]
    gates_ready = k.gates_ready

    def begin(i, acc):
        b, bank = k.banks.next()
        pe.wait(*k.banks.last_use[b])
        pe.wait(gates_ready)
        for q in range(TB):
            tr = pe.e.transpose(bank[0:8, q * P:(q + 1) * P], gates[:, q, :], weight(k, "ident"))
        act.wait(pe.mark(tr), *buf["gT_used"])
        m = act.mark(act.e.activation(gT[0:8, :], bank[0:8, :], ACT.Copy))
        pe.wait(m)
        for q in range(TB):
            mm = matmul(k, bank[:, q * P:(q + 1) * P], gT[0:8, q * P:(q + 1) * P], weight(k, "f2_b3", slice(0, 8)))
        m = pe.mark(mm)
        buf["gT_used"] = (m,)
        dve.wait(m)
        m = dve.mark(dve.e.tensor_tensor(acc, split(bank, TB), acc, ALU.add))
        k.banks.done(b, m)
        return m

    def end(i, acc, m):
        act.wait(m)
        m = act.mark(act.e.activation(acc, acc, ACT.Silu))
        for t in range(i * TB, (i + 1) * TB):
            k.g_ready[t] = m

    cfg = dict(E=8, NF=4, shared=0, blocks={i: hT}, xT_ready={i: m_hT}, w1=weight(k, "f2_w1"),
               w2=weight(k, "f2_w2"), w3=weight(k, "f2_w3"), b1=buf["half_b1"], b2=weight(k, "f2_b2"),
               gates=gates, t0=i * TB, bufs=bufs, begin=begin, end=end)
    yield from wide_experts(k, cfg, [i])


def layer2_room(k):
    dve, act, pool = k.dve, k.act, k.pool
    a = k.arena
    buf = dict(gT=a.f32(BLK), gT_used=(), kT_ready=[None] * 4, qst_used=(),
               qrest=a.f32(P), queries=[None, None], h_done=[None] * NT, half_b1=a.f32(32),
               kT=a.bf16(4 * SEQ).rearrange("p (g c) -> p g c", g=4),
               v9=a.f32(TPB * 36 + 32), values_used=None,
               qst=a.bf16(16 * 64).rearrange("p (h c) -> p h c", h=16),
               xT=Ring([a.f32(P) for _ in range(2)]),
               id16=a.bf16(P), negU=a.bf16(P), negL=a.bf16(4 * P),
               qT=Ring([a.bf16(8 * P) for _ in range(2)]), pr=Ring([a.f32(2 * BLK) for _ in range(4)]),
               pm=a.f32(32).rearrange("p (h c) -> p h c", c=2), mx=a.f32(16), mx2=a.f32(16), den=a.f32(16),
               att=Ring([a.f32(P) for _ in range(2)]), h=k.h2,
               hsq=a.f32(NT), hrs=a.f32(NT), htmp=a.f32(NT), xh=Ring([a.f32(P) for _ in range(2)]),
               room=route_room(k, 8, TB), lg=a.f32(TB * 8).rearrange("p (t e) -> p t e", e=8),
               gates=a.f32(TB * 8).rearrange("p (t e) -> p t e", e=8),
               rs=a.f32(NT), wide=wide_buffers(k))
    dve.mark(dve.e.tensor_copy(buf["id16"], weight(k, "ident")))
    dve.mark(dve.e.tensor_copy(buf["negU"], weight(k, "negU")))
    dve.mark(dve.e.tensor_copy(split(buf["negL"], 4), again(weight(k, "negL"), 4)))
    dve.mark(dve.e.memset(buf["v9"], 1.0))
    dve.mark(dve.e.tensor_scalar(buf["half_b1"], weight(k, "f2_b1"), 0.5, None, ALU.mult))
    dve.then(dve.e.memset(buf["qst"], 0.0))
    sq, tmp = a.f32(NT), a.f32(NT)
    for t in range(NT):
        act.wait(k.xn_ready[t // TB])
        ji, junk = k.junk.next()
        act.wait(*k.junk.last_use[ji])
        m = act.mark(act.e.activation(junk, k.xn[:, t, :], ACT.Square, accum_out=sq[:, t:t + 1]))
        k.junk.done(ji, m)
    dve.wait(m)
    dve.then(dve.e.tensor_scalar(sq, sq, 1.0 / D, 1e-6, ALU.mult, ALU.add))
    rsqrt(k, buf["rs"], sq, tmp)
    return buf


def layer3_prepare(k):
    pe, dve, act = k.pe, k.dve, k.act
    a = k.arena
    sq, rs, tmp = a.f32(NT), a.f32(NT), a.f32(NT)
    k.m3_xT = a.f32(NT * P)
    xh = Ring([a.f32(P) for _ in range(2)])
    k.m3_ready = []
    for t in range(NT):
        act.wait(k.xn_ready[t // TB])
        ji, junk = k.junk.next()
        act.wait(*k.junk.last_use[ji])
        m = act.mark(act.e.activation(junk, k.xn[:, t, :], ACT.Square, accum_out=sq[:, t:t + 1]))
        k.junk.done(ji, m)
    yield 1
    dve.wait(m)
    dve.then(dve.e.tensor_scalar(sq, sq, 1.0 / D, 1e-5, ALU.mult, ALU.add))
    rsqrt(k, rs, sq, tmp)
    for i in range(NBLK):
        b, bank = k.banks.next()
        pe.wait(*k.banks.last_use[b])
        for q in range(TB):
            t = i * TB + q
            xi, x = xh.next()
            dve.wait(*xh.last_use[xi])
            m = dve.mark(dve.e.tensor_scalar(x, k.xn[:, t, :], rs[:, t:t + 1], None, ALU.mult))
            pe.wait(m)
            m = pe.mark(pe.e.transpose(bank[:, q * P:(q + 1) * P], x, weight(k, "ident")))
            xh.done(xi, m)
        act.wait(m)
        m = act.mark(act.e.activation(k.m3_xT[:, i * BLK:(i + 1) * BLK], bank, ACT.Copy, scale=weight(k, "m3_nw")))
        k.banks.done(b, m)
        k.m3_ready.append(m)
        yield 1
    k.m3_out = [a.f32(P), a.f32(P)]
    for d in range(2):
        rows = slice(64 * d, 64 * d + 64)
        b, bank = k.banks.next()
        pe.wait(*k.banks.last_use[b])
        m = pe.mark(matmul(k, bank[:, 0:P], weight(k, "m3_outp", rows), weight(k, "m3_opw", rows)))
        dve.wait(m)
        m = dve.mark(dve.e.tensor_scalar(k.m3_out[d], bank[:, 0:P], weight(k, "m3_gn")[:, d:d + 1], None, ALU.mult))
        k.banks.done(b, m)
    pe.wait(m)
    dve.wait(*k.m3_ready)
    for t in range(NT):
        m = dve.mark(dve.e.tensor_tensor(k.xn[:, t, :], k.xn[:, t, :], weight(k, "m3_opb"), ALU.add))
    dve.wait(m)
    k.m3_A = [[a.f32(2), a.f32(2)] for _ in range(2)]
    yield 1


def layer3_direction(k, d, batch, buf):
    dve = k.dve
    n = "fb"[d]
    rows = slice(64 * d, 64 * d + 64)
    cfg = dict(H=2, rows=rows, back=d == 1, xT=k.m3_xT, xT_ready=k.m3_ready,
               zdt=weight(k, "m3_zdt", rows), xbc=weight(k, "m3_xbc", rows), cw=weight(k, "m3_cw" + n),
               cb=weight(k, "m3_cb" + n), dtb=weight(k, "m3_dtb" + n), alog=weight(k, "m3_alog" + n),
               A=k.m3_A[d][batch], Dh=weight(k, "m3_D" + n), out=k.m3_out[d])
    yield from mamba(k, cfg, batch, buf)
    for tt in range(TPB):
        t = batch * TPB + tt
        so, rs = buf["so"][:, tt, :], buf["rs"][:, tt:tt + 1]
        if d == 0:
            m = dve.mark(dve.e.scalar_tensor_tensor(k.s[:, t, :], so, rs, k.xn[:, t, :], ALU.mult, ALU.add))
        else:
            dst = k.xn if k.m3_first[batch] else k.s
            m = dve.mark(dve.e.scalar_tensor_tensor(dst[:, t, :], so, rs, dst[:, t, :], ALU.mult, ALU.add))
        k.s_ready[t] = m
    dve.wait(m)
    k.m3_first[batch] = False
    yield 1


def layer3_ffn(k):
    pe, dve, act = k.pe, k.dve, k.act
    a = k.arena
    E, NC = 16, 9
    lg = a.f32(NT * E).rearrange("p (t e) -> p t e", e=E)
    b, bank = k.banks.next()
    pe.wait(*k.banks.last_use[b])
    pe.wait(*k.xnT_ready)
    for t in range(NT):
        mm = matmul(k, bank[:, 16 * t:16 * t + 16], k.xnT[:, t * P:(t + 1) * P], weight(k, "f3_rt"))
    dve.wait(pe.mark(mm))
    m = dve.then(dve.e.tensor_tensor(lg, bank[:, 0:E * NT].rearrange("p (t e) -> p t e", e=E),
                                     again(weight(k, "f3_rb"), NT), ALU.add))
    k.banks.done(b, m)
    gates = a.f32(NT * E).rearrange("p (t e) -> p t e", e=E)
    yield from route(k, E, lg, gates, weight(k, "idx16"), route_room(k, E))
    across = Ring([a.f32(BLK) for _ in range(2)])
    hid, sgs = Ring([a.f32(BLK) for _ in range(3)]), Ring([a.f32(BLK) for _ in range(2)])
    for i in range(NBLK):
        gi, gT = across.next()
        act.wait(*across.last_use[gi])
        yield from gates_across(k, E, gates[:, i * TB:(i + 1) * TB, :], gT, tiles=TB)
        pe.wait(k.gT_ready)
        cols = slice(i * BLK, (i + 1) * BLK)
        ob, obank = k.banks.next()
        pe.wait(*k.banks.last_use[ob])

        def down(c, hi, h, m_h):
            pe.wait(m_h)
            for q in range(TB):
                mm = matmul(k, obank[:, q * P:(q + 1) * P], h[:, q * P:(q + 1) * P],
                             weight(k, "f3_down")[:, c * P:(c + 1) * P], start=(c == 0 and q == 0), stop=(c == NC - 1))
            m = pe.mark(mm)
            hid.done(hi, m)
            return m

        late = None
        for c in range(NC):
            b, bank = k.banks.next()
            pe.wait(*k.banks.last_use[b])
            m_g = pe.mark(matmul(k, bank, weight(k, "f3_gate")[:, c * P:(c + 1) * P], k.xnT[:, cols]))
            b2, bank2 = k.banks.next()
            pe.wait(*k.banks.last_use[b2])
            m_u = pe.mark(matmul(k, bank2, weight(k, "f3_up")[:, c * P:(c + 1) * P], k.xnT[:, cols]))
            si, sg = sgs.next()
            act.wait(*sgs.last_use[si])
            act.wait(m_g)
            m = act.mark(act.e.activation(sg, bank, ACT.Tanh, scale=0.5))
            hi, h = hid.next()
            dve.wait(*hid.last_use[hi])
            dve.wait(m, m_u)
            m = dve.then(dve.e.scalar_tensor_tensor(h, sg, 1.0, bank, ALU.add, ALU.mult))
            k.banks.done(b, m)
            m = dve.mark(dve.e.tensor_tensor(h, h, bank2, ALU.mult))
            sgs.done(si, m)
            k.banks.done(b2, m)
            if c < NC - 1:
                dve.wait(m)
                b, bank = k.banks.next()
                pe.wait(*k.banks.last_use[b])
                m_c = pe.mark(matmul(k, bank, weight(k, "f3_sel")[0:E, c * P:(c + 1) * P], gT[0:E, :]))
                dve.wait(m, m_c)
                m = dve.mark(dve.e.tensor_tensor(h, h, bank, ALU.mult))
                k.banks.done(b, m)
            if late:
                down(*late)
            late = (c, hi, h, m)
            yield 1
        m = down(*late)
        across.done(gi, m)
        act.wait(m)
        m = act.mark(act.e.activation(k.g[:, i * TB:(i + 1) * TB, :], split(obank, TB), ACT.Silu))
        k.banks.done(ob, m)
        for t in range(i * TB, (i + 1) * TB):
            k.g_ready[t] = m
        yield 1


def program(nc, x_dram, w_dram, out_dram):
    with ExitStack() as ctx:
        k = core(nc, ctx, x_dram, w_dram, out_dram)
        loads(k)
        open_arena(k, 0)
        weights_ready(k, 0)
        halve(k, weight(k, "m0_zdt")[:, 0:256], weight(k, "m0_cw"), weight(k, "m0_cb"))
        layernorm(k, closes=False)
        k.m0_A = [k.arena.f32(4), k.arena.f32(4)]
        k.m0_out = k.arena.f32(256)
        for c in range(2):
            m = k.dve.mark(k.dve.e.tensor_scalar(k.m0_out[:, c * P:(c + 1) * P], weight(k, "m0_out")[:, c * P:(c + 1) * P],
                                                 weight(k, "m0_nw")[:, c:c + 1], None, ALU.mult))
        k.pe.wait(m)
        interleave((layer0_mixer(k, 0, mamba_buffers(k, 4)), 1),
                   (behind(layer0_mixer(k, 1, mamba_buffers(k, 4)), 5), 1), (layer0_ffn(k), 0.5))
        open_arena(k, 1)
        late_loads(k, 4)
        weights_ready(k, 1)
        k.junk = Ring([k.arena.f32(P) for _ in range(2)])
        layernorm(k)
        keys = layer1_keys(k)
        ffn = layer1_ffn(k)
        interleave((keys, 1), (first_steps(ffn, 16), 1))
        interleave((layer1_mixer(k, 0), 1), (behind(layer1_mixer(k, 1), 10), 1), (ffn, 1.5))
        open_arena(k, 2)
        late_loads(k, 3)
        weights_ready(k, 2)
        weights_ready(k, 4)
        k.junk = Ring([k.arena.f32(P)])
        k.h2 = k.g
        layernorm(k)
        k.xnT_used = (-1, None)
        buf = layer2_room(k)
        interleave((layer2_mixer(k), 0.5), (in_turn(*(layer2_attention(k, n, buf) for n in range(NBATCH))), 1),
                   (in_turn(*(layer2_moe(k, i, buf) for i in range(NBLK))), 0.5))
        open_arena(k, 3)
        weights_ready(k, 3)
        halve(k, weight(k, "m3_zdt")[:, 0:128], *(weight(k, "m3_c" + n) for n in ("wf", "wb", "bf", "bb")),
              weight(k, "f3_down")[:, 8 * P:9 * P])
        k.junk = Ring([k.arena.f32(P) for _ in range(2)])
        layernorm(k)
        ffn = layer3_ffn(k)
        interleave((layer3_prepare(k), 1), (first_steps(ffn, 8), 1))
        k.m3_first = [True, True]
        streams = []
        for n in range(NBATCH):
            for d in range(2):
                so = k.s[:, n * TPB:(n + 1) * TPB, :] if d == 0 else None
                streams.append((behind(layer3_direction(k, d, n, mamba_buffers(k, 2, so)), 2 * (2 * n + d)), 1))
        interleave(*streams, (ffn, 0.5))
        results(k)


def constants():
    import numpy as np
    f = np.float32
    c = {}
    i = np.arange(P)
    c["ident"] = np.eye(P, dtype=f)
    c["triU"] = (i[:, None] <= i[None, :]).astype(f)
    c["triL"] = (i[:, None] >= i[None, :]).astype(f)
    c["ones"] = np.ones((P, P), f)
    c["idx8"] = np.broadcast_to(np.arange(8, dtype=f) + 64, (P, 8))
    c["idx16"] = np.broadcast_to(np.arange(16, dtype=f) + 64, (P, 16))
    lv = []
    for n in range(7):
        s = 1 << n
        lv.append(((i[:, None] // (2 * s) == i[None, :] // (2 * s)) & (i[:, None] % (2 * s) < s)
                   & (i[None, :] % (2 * s) >= s)).astype(f))
    c["lvlT"] = np.concatenate(lv, axis=1)
    c["lvl1"] = np.ascontiguousarray(lv[0].T)
    c["negU"] = np.where(i[None, :] > i[:, None], f(-1e9), f(0)).astype(f)
    c["negL"] = np.ascontiguousarray(c["negU"].T)
    bd = np.zeros((P, 36), f)
    for h in range(4):
        bd[32 * h:32 * h + 8, 9 * h:9 * h + 9] = 1
    c["a2_bd"] = bd
    half = D // 2
    theta = (f(1.0) / np.power(f(10000.0), (np.arange(half, dtype=f) / f(half)))).astype(f)
    ang = (np.arange(SEQ, dtype=f)[:, None] * theta[None, :]).astype(f)
    for name, fn in (("cos", np.cos), ("sin", np.sin)):
        c[name] = fn(ang).astype(f).reshape(TPB, P, half).transpose(1, 0, 2).reshape(P, TPB * half)
    sel = np.zeros((P, 4, P), f)
    for e in range(8):
        sel[e, e // 2, 64 * (e % 2):64 * (e % 2) + 64] = 1
    c["f0_sel"] = sel.reshape(P, 4 * P)
    sel = np.zeros((P, 8, P), f)
    for e in range(16):
        sel[e, e // 2, 64 * (e % 2):64 * (e % 2) + 64] = 0.5
    c["f3_sel"] = sel.reshape(P, 8 * P)
    return c


def weights(inputs):
    import numpy as np
    a = {n: np.asarray(v) for n, v in inputs.items()}

    def every(v):
        return np.broadcast_to(v.reshape(1, -1), (P, v.size))

    def chunks(v):
        return v.reshape(-1, P, v.shape[-1]).transpose(1, 0, 2).reshape(P, -1)

    def low(v):
        out = np.zeros((P, v.shape[1]), v.dtype)
        out[:v.shape[0]] = v
        return out

    w = {}
    W = a["L0_attn_W_in"].T
    w["m0_zdt"] = np.concatenate([W[:, 0:256], W[:, 768:772]], axis=1)
    w["m0_xbc"] = W[:, 256:768]
    w["m0_cw"] = chunks(a["L0_attn_conv_w"])
    w["m0_cb"] = a["L0_attn_conv_b"].reshape(4, P).T
    w["m0_dtb"], w["m0_alog"], w["m0_D"] = every(a["L0_attn_dt_bias"]), every(a["L0_attn_A_log"]), every(a["L0_attn_D"])
    w["m0_nw"] = a["L0_attn_norm_weight"].reshape(2, P).T
    w["m0_out"] = chunks(a["L0_attn_W_out"].T)
    w["f0_w1"] = a["L0_ffn_w1"].transpose(1, 0, 2).reshape(P, 512)
    w["f0_b1"] = a["L0_ffn_b1"].reshape(4, P).T
    w["f0_w2"] = chunks(a["L0_ffn_w2"].reshape(512, P))
    w["f0_b2"] = low(a["L0_ffn_b2"])
    w["f0_rt"] = np.concatenate([a["L0_ffn_centroids"].T, a["L0_ffn_w_route"].T], axis=1)

    w["a1_q"] = a["L1_attn_Wq"]
    w["a1_kvb"] = np.concatenate([a["L1_attn_Wk"], a["L1_attn_Wv"], a["L1_attn_Wb"].reshape(P, 1)], axis=1)
    w["a1_g"], w["a1_b"] = every(a["L1_attn_ln_g"]), every(a["L1_attn_ln_b"])
    w["f1_rt"], w["f1_rb"] = a["L1_ffn_router_w"].T, every(a["L1_ffn_experts_bias"])
    for n, m in (("w1", "sw1"), ("w3", "sw3")):
        v = np.concatenate([a["L1_ffn_" + m], a["L1_ffn_" + n]], axis=0)
        w["f1_" + n] = v.transpose(1, 0, 2).reshape(P, 9 * 256)
    w["f1_w2"] = chunks(np.concatenate([a["L1_ffn_sw2"], a["L1_ffn_w2"]], axis=0).reshape(9 * 256, P))

    w["a2_g"], w["a2_b"] = a["L2_attn_ln_g"].reshape(P, 1), a["L2_attn_ln_b"].reshape(P, 1)
    w["a2_qkv"], w["a2_bqkv"] = a["L2_attn_w_qkv"], every(a["L2_attn_b_qkv"])
    w["a2_gate"], w["a2_bgate"] = a["L2_attn_w_gate"], every(a["L2_attn_b_gate"])
    w["a2_proj"], w["a2_bproj"] = a["L2_attn_w_proj"], every(a["L2_attn_b_proj"])
    w["f2_n1"], w["f2_n2"] = every(a["L2_ffn_norm1_w"]), a["L2_ffn_norm2_w"].reshape(P, 1)
    w["f2_qkv"] = np.concatenate([a["L2_ffn_Wq"], a["L2_ffn_Wk"], a["L2_ffn_Wv"]], axis=1)
    w["f2_wo"], w["f2_rt"], w["f2_rb"] = a["L2_ffn_Wo"], a["L2_ffn_router_w"], every(a["L2_ffn_router_b"])
    w["f2_b1"], w["f2_b2"] = a["L2_ffn_b1"].reshape(32, P).T, a["L2_ffn_b2"].reshape(32, P).T
    w["f2_b3"] = low(a["L2_ffn_b3"])
    w["f2_w1"] = a["L2_ffn_W1"].transpose(1, 0, 2).reshape(P, 4096)
    w["f2_w2"] = a["L2_ffn_W2"].transpose(1, 0, 2).reshape(P, 4096)
    w["f2_w3"] = chunks(a["L2_ffn_W3"].reshape(4096, P))

    w["m3_nw"] = a["L3_attn_norm_w"].reshape(P, 1)
    both = np.concatenate([a["L3_attn_f_in_w"].T, a["L3_attn_b_in_w"].T], axis=0)
    w["m3_zdt"] = np.concatenate([both[:, 0:128], both[:, 512:514]], axis=1)
    w["m3_xbc"] = both[:, 128:512]
    for d in "fb":
        w["m3_cw" + d] = chunks(a[f"L3_attn_{d}_conv_w"])
        w["m3_cb" + d] = a[f"L3_attn_{d}_conv_b"].reshape(3, P).T
        w["m3_dtb" + d], w["m3_alog" + d] = every(a[f"L3_attn_{d}_dt_bias"]), every(a[f"L3_attn_{d}_A_log"])
        w["m3_D" + d] = every(a[f"L3_attn_{d}_D"])
    w["m3_gn"] = np.stack([a["L3_attn_f_gnorm_w"], a["L3_attn_b_gnorm_w"]], axis=1)
    w["m3_outp"] = np.concatenate([a["L3_attn_f_outp_w"], a["L3_attn_b_outp_w"]], axis=0)
    w["m3_opw"], w["m3_opb"] = a["L3_attn_op_w"].T, every(a["L3_attn_op_b"])
    w["f3_rt"], w["f3_rb"] = a["L3_ffn_router_w"].T, every(a["L3_ffn_router_bias"])
    for n, m, s in (("gate", "gate_proj", "sh_gate"), ("up", "up_proj", "sh_up")):
        v = a["L3_ffn_" + m].transpose(1, 0, 2).reshape(P, 1024)
        w["f3_" + n] = np.concatenate([v, a["L3_ffn_" + s].T], axis=1)
    w["f3_down"] = np.concatenate([chunks(a["L3_ffn_down_proj"].reshape(1024, P)), a["L3_ffn_sh_down"].T], axis=1)
    return w


def kernel(**inputs):
    import numpy as np
    import concourse.bacc as bacc
    from concourse.bass_utils import run_bass_kernel_spmd

    pack = layout()
    parts = {**constants(), **weights(inputs)}
    for name, (_, cols) in pack.at.items():
        assert parts[name].shape == (P, cols), (name, parts[name].shape, cols)
    packed = np.concatenate([parts[name] for name in pack.at], axis=1)
    x = np.ascontiguousarray(inputs["L0_attn_u"])
    nc = bacc.Bacc("TRN2", target_bir_lowering=False, num_devices=1)
    x_dram = nc.dram_tensor("x_in", list(x.shape), F32, kind="ExternalInput").ap()
    w_dram = nc.dram_tensor("w_in", list(packed.shape), F32, kind="ExternalInput").ap()
    out_dram = nc.dram_tensor("x_out", list(x.shape), F32, kind="ExternalOutput").ap()
    program(nc, x_dram, w_dram, out_dram)
    r = run_bass_kernel_spmd(nc, [{"x_in": x, "w_in": packed}], core_ids=[0])
    return r.results[0]["x_out"]
```
